# Optimizing a Trainium2 kernel written in Bass

```python
import numpy as np
import jax
import jax.numpy as jnp

def _softmax(x, axis=-1):
    return jax.nn.softmax(x, axis=axis)

def _gelu(x):
    return jax.nn.gelu(x, approximate=True)

def _silu(x):
    return jax.nn.silu(x)

def _sigmoid(x):
    return jax.nn.sigmoid(x)

def _layernorm(x, axis=-1, eps=1e-05):
    m = jnp.mean(x, axis=axis, keepdims=True)
    v = jnp.var(x, axis=axis, keepdims=True)
    return (x - m) / jnp.sqrt(v + eps)

def _scatter_add(tgt, idx, src, axis=0):
    return tgt.at[idx].add(src)

def _segment_sum(src, seg, n):
    return jax.ops.segment_sum(src, seg, n)
kernel_name = 'mk_sandwich_d1_jaxref_r4_c68879'

def setup_inputs(seed: int=0):
    np.random.seed(seed)
    _w = jnp.asarray

    def _L0_attn_setup():
        import jax, jax.numpy as jnp
        import numpy as np
        B, L, D_MODEL, D_INNER, D_STATE, DT_RANK, K = (2, 256, 256, 512, 16, 64, 4)
        key = jax.random.key(seed)
        ks = jax.random.split(key, 8)
        sc = lambda n: 1.0 / np.sqrt(n)
        return {'x': jax.random.normal(ks[0], (B, L, D_MODEL), jnp.float32), 'W_in': jax.random.normal(ks[1], (2 * D_INNER, D_MODEL), jnp.float32) * sc(D_MODEL), 'conv_w': jax.random.normal(ks[2], (D_INNER, K), jnp.float32) * sc(K), 'conv_b': jax.random.normal(ks[3], (D_INNER,), jnp.float32) * 0.1, 'W_x': jax.random.normal(ks[4], (DT_RANK + 2 * D_STATE, D_INNER), jnp.float32) * sc(D_INNER), 'W_dt': jax.random.normal(ks[5], (D_INNER, DT_RANK), jnp.float32) * sc(DT_RANK), 'b_dt': jax.random.normal(ks[6], (D_INNER,), jnp.float32) * 0.1, 'A_log': jnp.log(jnp.tile(jnp.arange(1.0, D_STATE + 1.0, dtype=jnp.float32)[None, :], (D_INNER, 1))), 'Dp': jnp.ones((D_INNER,), jnp.float32), 'W_out': jax.random.normal(ks[7], (D_MODEL, D_INNER), jnp.float32) * sc(D_INNER)}
    _L0_attn_in = _L0_attn_setup()

    def _L0_ffn_setup():
        import jax, jax.numpy as jnp
        import numpy as np
        E = 8
        TOPK = 2
        SCALE = 2.0
        key = jax.random.key(seed)
        ks = jax.random.split(key, 12)
        B, S, D, F, R = (2, 128, 256, 1024, 16)
        w = lambda k, shp: jax.random.normal(k, shp, dtype=jnp.float32) * 0.02
        return {'hidden_states': jax.random.normal(ks[0], (B, S, D), dtype=jnp.float32), 'gate_w': w(ks[1], (E, D)), 'w_gate': w(ks[2], (F, D)), 'w_up': w(ks[3], (F, D)), 'w_down': w(ks[4], (D, F)), 'A1': w(ks[5], (E, R, D)), 'B1': w(ks[6], (E, F, R)), 'A3': w(ks[7], (E, R, D)), 'B3': w(ks[8], (E, F, R)), 'A2': w(ks[9], (E, R, F)), 'B2': w(ks[10], (E, D, R))}
    _L0_ffn_in = _L0_ffn_setup()
    _d = {'L0_attn_x': _L0_attn_in['x'], 'L0_attn_W_in': _L0_attn_in['W_in'], 'L0_attn_conv_w': _L0_attn_in['conv_w'], 'L0_attn_conv_b': _L0_attn_in['conv_b'], 'L0_attn_W_x': _L0_attn_in['W_x'], 'L0_attn_W_dt': _L0_attn_in['W_dt'], 'L0_attn_b_dt': _L0_attn_in['b_dt'], 'L0_attn_A_log': _L0_attn_in['A_log'], 'L0_attn_Dp': _L0_attn_in['Dp'], 'L0_attn_W_out': _L0_attn_in['W_out'], 'L0_ffn_gate_w': _L0_ffn_in['gate_w'], 'L0_ffn_w_gate': _L0_ffn_in['w_gate'], 'L0_ffn_w_up': _L0_ffn_in['w_up'], 'L0_ffn_w_down': _L0_ffn_in['w_down'], 'L0_ffn_A1': _L0_ffn_in['A1'], 'L0_ffn_B1': _L0_ffn_in['B1'], 'L0_ffn_A3': _L0_ffn_in['A3'], 'L0_ffn_B3': _L0_ffn_in['B3'], 'L0_ffn_A2': _L0_ffn_in['A2'], 'L0_ffn_B2': _L0_ffn_in['B2']}
    _x0 = _d['L0_attn_x']
    _d['L0_attn_x'] = jax.random.normal(jax.random.fold_in(jax.random.key(seed), 1), (16, 512, 256), dtype=_x0.dtype)
    del _x0
    return _d

def reference(L0_attn_x, L0_attn_W_in, L0_attn_conv_w, L0_attn_conv_b, L0_attn_W_x, L0_attn_W_dt, L0_attn_b_dt, L0_attn_A_log, L0_attn_Dp, L0_attn_W_out, L0_ffn_gate_w, L0_ffn_w_gate, L0_ffn_w_up, L0_ffn_w_down, L0_ffn_A1, L0_ffn_B1, L0_ffn_A3, L0_ffn_B3, L0_ffn_A2, L0_ffn_B2):

    def _L0_attn_ref(x, W_in, conv_w, conv_b, W_x, W_dt, b_dt, A_log, Dp, W_out):
        import jax, jax.numpy as jnp
        import numpy as np
        B, L, D_MODEL, D_INNER, D_STATE, DT_RANK, K = (2, 256, 256, 512, 16, 64, 4)
        xz = x @ W_in.T
        xc, z = jnp.split(xz, 2, axis=-1)
        d_inner = xc.shape[-1]
        k = conv_w.shape[1]
        xt = xc.transpose(0, 2, 1)
        yt = jax.lax.conv_general_dilated(xt, conv_w[:, None, :], window_strides=(1,), padding=[(k - 1, 0)], dimension_numbers=('NCH', 'OIH', 'NCH'), feature_group_count=d_inner)
        xc = yt.transpose(0, 2, 1) + conv_b
        xc = jax.nn.silu(xc)
        dBC = xc @ W_x.T
        dt_rank = W_dt.shape[1]
        d_state = A_log.shape[1]
        delta = dBC[..., :dt_rank]
        Bm = dBC[..., dt_rank:dt_rank + d_state]
        Cm = dBC[..., dt_rank + d_state:]
        delta = jax.nn.softplus(delta @ W_dt.T + b_dt)
        A = -jnp.exp(A_log)
        deltaA = jnp.exp(delta[..., None] * A)
        BX = delta[..., None] * Bm[:, :, None, :] * xc[..., None]

        def combine(e1, e2):
            a1, x1 = e1
            a2, x2 = e2
            return (a1 * a2, a2 * x1 + x2)
        _, hs = jax.lax.associative_scan(combine, (deltaA, BX), axis=1)
        y = jnp.einsum('bldn,bln->bld', hs, Cm) + Dp * xc
        out = y * jax.nn.silu(z) @ W_out.T
        return out

    def _L0_ffn_ref(hidden_states, gate_w, w_gate, w_up, w_down, A1, B1, A3, B3, A2, B2):
        import jax, jax.numpy as jnp
        import numpy as np
        E = 8
        TOPK = 2
        SCALE = 2.0
        B, S, D = hidden_states.shape
        x = hidden_states.reshape(-1, D)
        N = x.shape[0]
        probs = jax.nn.softmax(x @ gate_w.T, axis=-1)
        vals, idx = jax.lax.top_k(probs, TOPK)
        rw = vals / jnp.sum(vals, axis=-1, keepdims=True)
        weight = jnp.zeros((N, E), x.dtype).at[jnp.arange(N)[:, None], idx].add(rw)
        common_w1 = x @ w_gate.T
        common_w3 = x @ w_up.T
        d1 = jnp.einsum('enr,efr->enf', jnp.einsum('nd,erd->enr', x, A1), B1) * SCALE
        d3 = jnp.einsum('enr,efr->enf', jnp.einsum('nd,erd->enr', x, A3), B3) * SCALE
        act = jax.nn.silu(common_w1[None] + d1) * (common_w3[None] + d3)
        out = jnp.einsum('ne,enf->nf', weight, act) @ w_down.T
        z = jnp.einsum('enf,erf->enr', act, A2)
        out = out + jnp.einsum('ne,enr,edr->nd', weight, z, B2) * SCALE
        return out.reshape(B, S, D)
    x = L0_attn_x
    x = x + _layernorm(_L0_attn_ref(_layernorm(x, axis=-1), L0_attn_W_in, L0_attn_conv_w, L0_attn_conv_b, L0_attn_W_x, L0_attn_W_dt, L0_attn_b_dt, L0_attn_A_log, L0_attn_Dp, L0_attn_W_out), axis=-1)
    x = x + _layernorm(_L0_ffn_ref(_layernorm(x, axis=-1), L0_ffn_gate_w, L0_ffn_w_gate, L0_ffn_w_up, L0_ffn_w_down, L0_ffn_A1, L0_ffn_B1, L0_ffn_A3, L0_ffn_B3, L0_ffn_A2, L0_ffn_B2), axis=-1)
    return x

_drawn_inputs = setup_inputs


def setup_inputs(seed=0):
    import zlib

    import numpy as np

    out = dict(_drawn_inputs(seed))
    spreads = {'L0_attn_Dp': (1.0, 0.2)}
    factors = {}
    for name, (base, spread) in spreads.items():
        noise = np.random.default_rng([zlib.crc32(name.encode()), seed]).standard_normal(out[name].shape)
        drawn = base * np.exp(spread * noise) if base else spread * noise
        out[name] = jnp.asarray(drawn.astype(out[name].dtype))
    for name, factor in factors.items():
        out[name] = (out[name] * factor).astype(out[name].dtype)
    return out
```

```python
from contextlib import ExitStack, contextmanager

import concourse.bass as bass
import concourse.mybir as mybir
from concourse.alu_op_type import AluOpType as ALU

F32 = mybir.dt.float32
ACT = mybir.ActivationFunctionType
AX = mybir.AxisListType

P = 128
SEQS, T, DM = 16, 512, 256
DI, NS, DTR, TAPS = 512, 16, 64, 4
TT, MC, DC = T // P, DM // P, DI // P
UNITS = NS * DC
E, R, FF = 8, 16, 1024
ER, FC = E * R, FF // P
EPS = 1e-5
LORA_SCALE = 2.0
PAD = TAPS


def begun(count):
    return not isinstance(count, int) or count > 0


def pass_waits(eng, passed):
    eng.sem_inc(passed, 1)


def up_to(s):
    return min(s, SEQS) if isinstance(s, int) else s


def over_tiles(eng, count, step):
    step(0, 0, True, False)
    with eng.Fori(1, count - 2, 2) as i:
        step(i, 1, False, False)
        step(i + 1, 0, False, False)
    step(count - 1, 1, False, True)


def row(ap4, s):
    if isinstance(s, int):
        return ap4[s]
    return ap4[bass.ds(s, 1)].rearrange("a p j d -> (a p) j d")


def mamba_phase(nc, x, w, x2_dram, consts):
    ident, eps, one = consts
    with ExitStack() as ctx:
        def sb(name, shape):
            return ctx.enter_context(nc.sbuf_tensor(name, shape, F32))

        def sem(name):
            return ctx.enter_context(nc.semaphore(name))

        w_in_z = sb("w_in_z", [P, MC, DI])
        w_tap = sb("w_tap", [P, TAPS, MC, DI])
        conv_b = sb("conv_b", [P, DC])
        w_x = sb("w_x", [P, DC, DTR + 2 * NS])
        w_dt = sb("w_dt", [DTR, DI])
        b_dt = sb("b_dt", [P, DC])
        a_neg = sb("a_neg", [P, DC, NS])
        d_skip = sb("d_skip", [P, DC])
        w_out = sb("w_out", [P, DC, DM])
        xs = sb("xs", [P, TT, DM])
        stats = sb("stats", [P, TT, 6])
        mv = sb("mv", [P, TT, 2])
        lnv = sb("lnv", [P, TT])
        rstd = sb("rstd", [P, TT])
        xn = sb("xn", [P, TT, DM])
        xn_t = sb("xn_t", [P, MC, PAD + T])
        xc = sb("xc", [P, 2, DC, T])
        zs = sb("zs", [P, 2, DC, T])
        dt_raw = sb("dt_raw", [DTR, T])
        bc = sb("bc", [P, 2, TT, 2 * NS])
        delta = sb("delta", [P, 2, DC, T])
        u_t = sb("u_t", [P, 2, TT, DI])
        v = sb("v", [P, 2, TT, DI])
        da = sb("da", [P, 2, DC, T])
        h = sb("h", [P, 2, DC, T])
        y_acc = sb("y_acc", [P, 2, TT, DI])
        o = sb("o", [P, TT, DM])
        stats2 = sb("stats2", [P, TT, 6])
        mv2 = sb("mv2", [P, TT, 2])
        lnv2 = sb("lnv2", [P, TT])
        rstd2 = sb("rstd2", [P, TT])
        xr = sb("xr", [P, TT, DM])
        x2 = sb("x2", [P, TT, DM])
        work_a = sb("work_a", [P, DC, T])
        work_b = sb("work_b", [P, DC, T])
        y1, sp_abs = work_a, work_a
        g, sp_relu, u = work_b, work_b, work_b
        tap_row = v[:, 0].rearrange("p j d -> p (j d)").rearrange("p (k d) -> p k d", k=TAPS)
        w_in_x = da[:, 0, 0:MC]

        bx_ps = [ctx.enter_context(nc.psum_tensor(f"bx_ps{i}", [P, 512], F32)) for i in range(DC)]
        ht_ps = [ctx.enter_context(nc.psum_tensor(f"ht_ps{i}", [P, 512], F32)) for i in range(2)]
        side = ctx.enter_context(nc.psum_tensor("side", [P, 2, 512], F32))

        loaded = sem("loaded")
        a_exp = sem("a_exp")
        setup = sem("setup")
        ident_ready = sem("ident_ready")
        xs_loaded = sem("xs_loaded")
        dve_passed = sem("dve_passed")
        pool_passed = sem("pool_passed")
        st_done = sem("st_done")
        mv_done = sem("mv_done")
        rstd_done = sem("rstd_done")
        xn_done = sem("xn_done")
        xn_tp = sem("xn_tp")
        xn_t_ready = sem("xn_t_ready")
        xin_done = sem("xin_done")
        zin_done = sem("zin_done")
        xc_raw_ready = sem("xc_raw_ready")
        z_raw_ready = sem("z_raw_ready")
        xc_ready = sem("xc_ready")
        dtr_done = sem("dtr_done")
        bc_done = sem("bc_done")
        dt_raw_ready = sem("dt_raw_ready")
        bc_ready = sem("bc_ready")
        dt_done = sem("dt_done")
        abs_ready = sem("abs_ready")
        relu_ready = sem("relu_ready")
        exp_ready = sem("exp_ready")
        ln_ready = sem("ln_ready")
        delta_ready = sem("delta_ready")
        u_ready = sem("u_ready")
        u_tp = sem("u_tp")
        u_t_ready = sem("u_t_ready")
        v_ready = sem("v_ready")
        bx_done = sem("bx_done")
        da_ready = sem("da_ready")
        scan_done = sem("scan_done")
        ht_done = sem("ht_done")
        y_done = sem("y_done")
        acc_tp = sem("acc_tp")
        y1_done = sem("y1_done")
        g_done = sem("g_done")
        oproj_done = sem("oproj_done")
        o_ready = sem("o_ready")
        st2_done = sem("st2_done")
        mv2_done = sem("mv2_done")
        lnv2_done = sem("lnv2_done")
        lnv_done = sem("lnv_done")
        rstd2_done = sem("rstd2_done")
        yn_done = sem("yn_done")
        xr_loaded = sem("xr_loaded")
        x2_ready = sem("x2_ready")
        x2_stored = sem("x2_stored")

        x_v = x.rearrange("s (j p) d -> s p j d", p=P)
        x2_v = x2_dram.rearrange("s (j p) d -> s p j d", p=P)
        LOADS = [(w_in_z[:, :, :], w["w_in"][:, :, DI:2 * DI]), (w_in_x, w["w_in"][:, :, 0:DI]), (conv_b[:, :], w["conv_b"]), (w_x[:, :, :], w["w_x"]), (w_dt[:, :], w["w_dt"]), (b_dt[:, :], w["b_dt"]),
                 (a_neg[:, :, :], w["a_log"]), (d_skip[:, :], w["d_skip"]), (w_out[:, :, :], w["w_out"])]
        ALL_LOADED = 16 * (len(LOADS) + 1)
        SETUP = 2 + TAPS * MC
        PIECES = UNITS
        X_PRODUCTS, PRODUCTS = TAPS * MC, TAPS * MC + MC
        IN_FIRST = 15

        def in_products(q):
            at = q - IN_FIRST
            return [divmod(r, PRODUCTS) for r in range(-(-at * 4 // 3), -(-(at + 1) * 4 // 3)) if 0 <= r < DC * PRODUCTS]

        block = ctx.enter_context(nc.Block())

        @block.sync
        def _(sp):
            sp.dma_start(xs[:, :, :], x_v[0]).then_inc(xs_loaded, 16)
            for dst, src in LOADS:
                sp.dma_start(dst, src).then_inc(loaded, 16)
            sp.dma_start(v[:, 0].rearrange("p j d -> p (j d)"),
                         w["conv_w"].rearrange("k d -> (k d)").partition_broadcast(P)).then_inc(loaded, 16)
            sp.sem_inc(x2_stored, 16)

            def main(m, par, first, last):
                if not last:
                    sp.wait_ge(xn_done, TT * (m + 1))
                    sp.dma_start(xs[:, :, :], row(x_v, m + 1)).then_inc(xs_loaded, 16)
                if not first:
                    sp.wait_ge(v_ready, UNITS * m + 1)
                    sp.dma_start(xr[:, :, :], row(x_v, m - 1)).then_inc(xr_loaded, 16)
                    sp.wait_ge(x2_ready, m)
                    sp.dma_start(row(x2_v, m - 1), x2[:, :, :]).then_inc(x2_stored, 16)

            over_tiles(sp, SEQS, main)
            sp.wait_ge(x2_ready, SEQS - 1)
            sp.dma_start(xr[:, :, :], x_v[SEQS - 1]).then_inc(xr_loaded, 16)
            sp.wait_ge(x2_ready, SEQS)
            sp.dma_start(x2_v[SEQS - 1], x2[:, :, :]).then_inc(x2_stored, 16)
            sp.wait_ge(x2_stored, 16 * (SEQS + 1))

        @block.gpsimd
        def _(pool):
            def prep(s, par, q):
                if q in (60, 61, 62, 63):
                    c = q - 60
                    if begun(UNITS * (s - 1)):
                        pool.wait_ge(da_ready, UNITS * (s - 1))
                    pool.wait_ge(ln_ready, DC * s + c + 1)
                    nc.gpsimd.tensor_tensor(delta[:, par, c], sp_relu[:, c], sp_abs[:, c], ALU.add).then_inc(delta_ready, 1)
                    pool.wait_ge(delta_ready, DC * s + c + 1)
                    nc.gpsimd.tensor_tensor(u[:, c], delta[:, par, c], xc[:, par, c], ALU.mult).then_inc(u_ready, 1)

            def tail(s, par, q):
                if q in (12, 13, 14, 15):
                    c = q - 12
                    pool.wait_ge(u_tp, DC * up_to(s + 2))
                    pool.wait_ge(y1_done, DC * s + c + 1)
                    nc.gpsimd.tensor_tensor(g[:, c], y1[:, c], zs[:, par, c], ALU.mult).then_inc(g_done, 1)

            def tail_end(s):
                pool.wait_ge(yn_done, TT * (s + 1))
                pool.wait_ge(xr_loaded, 16 * (s + 1))
                pool.wait_ge(x2_stored, 16 * (s + 1))
                nc.gpsimd.tensor_tensor(x2[:, :, :], o[:, :, :], xr[:, :, :], ALU.add).then_inc(x2_ready, 1)

            def main(m, par, first, last):
                pool.wait_ge(u_t_ready, DC * (m + 1))
                pool.wait_ge(bc_ready, m + 1)
                for n in range(NS):
                    if begun(UNITS * m + DC * (n - 1)):
                        pool.wait_ge(bx_done, UNITS * m + DC * (n - 1))
                    pass_waits(pool, pool_passed)
                    for j in range(TT):
                        nc.gpsimd.tensor_scalar(v[:, n % 2, j], u_t[:, par, j], bc[:, par, j, n:n + 1], 1.0,
                                                ALU.mult, ALU.mult).then_inc(v_ready, 1)
                    for q in range(DC * n, DC * (n + 1)):
                        if not first:
                            tail(m - 1, 1 - par, q)
                        if not last:
                            prep(m + 1, 1 - par, q)
                if not first:
                    tail_end(m - 1)

            nc.gpsimd.memset(ident[:, :], 0.0).then_inc(ident_ready, 1)
            nc.gpsimd.memset(eps[:, :], EPS).then_inc(ident_ready, 1)
            nc.gpsimd.memset(one[:, :], 1.0).then_inc(ident_ready, 1)
            pool.wait_ge(ident_ready, 3)
            nc.gpsimd.affine_select(out=ident[:, :], in_=ident[:, :], compare_op=ALU.not_equal, fill=1.0,
                                    base=0, pattern=[[-1, P]], channel_multiplier=1).then_inc(ident_ready, 1)
            pool.wait_ge(loaded, ALL_LOADED)
            pool.wait_ge(setup, SETUP)
            for q in range(PIECES):
                prep(0, 0, q)
            over_tiles(pool, SEQS, main)
            for q in range(PIECES):
                tail(SEQS - 1, 1, q)
            tail_end(SEQS - 1)

        @block.scalar
        def _(act):
            def prep(s, par, q):
                if q == 12:
                    act.wait_ge(mv_done, TT * (s + 1))
                    nc.scalar.activation(lnv[:, :], mv[:, :, 1], ACT.Ln, bias=eps[:, 0:1]).then_inc(lnv_done, 1)
                    act.wait_ge(lnv_done, s + 1)
                    nc.scalar.activation(rstd[:, :], lnv[:, :], ACT.Exp, scale=-0.5).then_inc(rstd_done, 1)
                if q in (17, 18):
                    k = q - 17
                    if begun(DC * s):
                        act.wait_ge(zin_done, DC * s)
                    act.wait_ge(xn_tp, MC * s + k + 1)
                    nc.scalar.activation(xn_t[:, k, PAD:PAD + T], side[:, k], ACT.Copy).then_inc(xn_t_ready, 1)
                for c in range(DC):
                    if q == (24, 32, 39, 47)[c]:
                        if begun(DC * (s - 1)):
                            act.wait_ge(y1_done, DC * (s - 1))
                        if begun(DC * (s - 1)):
                            act.wait_ge(u_ready, DC * (s - 1))
                        act.wait_ge(xin_done, DC * s + c + 1)
                        nc.scalar.activation(xc[:, par, c], side[:, 0], ACT.Identity, bias=conv_b[:, c:c + 1])\
                            .then_inc(xc_raw_ready, 1)
                    if q == (26, 34, 41, 48)[c]:
                        if begun(DC * (s - 1)):
                            act.wait_ge(g_done, DC * (s - 1))
                        act.wait_ge(zin_done, DC * s + c + 1)
                        nc.scalar.activation(zs[:, par, c], side[:, 1], ACT.Copy).then_inc(z_raw_ready, 1)
                if q == 48:
                    act.wait_ge(xc_raw_ready, DC * (s + 1))
                    nc.scalar.activation(xc[:, par], xc[:, par], ACT.Silu).then_inc(xc_ready, 1)
                    act.wait_ge(z_raw_ready, DC * (s + 1))
                    nc.scalar.activation(zs[:, par], zs[:, par], ACT.Silu).then_inc(xc_ready, 1)
                    nc.scalar.preload_act_table_set("natural_log_exp_and_others")
                if q == 53:
                    if begun(DC * s):
                        act.wait_ge(dt_done, DC * s)
                    act.wait_ge(dtr_done, s + 1)
                    nc.scalar.activation(dt_raw[:, :], side[0:DTR, 0], ACT.Copy).then_inc(dt_raw_ready, 1)
                if q == 54:
                    if begun(UNITS * (s - 1)):
                        act.wait_ge(y_done, UNITS * (s - 1))
                    if begun(UNITS * (s - 1)):
                        act.wait_ge(v_ready, UNITS * (s - 1))
                    act.wait_ge(bc_done, s + 1)
                    nc.scalar.activation(bc[:, par].rearrange("p j n -> p (j n)"), side[:, 1, 0:TT * 2 * NS], ACT.Copy)\
                        .then_inc(bc_ready, 1)
                if q in (56, 57, 58, 59):
                    c = q - 56
                    if begun(2 * (s - 1)):
                        act.wait_ge(oproj_done, 2 * (s - 1))
                    if begun(DC * (s - 1)):
                        act.wait_ge(g_done, DC * (s - 1))
                    if begun(DC * s):
                        act.wait_ge(u_tp, DC * s)
                    if begun(DC * s):
                        act.wait_ge(u_ready, DC * s)
                    act.wait_ge(dt_done, DC * s + c + 1)
                    nc.scalar.activation(sp_abs[:, c], side[:, c % 2], ACT.Abs, bias=b_dt[:, c:c + 1]).then_inc(abs_ready, 1)
                    nc.scalar.activation(sp_relu[:, c], side[:, c % 2], ACT.Relu, bias=b_dt[:, c:c + 1])\
                        .then_inc(relu_ready, 1)
                    act.wait_ge(abs_ready, DC * s + c + 1)
                    nc.scalar.activation(sp_abs[:, c], sp_abs[:, c], ACT.Exp, scale=-1.0).then_inc(exp_ready, 1)
                    act.wait_ge(exp_ready, DC * s + c + 1)
                    nc.scalar.activation(sp_abs[:, c], sp_abs[:, c], ACT.Ln, bias=one[:, 0:1]).then_inc(ln_ready, 1)

            def prep_end(s, par):
                if begun(UNITS * (s - 1)):
                    act.wait_ge(v_ready, UNITS * (s - 1))
                for c in range(DC):
                    act.wait_ge(u_tp, DC * s + c + 1)
                    nc.scalar.activation(u_t[:, par, :, c * P:(c + 1) * P],
                                         side[:, c % 2].rearrange("p (j d) -> p j d", j=TT), ACT.Copy).then_inc(u_t_ready, 1)

            def tail(s, par, q):
                if q in (50, 51):
                    k = q - 50
                    act.wait_ge(y_done, UNITS * (s + 1))
                    act.wait_ge(x2_stored, 16 * (s + 1))
                    act.wait_ge(oproj_done, 2 * s + k + 1)
                    nc.scalar.activation(o[:, 2 * k:2 * k + 2].rearrange("p j d -> p (j d)"), side[:, k], ACT.Copy)\
                        .then_inc(o_ready, 1)
                if q == 60:
                    act.wait_ge(mv2_done, TT * (s + 1))
                    nc.scalar.activation(lnv2[:, :], mv2[:, :, 1], ACT.Ln, bias=eps[:, 0:1]).then_inc(lnv2_done, 1)
                    act.wait_ge(lnv2_done, s + 1)
                    nc.scalar.activation(rstd2[:, :], lnv2[:, :], ACT.Exp, scale=-0.5).then_inc(rstd2_done, 1)

            def main(m, par, first, last):
                for n in range(NS):
                    for i in range(DC):
                        if n == 0:
                            act.wait_ge(delta_ready, DC * m + i + 1)
                        if begun(UNITS * m + DC * (n - 2) + i + 1):
                            act.wait_ge(scan_done, UNITS * m + DC * (n - 2) + i + 1)
                        nc.scalar.activation(da[:, n % 2, i], delta[:, par, i], ACT.Exp, scale=a_neg[:, i, n:n + 1])\
                            .then_inc(da_ready, 1)
                        if not first:
                            tail(m - 1, 1 - par, DC * n + i)
                        if not last:
                            prep(m + 1, 1 - par, DC * n + i)
                if not last:
                    prep_end(m + 1, 1 - par)

            act.wait_ge(loaded, ALL_LOADED)
            act.wait_ge(ident_ready, 3)
            nc.scalar.preload_act_table_set("natural_log_exp_and_others")
            nc.scalar.activation(a_neg[:, :, :], a_neg[:, :, :], ACT.Exp).then_inc(a_exp, 1)
            for q in range(PIECES):
                prep(0, 0, q)
            prep_end(0, 0)
            act.wait_ge(setup, SETUP)
            over_tiles(act, SEQS, main)
            for q in range(PIECES):
                tail(SEQS - 1, 1, q)

        @block.vector
        def _(dve):
            def prep(s, par, q):
                if q in (3, 4, 5, 6):
                    dve.wait_ge(xs_loaded, 16 * (s + 1))
                    if begun(TT * s):
                        dve.wait_ge(mv_done, TT * s)
                    nc.vector.bn_stats(stats[:, q - 3], xs[:, q - 3]).then_inc(st_done, 1)
                if q in (4, 5, 6, 7):
                    j = q - 4
                    if begun(TT * s):
                        dve.wait_ge(xn_done, TT * s)
                    dve.wait_ge(st_done, TT * s + j + 1)
                    pass_waits(dve, dve_passed)
                    nc.vector.bn_aggr(mv[:, j], stats[:, j]).then_inc(mv_done, 1)
                if q in (9, 10, 11, 12):
                    j = q - 9
                    dve.wait_ge(rstd_done, s + 1)
                    if begun(MC * s):
                        dve.wait_ge(xn_tp, MC * s)
                    nc.vector.tensor_scalar(xn[:, j], xs[:, j], mv[:, j, 0:1], rstd[:, j:j + 1],
                                            ALU.subtract, ALU.mult).then_inc(xn_done, 1)

            def tail(s, par, q):
                for c in range(DC):
                    if q == (3, 4, 7, 8)[c]:
                        dve.wait_ge(u_ready, DC * up_to(s + 2))
                        dve.wait_ge(acc_tp, DC * s + c + 1)
                        nc.vector.scalar_tensor_tensor(y1[:, c], xc[:, par, c], d_skip[:, c:c + 1], side[:, c % 2],
                                                       ALU.mult, ALU.add).then_inc(y1_done, 1)
                if q in (52, 53, 54, 55):
                    j = q - 52
                    dve.wait_ge(o_ready, 2 * s + j // 2 + 1)
                    dve.wait_ge(y_done, UNITS * (s + 1))
                    nc.vector.bn_stats(stats2[:, j], o[:, j]).then_inc(st2_done, 1)
                if q in (53, 54, 55, 56):
                    j = q - 53
                    dve.wait_ge(st2_done, TT * s + j + 1)
                    pass_waits(dve, dve_passed)
                    nc.vector.bn_aggr(mv2[:, j], stats2[:, j]).then_inc(mv2_done, 1)
                if q in (60, 61, 62, 63):
                    j = q - 60
                    dve.wait_ge(rstd2_done, s + 1)
                    nc.vector.tensor_scalar(o[:, j], o[:, j], mv2[:, j, 0:1], rstd2[:, j:j + 1],
                                            ALU.subtract, ALU.mult).then_inc(yn_done, 1)

            def main(m, par, first, last):
                for n in range(NS + 1):
                    for i in range(DC):
                        if n < NS:
                            at = UNITS * m + DC * n + i
                            if begun(UNITS * m + DC * (n - 1)):
                                dve.wait_ge(ht_done, UNITS * m + DC * (n - 1))
                            dve.wait_ge(da_ready, at + 1)
                            dve.wait_ge(bx_done, at + 1)
                            nc.vector.tensor_tensor_scan(h[:, n % 2, i], da[:, n % 2, i], bx_ps[i][:, :], 0.0,
                                                         ALU.mult, ALU.add).then_inc(scan_done, 1)
                        if n > 0:
                            at = UNITS * m + DC * (n - 1) + i
                            scale = bc[:, par, i, NS + n - 1:NS + n]
                            dve.wait_ge(ht_done, at + 1)
                            if n == 1:
                                nc.vector.tensor_scalar(y_acc[:, par, i], ht_ps[i % 2][:, :], scale, None, ALU.mult)\
                                    .then_inc(y_done, 1)
                            else:
                                dve.wait_ge(y_done, at - DC + 1)
                                nc.vector.scalar_tensor_tensor(y_acc[:, par, i], ht_ps[i % 2][:, :], scale,
                                                               y_acc[:, par, i], ALU.mult, ALU.add).then_inc(y_done, 1)
                        if n < NS:
                            if not first:
                                tail(m - 1, 1 - par, DC * n + i)
                            if not last:
                                prep(m + 1, 1 - par, DC * n + i)

            dve.wait_ge(loaded, ALL_LOADED)
            dve.wait_ge(a_exp, 1)
            nc.vector.tensor_scalar(a_neg[:, :, :], a_neg[:, :, :], -1.0, None, ALU.mult).then_inc(setup, 1)
            nc.vector.memset(xn_t[:, :, 0:PAD], 0.0).then_inc(setup, 1)
            for k in range(TAPS):
                for i in range(MC):
                    nc.vector.tensor_tensor(w_tap[:, k, i], w_in_x[:, i], tap_row[:, k], ALU.mult).then_inc(setup, 1)
            for q in range(PIECES):
                prep(0, 0, q)
            dve.wait_ge(bc_ready, 1)
            over_tiles(dve, SEQS, main)
            for q in range(PIECES):
                tail(SEQS - 1, 1, q)

        @block.tensor
        def _(pe):
            def mm(out, lhs, rhs, start, stop):
                return nc.tensor.matmul(out, lhs, rhs, start=start, stop=stop)

            def flip(out, blocks):
                for i, b in enumerate(blocks):
                    last = nc.tensor.transpose(out[:, i * P:(i + 1) * P], b, ident[:, :])
                return last

            def prep(s, par, q):
                if q in (13, 14):
                    k = q - 13
                    pe.wait_ge(xn_done, TT * (s + 1))
                    if begun(DC * s):
                        pe.wait_ge(u_t_ready, DC * s)
                    if begun(DC * (s - 1)):
                        pe.wait_ge(y1_done, DC * (s - 1))
                    flip(side[:, k], [xn[:, j, k * P:(k + 1) * P] for j in range(TT)]).then_inc(xn_tp, 1)
                for c, r in in_products(q):
                    if r < X_PRODUCTS:
                        if r == 0:
                            pe.wait_ge(xn_t_ready, MC * (s + 1))
                            if begun(DC * s + c):
                                pe.wait_ge(xc_raw_ready, DC * s + c)
                        k, e = divmod(r, MC)
                        at = PAD - (TAPS - 1) + k
                        last = mm(side[:, 0], w_tap[:, k, e, c * P:(c + 1) * P], xn_t[:, e, at:at + T], r == 0,
                                  r == X_PRODUCTS - 1)
                        if r == X_PRODUCTS - 1:
                            last.then_inc(xin_done, 1)
                    else:
                        e = r - X_PRODUCTS
                        if e == 0:
                            if begun(DC * s + c):
                                pe.wait_ge(z_raw_ready, DC * s + c)
                        last = mm(side[:, 1], w_in_z[:, e, c * P:(c + 1) * P], xn_t[:, e, PAD:PAD + T], e == 0, e == MC - 1)
                        if e == MC - 1:
                            last.then_inc(zin_done, 1)
                if q in (50, 51):
                    pe.wait_ge(xc_ready, 2 * s + 1)
                    pe.wait_ge(xc_raw_ready, DC * (s + 1))
                    if begun(2 * (s - 1)):
                        pe.wait_ge(o_ready, 2 * (s - 1))
                    for c in (2 * (q - 50), 2 * (q - 50) + 1):
                        last = mm(side[0:DTR, 0], w_x[:, c, 0:DTR], xc[:, par, c], c == 0, c == DC - 1)
                    if q == 51:
                        last.then_inc(dtr_done, 1)
                if q == 52:
                    pe.wait_ge(z_raw_ready, DC * (s + 1))
                    for j in range(TT):
                        for c in range(DC):
                            last = mm(side[:, 1, j * 2 * NS:(j + 1) * 2 * NS], xc[:, par, c, j * P:(j + 1) * P],
                                      w_x[:, c, DTR:DTR + 2 * NS], c == 0, c == DC - 1)
                    last.then_inc(bc_done, 1)
                if q in (54, 55, 56, 57):
                    c = q - 54
                    pe.wait_ge(dt_raw_ready, s + 1)
                    pe.wait_ge(bc_ready, s + 1)
                    if begun(DC * s + c - 1):
                        pe.wait_ge(relu_ready, DC * s + c - 1)
                    mm(side[:, c % 2], w_dt[:, c * P:(c + 1) * P], dt_raw[:, :], True, True).then_inc(dt_done, 1)

            def prep_end(s, par):
                pe.wait_ge(relu_ready, DC * (s + 1))
                for c in range(DC):
                    pe.wait_ge(u_ready, DC * s + c + 1)
                    if begun(DC * s + c - 1):
                        pe.wait_ge(u_t_ready, DC * s + c - 1)
                    flip(side[:, c % 2], [u[:, c, j * P:(j + 1) * P] for j in range(TT)]).then_inc(u_tp, 1)

            def tail(s, par, q):
                for c in range(DC):
                    if q == (0, 1, 4, 5)[c]:
                        pe.wait_ge(y_done, UNITS * (s + 1))
                        pe.wait_ge(u_t_ready, DC * up_to(s + 2))
                        if c >= 2:
                            pe.wait_ge(y1_done, DC * s + c - 1)
                        flip(side[:, c % 2], [y_acc[:, par, j, c * P:(c + 1) * P] for j in range(TT)]).then_inc(acc_tp, 1)
                if q in (46, 47, 48, 49):
                    j = q - 46
                    pe.wait_ge(g_done, DC * (s + 1))
                    pe.wait_ge(y1_done, DC * (s + 1))
                    pe.wait_ge(xc_raw_ready, DC * up_to(s + 3))
                    pe.wait_ge(z_raw_ready, DC * up_to(s + 3))
                    for c in range(DC):
                        last = mm(side[:, j // 2, (j % 2) * DM:(j % 2 + 1) * DM], g[:, c, j * P:(j + 1) * P],
                                  w_out[:, c], c == 0, c == DC - 1)
                    if j % 2:
                        last.then_inc(oproj_done, 1)

            def main(m, par, first, last):
                for n in range(NS + 1):
                    for i in range(DC):
                        if n < NS:
                            at = UNITS * m + DC * n + i
                            pe.wait_ge(v_ready, UNITS * m + TT * (n + 1))
                            if begun(at - DC + 1):
                                pe.wait_ge(scan_done, at - DC + 1)
                            flip(bx_ps[i], [v[:, n % 2, j, i * P:(i + 1) * P] for j in range(TT)]).then_inc(bx_done, 1)
                        if n > 0:
                            at = UNITS * m + DC * (n - 1) + i
                            pe.wait_ge(scan_done, UNITS * m + DC * n)
                            if begun(at - 1):
                                pe.wait_ge(y_done, at - 1)
                            flip(ht_ps[i % 2], [h[:, (n - 1) % 2, c, i * P:(i + 1) * P] for c in range(DC)])\
                                .then_inc(ht_done, 1)
                        if n < NS:
                            if not first:
                                tail(m - 1, 1 - par, DC * n + i)
                            if not last:
                                prep(m + 1, 1 - par, DC * n + i)
                if not last:
                    prep_end(m + 1, 1 - par)

            pe.wait_ge(loaded, ALL_LOADED)
            pe.wait_ge(ident_ready, 4)
            pe.wait_ge(setup, SETUP)
            for q in range(PIECES):
                prep(0, 0, q)
            prep_end(0, 0)
            over_tiles(pe, SEQS, main)
            for q in range(PIECES):
                tail(SEQS - 1, 1, q)



def ffn_phase(nc, x2_dram, w, out, consts):
    ident, eps, _ = consts
    with ExitStack() as ctx:
        def sb(name, shape):
            return ctx.enter_context(nc.sbuf_tensor("f_" + name, shape, F32))

        def sem(name):
            return ctx.enter_context(nc.semaphore("f_" + name))

        HG = 2 * ER + E
        DZ = DM + ER
        GROUPS = SEQS
        w_h = sb("w_h", [P, MC, HG])
        w_gate = sb("w_gate", [P, MC, FF])
        w_up = sb("w_up", [P, MC, FF])
        b_gate = sb("b_gate", [P, FF])
        b_up = sb("b_up", [P, FF])
        w_dz = sb("w_dz", [P, FC, DZ])
        b_down = sb("b_down", [P, DM])
        rank = sb("rank", [P, TT, E])
        xg = sb("xg", [P, TT, DM])
        xg_stats = sb("xg_stats", [P, TT, 6])
        xg_mv = sb("xg_mv", [P, TT, 2])
        xg_lnv = sb("xg_lnv", [P, TT])
        xg_rstd = sb("xg_rstd", [P, TT])
        xn = sb("xn", [P, TT, DM])
        x_t = sb("x_t", [P, 2, MC, T])
        hg = sb("hg", [P, TT, HG])
        row_max = sb("row_max", [P, TT])
        shifted = sb("shifted", [P, TT, E])
        expd = sb("expd", [P, TT, E])
        row_sum = sb("row_sum", [P, TT])
        row_inv = sb("row_inv", [P, TT])
        probs = sb("probs", [P, 2, TT, E])
        top = sb("top", [P, 2, TT])
        equal = sb("equal", [P, 2, TT, E])
        key = sb("key", [P, 2, TT, E])
        key_max = sb("key_max", [P, 2, TT])
        chosen = sb("chosen", [P, 2, TT, E])
        top_sum = sb("top_sum", [P, TT])
        top_inv = sb("top_inv", [P, TT])
        diff = sb("diff", [P, TT, E])
        pick = sb("pick", [P, 2, TT, E])
        route = sb("route", [P, 3, 2 * TT * (E + 1)])
        hm = sb("hm", [P, 2, TT, 2, ER])
        hm_t = sb("hm_t", [P, 2, 2, 2, T])
        silu = sb("silu", [P, 2, T])
        a = sb("a", [P, 2, 2, FC, T])
        o = sb("o", [P, 2, TT, DM])
        zm = sb("zm", [P, 2, TT, ER])
        zm_tmp = sb("zm_tmp", [P, ER])
        zm_t = sb("zm_t", [P, T])
        stats = sb("stats", [P, TT, 6])
        mv = sb("mv", [P, TT, 2])
        lnv = sb("lnv", [P, TT])
        rstd = sb("rstd", [P, TT])
        xr = sb("xr", [P, TT, DM])
        y = sb("y", [P, TT, DM])

        def routed(age):
            return (route[:, age, 0:2 * TT * E].rearrange("p (k j e) -> p k j e", k=2, j=TT),
                    route[:, age, 2 * TT * E:2 * TT * (E + 1)].rearrange("p (k j) -> p k j", k=2))

        gu_ps = ctx.enter_context(nc.psum_tensor("gu_ps", [P, 2, 2, 512], F32))
        dz_ps = ctx.enter_context(nc.psum_tensor("dz_ps", [P, 2, 512], F32))
        side = ctx.enter_context(nc.psum_tensor("f_side", [P, 2, 512], F32))

        loaded = sem("loaded")
        const_ready = sem("const_ready")
        xg_loaded = sem("xg_loaded")
        dve_passed = sem("dve_passed")
        xg_st_done = sem("xg_st_done")
        xg_mv_done = sem("xg_mv_done")
        xg_lnv_done = sem("xg_lnv_done")
        xg_rstd_done = sem("xg_rstd_done")
        xn_done = sem("xn_done")
        xn_tp = sem("xn_tp")
        x_t_ready = sem("x_t_ready")
        hg_done = sem("hg_done")
        hg_ready = sem("hg_ready")
        rt = sem("rt")
        exp_done = sem("exp_done")
        route_shift = sem("route_shift")
        hm_ready = sem("hm_ready")
        hm_tp = sem("hm_tp")
        hm_t_ready = sem("hm_t_ready")
        base_done = sem("base_done")
        diff_done = sem("diff_done")
        silu_ready = sem("silu_ready")
        a_ready = sem("a_ready")
        dz_done = sem("dz_done")
        o_step = sem("o_step")
        zm_step = sem("zm_step")
        z_tp = sem("z_tp")
        z_t_ready = sem("z_t_ready")
        b_done = sem("b_done")
        o_ready = sem("o_ready")
        st_done = sem("st_done")
        mv_done = sem("mv_done")
        lnv_done = sem("lnv_done")
        rstd_done = sem("rstd_done")
        yn_done = sem("yn_done")
        xr_loaded = sem("xr_loaded")
        y_ready = sem("y_ready")
        y_stored = sem("y_stored")

        x_v = x2_dram.rearrange("s (j p) d -> s p j d", p=P)
        out_v = out.rearrange("s (j p) d -> s p j d", p=P)
        LOADS = [(w_h[:, :, :], w["w_h"]), (w_gate[:, :, :], w["w_gate"]), (w_up[:, :, :], w["w_up"]),
                 (b_gate[:, :], w["b_gate"]), (b_up[:, :], w["b_up"]), (w_dz[:, :, :], w["w_dz"]), (b_down[:, :], w["b_down"])]
        ALL_LOADED = 16 * len(LOADS)
        RT = 25
        OWN = TT * 2
        CONSTS = E + 1

        def over_groups(main):
            def run(eng):
                main(0, 0, True, False, False, True, True)
                main(1, 1, True, True, False, True, True)
                with eng.Fori(2, GROUPS - 3, 2) as m:
                    main(m, 0, True, True, True, True, True)
                    main(m + 1, 1, True, True, True, True, True)
                main(GROUPS - 2, 0, True, True, True, True, False)
                main(GROUPS - 1, 1, True, True, True, False, False)
                main(GROUPS, 0, False, True, True, False, False)
                main(GROUPS + 1, 1, False, False, True, False, False)
            return run

        block = ctx.enter_context(nc.Block())

        @block.sync
        def _(sp):
            sp.dma_start(xg[:, :, :], x_v[0]).then_inc(xg_loaded, 16)
            for dst, src in LOADS:
                sp.dma_start(dst, src).then_inc(loaded, 16)
            sp.wait_ge(xn_done, TT)
            sp.dma_start(xg[:, :, :], x_v[1]).then_inc(xg_loaded, 16)
            sp.sem_inc(y_stored, 16)

            def main(m, par, act_on, dz_on, tail_on, prep_on, norm_on):
                if norm_on:
                    sp.wait_ge(xn_done, TT * (m + 2))
                    sp.dma_start(xg[:, :, :], row(x_v, m + 2)).then_inc(xg_loaded, 16)
                if tail_on:
                    sp.wait_ge(y_stored, 16 * (m - 1))
                    sp.dma_start(xr[:, :, :], row(x_v, m - 2)).then_inc(xr_loaded, 16)
                    sp.wait_ge(y_ready, m)
                    sp.dma_start(row(out_v, m - 2), y[:, :, :]).then_inc(y_stored, 16)

            over_groups(main)(sp)
            sp.wait_ge(y_stored, 16 * (GROUPS + 1))

        @block.gpsimd
        def _(pool):
            def prep(s, par, f):
                if f == 6:
                    pool.wait_ge(rt, RT * (s + 1))
                    if begun(4 * s):
                        pool.wait_ge(hm_tp, 4 * s)
                    for k in range(2):
                        for j in range(TT):
                            nc.gpsimd.tensor_tensor(
                                hm[:, k, j].rearrange("p t (e r) -> p t e r", e=E),
                                hg[:, j, 0:2 * ER].rearrange("p (t e r) -> p t e r", t=2, e=E),
                                pick[:, k, j].unsqueeze(1).unsqueeze(3).broadcast_to([P, 2, E, R]), ALU.mult)\
                                .then_inc(hm_ready, 1)

            def tail(s, par, f):
                if f == 7:
                    pool.wait_ge(yn_done, TT * (s + 1))
                    pool.wait_ge(xr_loaded, 16 * (s + 1))
                    pool.wait_ge(y_stored, 16 * (s + 1))
                    nc.gpsimd.tensor_tensor(y[:, :, :], o[:, par], xr[:, :, :], ALU.add).then_inc(y_ready, 1)

            def main(m, par, act_on, dz_on, tail_on, prep_on, norm_on):
                for f in range(FC):
                    if tail_on:
                        tail(m - 2, par, f)
                    if prep_on:
                        prep(m + 1, 1 - par, f)

            for e in range(E):
                nc.gpsimd.memset(rank[:, :, e:e + 1], float(E - e)).then_inc(const_ready, 1)
            nc.gpsimd.memset(route[:, :, :], 0.0).then_inc(const_ready, 1)
            pool.sem_inc(y_ready, 1)
            for f in range(FC):
                prep(0, 0, f)
            over_groups(main)(pool)

        @block.scalar
        def _(act):
            def prep(s, par, f):
                if f == 2:
                    if begun(FC * (s - 1)):
                        act.wait_ge(base_done, FC * (s - 1))
                    for k in range(MC):
                        act.wait_ge(xn_tp, MC * s + k + 1)
                        nc.scalar.activation(x_t[:, par, k], side[:, k], ACT.Copy).then_inc(x_t_ready, 1)
                if f in (3, 4):
                    if begun(OWN * s):
                        act.wait_ge(hm_ready, OWN * s)
                    for j in (2 * (f - 3), 2 * (f - 3) + 1):
                        act.wait_ge(hg_done, TT * s + j + 1)
                        nc.scalar.activation(hg[:, j], side[:, j % 2, 0:HG], ACT.Copy).then_inc(hg_ready, 1)
                if f == 5:
                    act.wait_ge(rt, RT * s + 2)
                    nc.scalar.activation(expd[:, :, :], shifted[:, :, :], ACT.Exp).then_inc(exp_done, 1)
                if f == 7:
                    if begun(FC * (s - 1)):
                        act.wait_ge(diff_done, FC * (s - 1))
                    for i in range(4):
                        k, t = divmod(i, 2)
                        act.wait_ge(hm_tp, 4 * s + i + 1)
                        nc.scalar.activation(hm_t[:, par, k, t], side[:, i % 2], ACT.Copy).then_inc(hm_t_ready, 1)

            def norm(s, f):
                if f == 5:
                    act.wait_ge(xg_mv_done, TT * (s + 1))
                    nc.scalar.activation(xg_lnv[:, :], xg_mv[:, :, 1], ACT.Ln, bias=eps[:, 0:1]).then_inc(xg_lnv_done, 1)
                    act.wait_ge(xg_lnv_done, s + 1)
                    nc.scalar.activation(xg_rstd[:, :], xg_lnv[:, :], ACT.Exp, scale=-0.5).then_inc(xg_rstd_done, 1)

            def tail(s, par, f):
                if f == 0:
                    act.wait_ge(z_tp, s + 1)
                    nc.scalar.activation(zm_t[:, :], side[:, 0], ACT.Copy).then_inc(z_t_ready, 1)
                if f == 5:
                    act.wait_ge(mv_done, TT * (s + 1))
                    nc.scalar.activation(lnv[:, :], mv[:, :, 1], ACT.Ln, bias=eps[:, 0:1]).then_inc(lnv_done, 1)
                    act.wait_ge(lnv_done, s + 1)
                    nc.scalar.activation(rstd[:, :], lnv[:, :], ACT.Exp, scale=-0.5).then_inc(rstd_done, 1)

            def main(m, par, act_on, dz_on, tail_on, prep_on, norm_on):
                for f in range(FC):
                    if act_on:
                        for k in range(2):
                            at = 2 * (FC * m + f) + k
                            act.wait_ge((base_done, diff_done)[k], FC * m + f + 1)
                            if begun(at - 1):
                                act.wait_ge(a_ready, at - 1)
                            nc.scalar.activation(silu[:, k], gu_ps[:, f % 2, 0], ACT.Silu).then_inc(silu_ready, 1)
                    if f == 5:
                        nc.scalar.preload_act_table_set("natural_log_exp_and_others")
                    if tail_on:
                        tail(m - 2, par, f)
                    if prep_on:
                        prep(m + 1, 1 - par, f)
                    if norm_on:
                        norm(m + 2, f)

            nc.scalar.preload_act_table_set("natural_log_exp_and_others")
            for f in range(FC):
                norm(0, f)
            for f in range(FC):
                prep(0, 0, f)
            for f in range(FC):
                norm(1, f)
            over_groups(main)(act)

        @block.vector
        def _(dve):
            def last_axis(ap):
                return ap.unsqueeze(2).broadcast_to([P, TT, E])

            def prep(s, par, f):
                logits = hg[:, :, 2 * ER:HG]
                masks, weights = routed(0)
                if f == 4:
                    dve.wait_ge(hg_ready, TT * (s + 1))
                    if begun(2 * s):
                        dve.wait_ge(route_shift, 2 * s)
                    if begun(RT * s):
                        dve.wait_ge(rt, RT * s)
                    nc.vector.tensor_reduce(row_max[:, :], logits, AX.X, ALU.max).then_inc(rt, 1)
                    dve.wait_ge(rt, RT * s + 1)
                    nc.vector.tensor_tensor(shifted[:, :, :], logits, last_axis(row_max[:, :]), ALU.subtract).then_inc(rt, 1)
                if f == 5:
                    dve.wait_ge(exp_done, s + 1)
                    if begun(OWN * s):
                        dve.wait_ge(hm_ready, OWN * s)
                    dve.wait_ge(rt, RT * s + 2)
                    nc.vector.tensor_reduce(row_sum[:, :], expd[:, :, :], AX.X, ALU.add).then_inc(rt, 1)
                    dve.wait_ge(rt, RT * s + 3)
                    nc.vector.reciprocal(row_inv[:, :], row_sum[:, :]).then_inc(rt, 1)
                    dve.wait_ge(rt, RT * s + 4)
                    nc.vector.tensor_tensor(probs[:, 0], expd[:, :, :], last_axis(row_inv[:, :]), ALU.mult).then_inc(rt, 1)
                    for k in range(2):
                        at = RT * s + 5 + 6 * k
                        dve.wait_ge(rt, at)
                        nc.vector.tensor_reduce(top[:, k], probs[:, k], AX.X, ALU.max).then_inc(rt, 1)
                        dve.wait_ge(rt, at + 1)
                        nc.vector.tensor_tensor(equal[:, k], probs[:, k], last_axis(top[:, k]), ALU.is_equal).then_inc(rt, 1)
                        dve.wait_ge(rt, at + 2)
                        nc.vector.tensor_tensor(key[:, k], equal[:, k], rank[:, :, :], ALU.mult).then_inc(rt, 1)
                        dve.wait_ge(rt, at + 3)
                        nc.vector.tensor_reduce(key_max[:, k], key[:, k], AX.X, ALU.max).then_inc(rt, 1)
                        dve.wait_ge(rt, at + 4)
                        nc.vector.tensor_tensor(chosen[:, k], key[:, k], last_axis(key_max[:, k]), ALU.is_equal).then_inc(rt, 1)
                        if k == 0:
                            dve.wait_ge(rt, at + 5)
                            nc.vector.scalar_tensor_tensor(probs[:, 1], chosen[:, 0], -2.0, probs[:, 0],
                                                           ALU.mult, ALU.add).then_inc(rt, 1)
                    dve.wait_ge(rt, RT * s + 16)
                    nc.vector.tensor_tensor(top_sum[:, :], top[:, 0], top[:, 1], ALU.add).then_inc(rt, 1)
                    dve.wait_ge(rt, RT * s + 17)
                    nc.vector.reciprocal(top_inv[:, :], top_sum[:, :]).then_inc(rt, 1)
                    dve.wait_ge(rt, RT * s + 18)
                    nc.vector.tensor_tensor(weights[:, 0], top[:, 0], top_inv[:, :], ALU.mult).then_inc(rt, 1)
                    dve.wait_ge(rt, RT * s + 19)
                    nc.vector.tensor_tensor(weights[:, 1], top[:, 1], top_inv[:, :], ALU.mult).then_inc(rt, 1)
                    dve.wait_ge(rt, RT * s + 20)
                    nc.vector.tensor_scalar(pick[:, 0], chosen[:, 0], LORA_SCALE, None, ALU.mult).then_inc(rt, 1)
                    dve.wait_ge(rt, RT * s + 21)
                    nc.vector.tensor_tensor(diff[:, :, :], chosen[:, 1], chosen[:, 0], ALU.subtract).then_inc(rt, 1)
                    dve.wait_ge(rt, RT * s + 22)
                    nc.vector.tensor_scalar(pick[:, 1], diff[:, :, :], LORA_SCALE, None, ALU.mult).then_inc(rt, 1)
                    for k in range(2):
                        dve.wait_ge(rt, RT * s + 23 + k)
                        nc.vector.scalar_tensor_tensor(masks[:, k], chosen[:, k], LORA_SCALE, last_axis(weights[:, k]),
                                                       ALU.mult, ALU.mult).then_inc(rt, 1)

            def norm(s, f):
                if f == 3:
                    dve.wait_ge(xg_loaded, 16 * (s + 1))
                    for j in range(TT):
                        nc.vector.bn_stats(xg_stats[:, j], xg[:, j]).then_inc(xg_st_done, 1)
                    dve.wait_ge(xg_st_done, TT * (s + 1))
                    pass_waits(dve, dve_passed)
                    for j in range(TT):
                        nc.vector.bn_aggr(xg_mv[:, j], xg_stats[:, j]).then_inc(xg_mv_done, 1)
                if f == 6:
                    dve.wait_ge(xg_rstd_done, s + 1)
                    if begun(MC * s):
                        dve.wait_ge(xn_tp, MC * s)
                    for j in range(TT):
                        nc.vector.tensor_scalar(xn[:, j], xg[:, j], xg_mv[:, j, 0:1], xg_rstd[:, j:j + 1],
                                                ALU.subtract, ALU.mult).then_inc(xn_done, 1)

            def tail(s, par, f):
                if f == 1:
                    for k in range(2):
                        tiles = o[:, par, 2 * k:2 * k + 2].rearrange("p j d -> p (j d)")
                        dve.wait_ge(b_done, 2 * s + k + 1)
                        dve.wait_ge(o_step, OWN * (s + 1))
                        nc.vector.tensor_tensor(tiles, side[:, 1 - k], tiles, ALU.add).then_inc(o_ready, 1)
                if f == 2:
                    dve.wait_ge(o_ready, 2 * (s + 1))
                    for j in range(TT):
                        nc.vector.bn_stats(stats[:, j], o[:, par, j]).then_inc(st_done, 1)
                    dve.wait_ge(st_done, TT * (s + 1))
                    pass_waits(dve, dve_passed)
                    for j in range(TT):
                        nc.vector.bn_aggr(mv[:, j], stats[:, j]).then_inc(mv_done, 1)
                if f == 6:
                    dve.wait_ge(rstd_done, s + 1)
                    for j in range(TT):
                        nc.vector.tensor_scalar(o[:, par, j], o[:, par, j], mv[:, j, 0:1], rstd[:, j:j + 1],
                                                ALU.subtract, ALU.mult).then_inc(yn_done, 1)

            def unit(g, par, f):
                masks, weights = routed(2)
                j, k = divmod(f, 2)
                by_expert = (lambda ap: ap.rearrange("p (e r) -> p e r", e=E))
                z = by_expert(dz_ps[:, k, DM:DZ])
                mask = masks[:, k, j].unsqueeze(2).broadcast_to([P, E, R])
                dve.wait_ge(dz_done, OWN * g + f + 1)
                if k == 0:
                    if j == 0:
                        if begun(g):
                            dve.wait_ge(y_ready, g)
                    nc.vector.tensor_scalar(o[:, par, j], dz_ps[:, 0, 0:DM], weights[:, 0, j:j + 1], None, ALU.mult)\
                        .then_inc(o_step, 1)
                    nc.vector.tensor_tensor(by_expert(zm[:, par, j]), z, mask, ALU.mult).then_inc(zm_step, 1)
                else:
                    dve.wait_ge(o_step, OWN * g + f)
                    nc.vector.scalar_tensor_tensor(o[:, par, j], dz_ps[:, 1, 0:DM], weights[:, 1, j:j + 1], o[:, par, j],
                                                   ALU.mult, ALU.add).then_inc(o_step, 1)
                    nc.vector.tensor_tensor(by_expert(zm_tmp[:, :]), z, mask, ALU.mult).then_inc(zm_step, 1)
                    dve.wait_ge(zm_step, 3 * (TT * g + j) + 2)
                    nc.vector.tensor_tensor(zm[:, par, j], zm[:, par, j], zm_tmp[:, :], ALU.add).then_inc(zm_step, 1)

            def shift(m):
                for age in (2, 1):
                    if begun(2 * (m + 1) + 2 - age):
                        dve.wait_ge(route_shift, 2 * (m + 1) + 2 - age)
                    if age == 1:
                        dve.wait_ge(rt, RT * up_to(m + 2))
                    nc.vector.tensor_copy(route[:, age], route[:, age - 1]).then_inc(route_shift, 1)

            def main(m, par, act_on, dz_on, tail_on, prep_on, norm_on):
                if act_on:
                    if begun(OWN * (m - 1)):
                        dve.wait_ge(dz_done, OWN * (m - 1))
                if dz_on:
                    dve.wait_ge(route_shift, 2 * (m + 1))
                for f in range(FC):
                    for k in range(2):
                        if act_on:
                            at = 2 * (FC * m + f) + k
                            dve.wait_ge(silu_ready, at + 1)
                            nc.vector.tensor_tensor(a[:, par, k, f], silu[:, k], gu_ps[:, f % 2, 1], ALU.mult)\
                                .then_inc(a_ready, 1)
                        if k == 0 and dz_on:
                            unit(m - 1, 1 - par, f)
                    if tail_on:
                        tail(m - 2, par, f)
                    if prep_on:
                        prep(m + 1, 1 - par, f)
                    if norm_on:
                        norm(m + 2, f)
                if dz_on or act_on:
                    shift(m)

            dve.wait_ge(const_ready, CONSTS)
            for f in range(FC):
                norm(0, f)
            for f in range(FC):
                prep(0, 0, f)
            shift(-1)
            for f in range(FC):
                norm(1, f)
            over_groups(main)(dve)

        @block.tensor
        def _(pe):
            def mm(out_, lhs, rhs, start, stop):
                return nc.tensor.matmul(out_, lhs, rhs, start=start, stop=stop)

            def flip(out_, blocks):
                for i, b in enumerate(blocks):
                    last = nc.tensor.transpose(out_[:, i * P:(i + 1) * P], b, ident[:, :])
                return last

            def prep(s, par, f):
                if f == 2:
                    pe.wait_ge(xn_done, TT * (s + 1))
                    if begun(4 * s):
                        pe.wait_ge(hm_t_ready, 4 * s)
                    if not isinstance(s, int) or s > 2:
                        pe.wait_ge(o_ready, 2 * (s - 2))
                    for k in range(MC):
                        flip(side[:, k], [xn[:, j, k * P:(k + 1) * P] for j in range(TT)]).then_inc(xn_tp, 1)
                if f in (3, 4):
                    pe.wait_ge(x_t_ready, MC * (s + 1))
                    for j in (2 * (f - 3), 2 * (f - 3) + 1):
                        if begun(TT * s + j - 1):
                            pe.wait_ge(hg_ready, TT * s + j - 1)
                        for k in range(MC):
                            last = mm(side[:, j % 2, 0:HG], x_t[:, par, k, j * P:(j + 1) * P], w_h[:, k], k == 0, k == MC - 1)
                        last.then_inc(hg_done, 1)
                if f == 7:
                    pe.wait_ge(hm_ready, OWN * (s + 1))
                    pe.wait_ge(hg_ready, TT * (s + 1))
                    for i in range(4):
                        k, t = divmod(i, 2)
                        if begun(4 * s + i - 1):
                            pe.wait_ge(hm_t_ready, 4 * s + i - 1)
                        flip(side[:, i % 2], [hm[:, k, j, t] for j in range(TT)]).then_inc(hm_tp, 1)

            def tail(s, par, f):
                if f == 0:
                    pe.wait_ge(zm_step, 3 * TT * (s + 1))
                    pe.wait_ge(hm_t_ready, 4 * up_to(s + 3))
                    flip(side[:, 0], [zm[:, par, j] for j in range(TT)]).then_inc(z_tp, 1)
                if f == 1:
                    pe.wait_ge(z_t_ready, s + 1)
                    for j in range(TT):
                        last = mm(side[:, 1 - j // 2, (j % 2) * DM:(j % 2 + 1) * DM], zm_t[:, j * P:(j + 1) * P],
                                  b_down[:, :], True, True)
                        if j % 2:
                            last.then_inc(b_done, 1)

            def main(m, par, act_on, dz_on, tail_on, prep_on, norm_on):
                for f in range(FC):
                    cols = slice(f * P, (f + 1) * P)
                    if act_on:
                        at = 2 * (FC * m + f)
                        if f == 0:
                            pe.wait_ge(x_t_ready, MC * (m + 1))
                        if begun(at - 2):
                            pe.wait_ge(a_ready, at - 2)
                        for t, wide, lora in ((0, w_gate, b_gate), (1, w_up, b_up)):
                            for k in range(MC):
                                mm(gu_ps[:, f % 2, t], wide[:, k, cols], x_t[:, par, k], k == 0, False)
                            if f == 0 and t == 0:
                                pe.wait_ge(hm_t_ready, 4 * (m + 1))
                            last = mm(gu_ps[:, f % 2, t], lora[:, cols], hm_t[:, par, 0, t], False, True)
                        last.then_inc(base_done, 1)
                    if dz_on:
                        g, j, k = m - 1, f // 2, f % 2
                        if f == 0:
                            pe.wait_ge(a_ready, 2 * FC * m)
                        if begun(3 * (TT * g + j - 1) + 1 + k):
                            pe.wait_ge(zm_step, 3 * (TT * g + j - 1) + 1 + k)
                        for c in range(FC):
                            last = mm(dz_ps[:, k, 0:DZ], a[:, 1 - par, k, c, j * P:(j + 1) * P], w_dz[:, c],
                                      c == 0, c == FC - 1)
                        last.then_inc(dz_done, 1)
                    if act_on:
                        pe.wait_ge(a_ready, at + 1)
                        for t, lora in ((0, b_gate), (1, b_up)):
                            last = nc.tensor.matmul(gu_ps[:, f % 2, t], lora[:, cols], hm_t[:, par, 1, t], start=False,
                                                    stop=True, skip_group_check=True)
                        last.then_inc(diff_done, 1)
                    if tail_on:
                        tail(m - 2, par, f)
                    if prep_on:
                        prep(m + 1, 1 - par, f)

            pe.wait_ge(loaded, ALL_LOADED)
            for f in range(FC):
                prep(0, 0, f)
            over_groups(main)(pe)


@contextmanager
def consts_of(nc):
    with (nc.sbuf_tensor("ident", [P, P], F32) as ident, nc.sbuf_tensor("eps", [P, 1], F32) as eps,
          nc.sbuf_tensor("one", [P, 1], F32) as one):
        yield ident, eps, one


def build(nc, dram, out):
    x2 = nc.dram_tensor("x2_between", out.shape, F32, kind="Internal").ap()
    with consts_of(nc) as consts:
        mamba_phase(nc, dram["x"], dram, x2, consts)
        ffn_phase(nc, x2, dram, out, consts)


def lay_out(i):
    import numpy as np

    def chunks(a):
        a = np.asarray(a)
        return np.ascontiguousarray(a.reshape(-1, P, *a.shape[1:]).swapaxes(0, 1))

    at, ff = (lambda n: np.asarray(i["L0_attn_" + n])), (lambda n: np.asarray(i["L0_ffn_" + n]))
    return {
        "x": at("x"),
        "w_in": chunks(at("W_in").T), "conv_w": np.ascontiguousarray(at("conv_w").T), "conv_b": chunks(at("conv_b")),
        "w_x": chunks(at("W_x").T), "w_dt": np.ascontiguousarray(at("W_dt").T), "b_dt": chunks(at("b_dt")),
        "a_log": chunks(at("A_log")), "d_skip": chunks(at("Dp")), "w_out": chunks(at("W_out").T),
        "w_h": chunks(np.concatenate([ff("A1").reshape(ER, DM), ff("A3").reshape(ER, DM), ff("gate_w")]).T),
        "w_gate": chunks(ff("w_gate").T), "w_up": chunks(ff("w_up").T),
        "b_gate": np.ascontiguousarray(ff("B1").transpose(0, 2, 1).reshape(ER, FF)),
        "b_up": np.ascontiguousarray(ff("B3").transpose(0, 2, 1).reshape(ER, FF)),
        "w_dz": chunks(np.concatenate([ff("w_down"), ff("A2").reshape(ER, FF)]).T),
        "b_down": np.ascontiguousarray(ff("B2").transpose(0, 2, 1).reshape(ER, DM)),
    }


def kernel(**inputs):
    import numpy as np
    import concourse.bacc as bacc
    from concourse.bass_utils import run_bass_kernel_spmd

    arrays = lay_out(inputs)
    nc = bacc.Bacc("TRN2", target_bir_lowering=False, num_devices=1)
    dram = {n: nc.dram_tensor("in_" + n, a.shape, mybir.dt.from_np(a.dtype), kind="ExternalInput").ap()
            for n, a in arrays.items()}
    out = nc.dram_tensor("out", arrays["x"].shape, F32, kind="ExternalOutput").ap()
    build(nc, dram, out)
    r = run_bass_kernel_spmd(nc, [{"in_" + n: a for n, a in arrays.items()}], core_ids=[0])
    return r.results[0]["out"]
```

```python
import math
from contextlib import ExitStack, contextmanager

import concourse.bass as bass
import concourse.mybir as mybir
from concourse.alu_op_type import AluOpType as ALU

F32 = mybir.dt.float32
F32R = mybir.dt.float32r
ACT = mybir.ActivationFunctionType
AX = mybir.AxisListType

P = 128
SEQS, T, DM = 16, 512, 256
DI, NS, DTR, TAPS = 512, 16, 64, 4
TT, MC, DC = T // P, DM // P, DI // P
UNITS = NS * DC
E, R, FF = 8, 16, 1024
ER, FC = E * R, FF // P
EPS = 1e-5
LORA_SCALE = 2.0


def begun(count):
    return not isinstance(count, int) or count > 0


def pass_waits(eng, passed):
    eng.sem_inc(passed, 1)


def up_to(s):
    return min(s, SEQS) if isinstance(s, int) else s


def over_tiles(eng, count, step):
    step(0, 0, 0)
    step(1, 1, 1)
    with eng.Fori(2, count - 3, 2) as i:
        step(i, 0, None)
        step(i + 1, 1, None)
    step(count - 2, 0, count - 2)
    step(count - 1, 1, count - 1)


def row(ap4, s):
    if isinstance(s, int):
        return ap4[s]
    return ap4[bass.ds(s, 1)].rearrange("a p j d -> (a p) j d")


def mamba_phase(nc, x, w, x2_dram, consts):
    ident, eps, one = consts
    with ExitStack() as ctx:
        def sb(name, shape):
            return ctx.enter_context(nc.sbuf_tensor(name, shape, F32))

        def sem(name):
            return ctx.enter_context(nc.semaphore(name))

        w_in = sb("w_in", [P, MC, 2 * DI])
        conv_w = sb("conv_w", [P, DC, TAPS])
        conv_b = sb("conv_b", [P, DC])
        w_x = sb("w_x", [P, DC, DTR + 2 * NS])
        w_dt = sb("w_dt", [DTR, DI])
        b_dt = sb("b_dt", [P, DC])
        a_neg = sb("a_neg", [P, DC, NS])
        d_skip = sb("d_skip", [P, DC])
        w_out = sb("w_out", [P, DC, DM])
        xs = sb("xs", [P, TT, DM])
        stats = sb("stats", [P, TT, 6])
        mv = sb("mv", [P, TT, 2])
        lnv = sb("lnv", [P, TT])
        rstd = sb("rstd", [P, TT])
        xn = sb("xn", [P, TT, DM])
        xn_t = sb("xn_t", [P, MC, T])
        tap = sb("tap", [P, 2, TAPS - 1, T])
        xc = sb("xc", [P, 2, DC, T])
        zs = sb("zs", [P, 2, DC, T])
        dt_raw = sb("dt_raw", [DTR, T])
        bc = sb("bc", [P, 2, TT, 2 * NS])
        delta = sb("delta", [P, 2, DC, T])
        u_t = sb("u_t", [P, 2, TT, DI])
        v = sb("v", [P, 2, TT, DI])
        da = sb("da", [P, 2, DC, T])
        h = sb("h", [P, 2, DC, T])
        y_acc = sb("y_acc", [P, 2, TT, DI])
        o = sb("o", [P, TT, DM])
        stats2 = sb("stats2", [P, TT, 6])
        mv2 = sb("mv2", [P, TT, 2])
        lnv2 = sb("lnv2", [P, TT])
        rstd2 = sb("rstd2", [P, TT])
        xr = sb("xr", [P, TT, DM])
        x2 = sb("x2", [P, TT, DM])
        work_a = sb("work_a", [P, DC, T])
        work_b = sb("work_b", [P, DC, T])
        y1, sp_abs = work_a, work_a
        g, sp_relu, u = work_b, work_b, work_b

        bx_ps = [ctx.enter_context(nc.psum_tensor(f"bx_ps{i}", [P, 512], F32)) for i in range(DC)]
        ht_ps = [ctx.enter_context(nc.psum_tensor(f"ht_ps{i}", [P, 512], F32)) for i in range(2)]
        side = ctx.enter_context(nc.psum_tensor("side", [P, 2, 512], F32))

        loaded = sem("loaded")
        a_exp = sem("a_exp")
        setup = sem("setup")
        ident_ready = sem("ident_ready")
        xs_loaded = sem("xs_loaded")
        dve_passed = sem("dve_passed")
        pool_passed = sem("pool_passed")
        st_done = sem("st_done")
        mv_done = sem("mv_done")
        rstd_done = sem("rstd_done")
        xn_done = sem("xn_done")
        xn_tp = sem("xn_tp")
        xn_t_ready = sem("xn_t_ready")
        xin_done = sem("xin_done")
        zin_done = sem("zin_done")
        tap_step = sem("tap_step")
        tap_ready = sem("tap_ready")
        conv_step = sem("conv_step")
        z_raw_ready = sem("z_raw_ready")
        xc_ready = sem("xc_ready")
        dtr_done = sem("dtr_done")
        bc_done = sem("bc_done")
        dt_raw_ready = sem("dt_raw_ready")
        bc_ready = sem("bc_ready")
        dt_done = sem("dt_done")
        abs_ready = sem("abs_ready")
        relu_ready = sem("relu_ready")
        exp_ready = sem("exp_ready")
        ln_ready = sem("ln_ready")
        delta_ready = sem("delta_ready")
        u_ready = sem("u_ready")
        u_tp = sem("u_tp")
        u_t_ready = sem("u_t_ready")
        v_ready = sem("v_ready")
        bx_done = sem("bx_done")
        da_ready = sem("da_ready")
        scan_done = sem("scan_done")
        ht_done = sem("ht_done")
        y_done = sem("y_done")
        acc_tp = sem("acc_tp")
        y1_done = sem("y1_done")
        g_done = sem("g_done")
        oproj_done = sem("oproj_done")
        o_ready = sem("o_ready")
        st2_done = sem("st2_done")
        mv2_done = sem("mv2_done")
        lnv2_done = sem("lnv2_done")
        lnv_done = sem("lnv_done")
        rstd2_done = sem("rstd2_done")
        yn_done = sem("yn_done")
        xr_loaded = sem("xr_loaded")
        x2_ready = sem("x2_ready")
        x2_stored = sem("x2_stored")

        x_v = x.rearrange("s (j p) d -> s p j d", p=P)
        x2_v = x2_dram.rearrange("s (j p) d -> s p j d", p=P)
        LOADS = [(w_in[:, :, :], w["w_in"]), (conv_w[:, :, :], w["conv_w"]), (conv_b[:, :], w["conv_b"]),
                 (w_x[:, :, :], w["w_x"]), (w_dt[:, :], w["w_dt"]), (b_dt[:, :], w["b_dt"]),
                 (a_neg[:, :, :], w["a_log"]), (d_skip[:, :], w["d_skip"]), (w_out[:, :, :], w["w_out"])]
        ALL_LOADED = 16 * len(LOADS)
        SETUP = 1
        PIECES = UNITS + 2
        XN_FLIP = (0, 1)
        ACC_FLIP = (5, 6, 7, 8)
        X_IN, Z_IN = (10, 14, 22, 26), (18, 30, 34, 38)
        OUT = (20, 24, 28, 32, 35, 37, 40, 42)
        DT_IN, BC_IN = (46, 47, 48, 49), (50, 51, 52, 53)
        DT = (52, 55, 56, 58)
        U_FLIP = (60, 61, 63, 64)
        GATE = (12, 13, 16, 17)
        CONV = ((18, 20, 22), (24, 25, 27), (30, 31, 33), (34, 36, 38))
        DELTA = (56, 58, 60, 62)

        block = ctx.enter_context(nc.Block())

        @block.sync
        def _(sp):
            sp.dma_start(xs[:, :, :], x_v[0]).then_inc(xs_loaded, 16)
            for dst, src in LOADS:
                sp.dma_start(dst, src).then_inc(loaded, 16)
            sp.wait_ge(xn_done, TT)
            sp.dma_start(xs[:, :, :], x_v[1]).then_inc(xs_loaded, 16)
            sp.sem_inc(x2_stored, 16)

            def main(m, par, edge):
                first, last = edge == 0, edge == SEQS - 1
                ahead = edge in (None, 0, 1)
                if ahead:
                    sp.wait_ge(xn_done, TT * (m + 2))
                    sp.dma_start(xs[:, :, :], row(x_v, m + 2)).then_inc(xs_loaded, 16)
                if edge not in (0, 1):
                    sp.wait_ge(x2_ready, m - 1)
                    sp.dma_start(row(x2_v, m - 2), x2[:, :, :]).then_inc(x2_stored, 16)
                if not first:
                    sp.dma_start(xr[:, :, :], row(x_v, m - 1)).then_inc(xr_loaded, 16)

            over_tiles(sp, SEQS, main)
            sp.wait_ge(x2_ready, SEQS - 1)
            sp.dma_start(x2_v[SEQS - 2], x2[:, :, :]).then_inc(x2_stored, 16)
            sp.dma_start(xr[:, :, :], x_v[SEQS - 1]).then_inc(xr_loaded, 16)
            sp.wait_ge(x2_ready, SEQS)
            sp.dma_start(x2_v[SEQS - 1], x2[:, :, :]).then_inc(x2_stored, 16)
            sp.wait_ge(x2_stored, 16 * (SEQS + 1))

        @block.gpsimd
        def _(pool):
            def prep(s, par, q):
                for c in range(DC):
                    if q in CONV[c]:
                        back = 1 + CONV[c].index(q)
                        if back == 1:
                            pool.wait_ge(tap_ready, DC * s + c + 1)
                        else:
                            pool.wait_ge(conv_step, (TAPS - 1) * (DC * s + c) + back - 1)
                        nc.gpsimd.tensor_tensor(xc[:, par, c, back:T], xc[:, par, c, back:T],
                                                tap[:, c % 2, TAPS - 1 - back, 0:T - back], ALU.add).then_inc(conv_step, 1)

            def tail(s, par, q):
                if q in GATE:
                    c = GATE.index(q)
                    pool.wait_ge(u_tp, DC * up_to(s + 2))
                    pool.wait_ge(y1_done, DC * s + c + 1)
                    nc.gpsimd.tensor_tensor(g[:, c], y1[:, c], zs[:, par, c], ALU.mult).then_inc(g_done, 1)


            def residual(s, q):
                if q == 2:
                    pool.wait_ge(yn_done, TT * (s + 1))
                    pool.wait_ge(xr_loaded, 16 * (s + 1))
                    pool.wait_ge(x2_stored, 16 * (s + 1))
                    nc.gpsimd.tensor_tensor(x2[:, :, :], o[:, :, :], xr[:, :, :], ALU.add).then_inc(x2_ready, 1)

            def main(m, par, edge):
                first, last = edge == 0, edge == SEQS - 1
                ahead = edge in (None, 0, 1)
                pool.wait_ge(u_t_ready, DC * (m + 1))
                pool.wait_ge(bc_ready, m + 1)
                for n in range(NS):
                    if begun(UNITS * m + DC * (n - 1)):
                        pool.wait_ge(bx_done, UNITS * m + DC * (n - 1))
                    pass_waits(pool, pool_passed)
                    for j in range(TT):
                        nc.gpsimd.tensor_scalar(v[:, n % 2, j], u_t[:, par, j], bc[:, par, j, n:n + 1], 1.0,
                                                ALU.mult, ALU.mult).then_inc(v_ready, 1)
                    for q in range(DC * n, DC * (n + 1)):
                        if not first:
                            tail(m - 1, 1 - par, q)
                        if not last:
                            prep(m + 1, 1 - par, q)
                        if edge not in (0, 1):
                            residual(m - 2, q)

            nc.gpsimd.memset(ident[:, :], 0.0).then_inc(ident_ready, 1)
            nc.gpsimd.memset(eps[:, :], EPS).then_inc(ident_ready, 1)
            nc.gpsimd.memset(one[:, :], 1.0).then_inc(ident_ready, 1)
            pool.wait_ge(ident_ready, 3)
            nc.gpsimd.affine_select(out=ident[:, :], in_=ident[:, :], compare_op=ALU.not_equal, fill=1.0,
                                    base=0, pattern=[[-1, P]], channel_multiplier=1).then_inc(ident_ready, 1)
            pool.wait_ge(loaded, ALL_LOADED)
            for q in range(PIECES):
                prep(0, 0, q)
            over_tiles(pool, SEQS, main)
            residual(SEQS - 2, 2)
            for q in range(PIECES):
                tail(SEQS - 1, 1, q)
            residual(SEQS - 1, 2)

        @block.scalar
        def _(act):
            def norm(s, q):
                if q == 49:
                    act.wait_ge(mv_done, TT * (s + 1))
                    nc.scalar.activation(lnv[:, :], mv[:, :, 1], ACT.Ln, bias=eps[:, 0:1]).then_inc(lnv_done, 1)
                    act.wait_ge(lnv_done, s + 1)
                    nc.scalar.activation(rstd[:, :], lnv[:, :], ACT.Exp, scale=-0.5).then_inc(rstd_done, 1)

            def prep(s, par, q):
                if q in (2, 3):
                    k = q - 2
                    if begun(DC * s):
                        act.wait_ge(zin_done, DC * s)
                    act.wait_ge(xn_tp, MC * s + k + 1)
                    nc.scalar.activation(xn_t[:, k], side[:, k], ACT.Copy).then_inc(xn_t_ready, 1)
                for c in range(DC):
                    if q == X_IN[c] + 3:
                        if begun(DC * (s - 2) + c + 1):
                            act.wait_ge(y1_done, DC * (s - 2) + c + 1)
                            act.wait_ge(u_ready, DC * (s - 1))
                        if begun(DC * s + c - 1):
                            act.wait_ge(conv_step, (TAPS - 1) * (DC * s + c - 1))
                        act.wait_ge(xin_done, DC * s + c + 1)
                        for k in range(TAPS - 1):
                            nc.scalar.activation(tap[:, c % 2, k], side[:, 0], ACT.Copy, scale=conv_w[:, c, k:k + 1])\
                                .then_inc(tap_step, 1)
                        nc.scalar.activation(xc[:, par, c], side[:, 0], ACT.Identity, bias=conv_b[:, c:c + 1],
                                             scale=conv_w[:, c, TAPS - 1:TAPS]).then_inc(tap_ready, 1)
                    if q == Z_IN[c] + 3:
                        if begun(DC * (s - 2) + c + 1):
                            act.wait_ge(g_done, DC * (s - 2) + c + 1)
                        act.wait_ge(zin_done, DC * s + c + 1)
                        nc.scalar.activation(zs[:, par, c], side[:, 0], ACT.Copy).then_inc(z_raw_ready, 1)
                if q == 42:
                    act.wait_ge(conv_step, (TAPS - 1) * DC * (s + 1))
                    nc.scalar.activation(xc[:, par], xc[:, par], ACT.Silu).then_inc(xc_ready, 1)
                    act.wait_ge(z_raw_ready, DC * (s + 1))
                    nc.scalar.activation(zs[:, par], zs[:, par], ACT.Silu).then_inc(xc_ready, 1)
                    nc.scalar.preload_act_table_set("natural_log_exp_and_others")
                if q == 51:
                    if begun(DC * s):
                        act.wait_ge(dt_done, DC * s)
                    act.wait_ge(dtr_done, s + 1)
                    nc.scalar.activation(dt_raw[:, :], side[0:DTR, 0], ACT.Copy).then_inc(dt_raw_ready, 1)
                if q == 54:
                    if begun(UNITS * (s - 1)):
                        act.wait_ge(y_done, UNITS * (s - 1))
                    if begun(UNITS * (s - 1)):
                        act.wait_ge(v_ready, UNITS * (s - 1))
                    act.wait_ge(bc_done, s + 1)
                    nc.scalar.activation(bc[:, par].rearrange("p j n -> p (j n)"), side[:, 1, 0:TT * 2 * NS], ACT.Copy)\
                        .then_inc(bc_ready, 1)
                if q in (53, 56, 58, 60):
                    c = (53, 56, 58, 60).index(q)
                    if begun(2 * (s - 1)):
                        act.wait_ge(oproj_done, 2 * (s - 1))
                    if begun(DC * (s - 1)):
                        act.wait_ge(g_done, DC * (s - 1))
                    if begun(DC * s):
                        act.wait_ge(u_tp, DC * s)
                    if begun(DC * s):
                        act.wait_ge(u_ready, DC * s)
                    act.wait_ge(dt_done, DC * s + c + 1)
                    nc.scalar.activation(sp_abs[:, c], side[:, c % 2], ACT.Abs, bias=b_dt[:, c:c + 1]).then_inc(abs_ready, 1)
                    nc.scalar.activation(sp_relu[:, c], side[:, c % 2], ACT.Relu, bias=b_dt[:, c:c + 1])\
                        .then_inc(relu_ready, 1)
                    act.wait_ge(abs_ready, DC * s + c + 1)
                    nc.scalar.activation(sp_abs[:, c], sp_abs[:, c], ACT.Exp, scale=-1.0).then_inc(exp_ready, 1)
                    act.wait_ge(exp_ready, DC * s + c + 1)
                    nc.scalar.activation(sp_abs[:, c], sp_abs[:, c], ACT.Ln, bias=one[:, 0:1]).then_inc(ln_ready, 1)

                for c in range(DC):
                    if q == U_FLIP[c] + 1:
                        if begun(UNITS * (s - 1)):
                            act.wait_ge(v_ready, UNITS * (s - 1))
                        act.wait_ge(u_tp, DC * s + c + 1)
                        nc.scalar.activation(u_t[:, par, :, c * P:(c + 1) * P],
                                             side[:, c % 2].rearrange("p (j d) -> p j d", j=TT), ACT.Copy)\
                            .then_inc(u_t_ready, 1)

            def tail(s, par, q):
                if q in (34, 44):
                    k = (q - 34) // 10
                    act.wait_ge(y_done, UNITS * (s + 1))
                    act.wait_ge(x2_stored, 16 * (s + 1))
                    act.wait_ge(oproj_done, 2 * s + k + 1)
                    nc.scalar.activation(o[:, 2 * k:2 * k + 2].rearrange("p j d -> p (j d)"), side[:, 1], ACT.Copy)\
                        .then_inc(o_ready, 1)
                if q == 50:
                    act.wait_ge(mv2_done, TT * (s + 1))
                    nc.scalar.activation(lnv2[:, :], mv2[:, :, 1], ACT.Ln, bias=eps[:, 0:1]).then_inc(lnv2_done, 1)
                    act.wait_ge(lnv2_done, s + 1)
                    nc.scalar.activation(rstd2[:, :], lnv2[:, :], ACT.Exp, scale=-0.5).then_inc(rstd2_done, 1)

            def main(m, par, edge):
                first, last = edge == 0, edge == SEQS - 1
                ahead = edge in (None, 0, 1)
                for n in range(NS):
                    for i in range(DC):
                        if n == 0:
                            act.wait_ge(delta_ready, DC * m + i + 1)
                        if begun(UNITS * m + DC * (n - 2) + i + 1):
                            act.wait_ge(scan_done, UNITS * m + DC * (n - 2) + i + 1)
                        nc.scalar.activation(da[:, n % 2, i], delta[:, par, i], ACT.Exp, scale=a_neg[:, i, n:n + 1])\
                            .then_inc(da_ready, 1)
                        if not first:
                            tail(m - 1, 1 - par, DC * n + i)
                        if not last:
                            prep(m + 1, 1 - par, DC * n + i)
                        if ahead:
                            norm(m + 2, DC * n + i)
                if not last:
                    for q in range(UNITS, PIECES):
                        prep(m + 1, 1 - par, q)

            act.wait_ge(loaded, ALL_LOADED)
            act.wait_ge(ident_ready, 3)
            nc.scalar.preload_act_table_set("natural_log_exp_and_others")
            nc.scalar.activation(a_neg[:, :, :], a_neg[:, :, :], ACT.Exp).then_inc(a_exp, 1)
            for q in range(PIECES):
                norm(0, q)
            for q in range(PIECES):
                prep(0, 0, q)
            for q in range(PIECES):
                norm(1, q)
            act.wait_ge(setup, SETUP)
            over_tiles(act, SEQS, main)
            for q in range(PIECES):
                tail(SEQS - 1, 1, q)

        @block.vector
        def _(dve):
            def norm(s, q):
                if q in (43, 44, 45, 46):
                    dve.wait_ge(xs_loaded, 16 * (s + 1))
                    if begun(TT * s):
                        dve.wait_ge(mv_done, TT * s)
                    nc.vector.bn_stats(stats[:, q - 43], xs[:, q - 43]).then_inc(st_done, 1)
                if q in (44, 45, 46, 47):
                    j = q - 44
                    if begun(TT * s):
                        dve.wait_ge(xn_done, TT * s)
                    dve.wait_ge(st_done, TT * s + j + 1)
                    pass_waits(dve, dve_passed)
                    nc.vector.bn_aggr(mv[:, j], stats[:, j]).then_inc(mv_done, 1)
                if q in (51, 52, 53, 54):
                    j = q - 51
                    dve.wait_ge(rstd_done, s + 1)
                    if begun(MC * s):
                        dve.wait_ge(xn_tp, MC * s)
                    nc.vector.tensor_scalar(xn[:, j], xs[:, j], mv[:, j, 0:1], rstd[:, j:j + 1],
                                            ALU.subtract, ALU.mult).then_inc(xn_done, 1)

            def prep(s, par, q):
                if q in DELTA:
                    c = DELTA.index(q)
                    if begun(UNITS * (s - 1)):
                        dve.wait_ge(da_ready, UNITS * (s - 1))
                    dve.wait_ge(ln_ready, DC * s + c + 1)
                    nc.vector.tensor_tensor(delta[:, par, c], sp_relu[:, c], sp_abs[:, c], ALU.add).then_inc(delta_ready, 1)
                    dve.wait_ge(delta_ready, DC * s + c + 1)
                    nc.vector.tensor_tensor(u[:, c], delta[:, par, c], xc[:, par, c], ALU.mult).then_inc(u_ready, 1)

            def tail(s, par, q):
                for c in range(DC):
                    if q == ACC_FLIP[c] + 1:
                        dve.wait_ge(u_ready, DC * up_to(s + 2))
                        dve.wait_ge(acc_tp, DC * s + c + 1)
                        nc.vector.scalar_tensor_tensor(y1[:, c], xc[:, par, c], d_skip[:, c:c + 1], side[:, c % 2],
                                                       ALU.mult, ALU.add).then_inc(y1_done, 1)
                if q in (36, 37, 46, 47):
                    j = (36, 37, 46, 47).index(q)
                    dve.wait_ge(o_ready, 2 * s + j // 2 + 1)
                    dve.wait_ge(y_done, UNITS * (s + 1))
                    nc.vector.bn_stats(stats2[:, j], o[:, j]).then_inc(st2_done, 1)
                if q in (37, 38, 47, 48):
                    j = (37, 38, 47, 48).index(q)
                    dve.wait_ge(st2_done, TT * s + j + 1)
                    pass_waits(dve, dve_passed)
                    nc.vector.bn_aggr(mv2[:, j], stats2[:, j]).then_inc(mv2_done, 1)
                if q in (55, 57, 59, 61):
                    j = (q - 55) // 2
                    dve.wait_ge(rstd2_done, s + 1)
                    nc.vector.tensor_scalar(o[:, j], o[:, j], mv2[:, j, 0:1], rstd2[:, j:j + 1],
                                            ALU.subtract, ALU.mult).then_inc(yn_done, 1)

            def add(m, par, n, i):
                at = UNITS * m + DC * n + i
                scale = bc[:, par, i, NS + n:NS + n + 1]
                dve.wait_ge(ht_done, at + 1)
                if n == 0:
                    nc.vector.tensor_scalar(y_acc[:, par, i], ht_ps[i % 2][:, :], scale, None, ALU.mult).then_inc(y_done, 1)
                else:
                    dve.wait_ge(y_done, at - DC + 1)
                    nc.vector.scalar_tensor_tensor(y_acc[:, par, i], ht_ps[i % 2][:, :], scale, y_acc[:, par, i],
                                                   ALU.mult, ALU.add).then_inc(y_done, 1)

            def main(m, par, edge):
                first, last = edge == 0, edge == SEQS - 1
                ahead = edge in (None, 0, 1)
                for n in range(NS):
                    for i in range(DC):
                        at = UNITS * m + DC * n + i
                        if begun(UNITS * m + DC * (n - 1)):
                            dve.wait_ge(ht_done, UNITS * m + DC * (n - 1))
                        dve.wait_ge(da_ready, at + 1)
                        dve.wait_ge(bx_done, at + 1)
                        nc.vector.tensor_tensor_scan(h[:, n % 2, i], da[:, n % 2, i], bx_ps[i][:, :], 0.0,
                                                     ALU.mult, ALU.add).then_inc(scan_done, 1)
                        if n > 0:
                            add(m, par, n - 1, i)
                        elif not first:
                            add(m - 1, 1 - par, NS - 1, i)
                        if not first:
                            tail(m - 1, 1 - par, DC * n + i)
                        if not last:
                            prep(m + 1, 1 - par, DC * n + i)
                        if ahead:
                            norm(m + 2, DC * n + i)

            dve.wait_ge(loaded, ALL_LOADED)
            dve.wait_ge(a_exp, 1)
            nc.vector.tensor_scalar(a_neg[:, :, :], a_neg[:, :, :], -1.0, None, ALU.mult).then_inc(setup, 1)
            for q in range(PIECES):
                norm(0, q)
            for q in range(PIECES):
                prep(0, 0, q)
            for q in range(PIECES):
                norm(1, q)
            dve.wait_ge(bc_ready, 1)
            over_tiles(dve, SEQS, main)
            for i in range(DC):
                add(SEQS - 1, 1, NS - 1, i)
            for q in range(PIECES):
                tail(SEQS - 1, 1, q)

        @block.tensor
        def _(pe):
            def mm(out, lhs, rhs, start, stop):
                return nc.tensor.matmul(out, lhs, rhs, start=start, stop=stop)

            def flip(out, blocks):
                for i, b in enumerate(blocks):
                    last = nc.tensor.transpose(out[:, i * P:(i + 1) * P], b, ident[:, :])
                return last

            def prep(s, par, q):
                if q in XN_FLIP:
                    k = XN_FLIP.index(q)
                    pe.wait_ge(xn_done, TT * (s + 1))
                    if begun(DC * s):
                        pe.wait_ge(u_t_ready, DC * s)
                    flip(side[:, k], [xn[:, j, k * P:(k + 1) * P] for j in range(TT)]).then_inc(xn_tp, 1)
                for c in range(DC):
                    e = q - X_IN[c]
                    if e == 0:
                        pe.wait_ge(xn_t_ready, MC * (s + 1))
                        if begun(DC * (s - 1)):
                            pe.wait_ge(y1_done, DC * (s - 1))
                        if begun(DC * s + c):
                            pe.wait_ge(tap_ready, DC * s + c)
                        if c > 1:
                            pe.wait_ge(z_raw_ready, DC * s + 1)
                    if e in range(MC):
                        last = mm(side[:, 0], w_in[:, e, c * P:(c + 1) * P], xn_t[:, e], e == 0, e == MC - 1)
                        if e == MC - 1:
                            last.then_inc(xin_done, 1)
                    e = q - Z_IN[c]
                    if e == 0:
                        pe.wait_ge(tap_ready, DC * s + (2 if c == 0 else DC))
                        if begun(DC * s + c):
                            pe.wait_ge(z_raw_ready, DC * s + c)
                    if e in range(MC):
                        last = mm(side[:, 0], w_in[:, e, DI + c * P:DI + (c + 1) * P], xn_t[:, e], e == 0, e == MC - 1)
                        if e == MC - 1:
                            last.then_inc(zin_done, 1)
                if q in DT_IN:
                    c = DT_IN.index(q)
                    pe.wait_ge(xc_ready, 2 * s + 1)
                    pe.wait_ge(z_raw_ready, DC * (s + 1))
                    last = mm(side[0:DTR, 0], w_x[:, c, 0:DTR], xc[:, par, c], c == 0, c == DC - 1)
                    if c == DC - 1:
                        last.then_inc(dtr_done, 1)
                if q in BC_IN:
                    j = BC_IN.index(q)
                    if begun(2 * (s - 1)):
                        pe.wait_ge(o_ready, 2 * (s - 1))
                    for c in range(DC):
                        last = mm(side[:, 1, j * 2 * NS:(j + 1) * 2 * NS], xc[:, par, c, j * P:(j + 1) * P],
                                  w_x[:, c, DTR:DTR + 2 * NS], c == 0, c == DC - 1)
                    if j == TT - 1:
                        last.then_inc(bc_done, 1)
                if q in DT:
                    c = DT.index(q)
                    pe.wait_ge(dt_raw_ready, s + 1)
                    if c % 2:
                        pe.wait_ge(bc_ready, s + 1)
                    if begun(DC * s + c - 1):
                        pe.wait_ge(relu_ready, DC * s + c - 1)
                    mm(side[:, c % 2], w_dt[:, c * P:(c + 1) * P], dt_raw[:, :], True, True).then_inc(dt_done, 1)
                if q in U_FLIP:
                    c = U_FLIP.index(q)
                    pe.wait_ge(u_ready, DC * s + c + 1)
                    if c < 2:
                        pe.wait_ge(relu_ready, DC * s + c + 3)
                    else:
                        pe.wait_ge(u_t_ready, DC * s + c - 1)
                    flip(side[:, c % 2], [u[:, c, j * P:(j + 1) * P] for j in range(TT)]).then_inc(u_tp, 1)

            def tail(s, par, q):
                if q in ACC_FLIP:
                    c = ACC_FLIP.index(q)
                    pe.wait_ge(y_done, UNITS * (s + 1))
                    if c < 2:
                        pe.wait_ge(u_t_ready, DC * up_to(s + 2))
                        pe.wait_ge(xn_t_ready, MC * up_to(s + 3))
                    else:
                        pe.wait_ge(y1_done, DC * s + c - 1)
                    flip(side[:, c % 2], [y_acc[:, par, j, c * P:(c + 1) * P] for j in range(TT)]).then_inc(acc_tp, 1)
                if q in OUT:
                    j, half = divmod(OUT.index(q), 2)
                    pe.wait_ge(g_done, DC * (s + 1))
                    pe.wait_ge(y1_done, DC * (s + 1))
                    if j >= 2:
                        pe.wait_ge(o_ready, 2 * s + 1)
                    for c in (2 * half, 2 * half + 1):
                        last = mm(side[:, 1, (j % 2) * DM:(j % 2 + 1) * DM], g[:, c, j * P:(j + 1) * P],
                                  w_out[:, c], c == 0, c == DC - 1)
                    if j % 2 and half:
                        last.then_inc(oproj_done, 1)

            def flip_h(m, n, i):
                at = UNITS * m + DC * n + i
                pe.wait_ge(scan_done, UNITS * m + DC * (n + 1))
                if begun(at - 1):
                    pe.wait_ge(y_done, at - 1)
                flip(ht_ps[i % 2], [h[:, n % 2, c, i * P:(i + 1) * P] for c in range(DC)]).then_inc(ht_done, 1)

            def main(m, par, edge):
                first, last = edge == 0, edge == SEQS - 1
                ahead = edge in (None, 0, 1)
                for n in range(NS):
                    for i in range(DC):
                        at = UNITS * m + DC * n + i
                        pe.wait_ge(v_ready, UNITS * m + TT * (n + 1))
                        if begun(at - DC + 1):
                            pe.wait_ge(scan_done, at - DC + 1)
                        flip(bx_ps[i], [v[:, n % 2, j, i * P:(i + 1) * P] for j in range(TT)]).then_inc(bx_done, 1)
                        if n > 0:
                            flip_h(m, n - 1, i)
                        elif not first:
                            flip_h(m - 1, NS - 1, i)
                        if not first:
                            tail(m - 1, 1 - par, DC * n + i)
                        if not last:
                            prep(m + 1, 1 - par, DC * n + i)
                if not last:
                    for q in range(UNITS, PIECES):
                        prep(m + 1, 1 - par, q)

            pe.wait_ge(loaded, ALL_LOADED)
            pe.wait_ge(ident_ready, 4)
            for q in range(PIECES):
                prep(0, 0, q)
            over_tiles(pe, SEQS, main)
            for i in range(DC):
                flip_h(SEQS - 1, NS - 1, i)
            for q in range(PIECES):
                tail(SEQS - 1, 1, q)



def split_weights(nc, ctx, w):
    def sb(name, shape, dtype):
        return ctx.enter_context(nc.sbuf_tensor("f_" + name, shape, dtype))

    names = ("w_h", "w_gate", "w_up", "b_gate", "b_up", "w_down", "a2")
    shapes = ([MC, 2 * ER], [MC, FF], [MC, FF], [FF], [FF], [FC, DM], [FC, ER])
    sizes = [int(math.prod(s)) for s in shapes]
    split = {n: sb(n, [P, 2, size], F32R) for n, size in zip(names, sizes)}
    weights = {"b_down": sb("b_down", [P, DM], F32), "w_router": sb("w_router", [P, MC, E], F32),
               "expand": sb("expand", [4 * E, 4, P], F32R), "half": sb("half", [4 * E, 2, P], F32R),
               "rank": sb("rank", [P, TT, E], F32)}
    with ExitStack() as setup:
        raw = [setup.enter_context(nc.sbuf_tensor("raw_" + n, [P, size], F32)) for n, size in zip(names, sizes)]
        expand = setup.enter_context(nc.sbuf_tensor("expand_raw", [4 * E, 4, P], F32))
        half = setup.enter_context(nc.sbuf_tensor("half_raw", [4 * E, 2, P], F32))
        raw_loaded = [setup.enter_context(nc.semaphore("loaded_" + n)) for n in names]
        small_loaded = setup.enter_context(nc.semaphore("small_loaded"))
        high_ready = setup.enter_context(nc.semaphore("high_ready"))
        low_ready = setup.enter_context(nc.semaphore("low_ready"))
        const_step = setup.enter_context(nc.semaphore("const_step"))
        rank_ready = setup.enter_context(nc.semaphore("rank_ready"))
        block = setup.enter_context(nc.Block())

        @block.sync
        def _(sp):
            for i, n in enumerate(names):
                flat = w[n].rearrange("p k d -> p (k d)") if len(shapes[i]) == 2 else w[n]
                sp.dma_start(raw[i][:, :], flat).then_inc(raw_loaded[i], 16)
            sp.dma_start(weights["b_down"][:, :], w["b_down"]).then_inc(small_loaded, 16)
            sp.dma_start(weights["w_router"][:, :, :], w["w_router"]).then_inc(small_loaded, 16)
            sp.wait_ge(small_loaded, 32)

        @block.scalar
        def _(act):
            for i, n in enumerate(names):
                act.wait_ge(raw_loaded[i], 16)
                nc.scalar.activation(split[n][:, 0], raw[i][:, :], ACT.Copy).then_inc(high_ready, 1)
            act.wait_ge(const_step, 5)
            nc.scalar.activation(weights["expand"][:, :, :], expand[:, :, :], ACT.Copy).then_inc(high_ready, 1)
            nc.scalar.activation(weights["half"][:, :, :], half[:, :, :], ACT.Copy).then_inc(high_ready, 1)
            act.wait_ge(high_ready, len(names) + 2)

        @block.vector
        def _(dve):
            for i, n in enumerate(names):
                dve.wait_ge(raw_loaded[i], 16)
                dve.wait_ge(high_ready, i + 1)
                nc.vector.tensor_tensor(split[n][:, 1], raw[i][:, :], split[n][:, 0].bitcast(F32), ALU.subtract)\
                    .then_inc(low_ready, 1)
            dve.wait_ge(low_ready, len(names))

        @block.gpsimd
        def _(pool):
            nc.gpsimd.memset(expand[:, :, :], 0.0).then_inc(const_step, 1)
            pool.wait_ge(const_step, 1)
            nc.gpsimd.affine_select(out=expand.rearrange("p q (e r) -> p q e r", e=E), in_=expand.rearrange("p q (e r) -> p q e r", e=E),
                                    compare_op=ALU.not_equal, fill=1.0, base=0,
                                    pattern=[[-E, 4], [-1, E], [0, R]], channel_multiplier=1).then_inc(const_step, 1)
            nc.gpsimd.memset(half[:, :, :], 1.0 / LORA_SCALE).then_inc(const_step, 1)
            pool.wait_ge(const_step, 3)
            nc.gpsimd.affine_select(out=half[:, :, :], in_=half[:, :, :], compare_op=ALU.is_ge, fill=0.0, base=-2 * E,
                                    pattern=[[-E, 2], [0, P]], channel_multiplier=1).then_inc(const_step, 1)
            pool.wait_ge(const_step, 4)
            nc.gpsimd.affine_select(out=half[:, :, :], in_=half[:, :, :], compare_op=ALU.is_ge, fill=0.0, base=3 * E - 1,
                                    pattern=[[E, 2], [0, P]], channel_multiplier=-1).then_inc(const_step, 1)
            for e in range(E):
                nc.gpsimd.memset(weights["rank"][:, :, e:e + 1], float(E - e)).then_inc(rank_ready, 1)
            pool.wait_ge(rank_ready, E)
            pool.wait_ge(const_step, 5)

    for n, shape in zip(names, shapes):
        t = split[n]
        weights[n] = t.rearrange("p a (k d) -> p a k d", k=shape[0]) if len(shape) == 2 else t[:, :, :]
    return weights


def ffn_phase(nc, x2_dram, w, out, consts):
    ident, eps, _ = consts
    with ExitStack() as ctx:
        weights = split_weights(nc, ctx, w)
        w_h, w_gate, w_up, b_gate, b_up = (weights[n] for n in ("w_h", "w_gate", "w_up", "b_gate", "b_up"))
        w_down, a2, b_down, w_router = (weights[n] for n in ("w_down", "a2", "b_down", "w_router"))
        expand, half, rank = (weights[n] for n in ("expand", "half", "rank"))

        def sb(name, shape, dtype=F32):
            return ctx.enter_context(nc.sbuf_tensor("f_" + name, shape, dtype))

        def sem(name):
            return ctx.enter_context(nc.semaphore("f_" + name))

        GROUPS = SEQS
        xg = sb("xg", [P, TT, DM])
        xg_stats = sb("xg_stats", [P, TT, 6])
        xg_mv = sb("xg_mv", [P, TT, 2])
        xg_lnv = sb("xg_lnv", [P, TT])
        xg_rstd = sb("xg_rstd", [P, TT])
        x_t = sb("x_t", [P, 2, 2, MC, T], F32R)
        x_f = sb("x_f", [P, MC, T])
        hx = sb("hx", [P, 2, 2, T], F32R)
        hm = sb("hm", [P, 2, 2, 2, 2, T], F32R)
        row_max = sb("row_max", [P, TT])
        shifted = sb("shifted", [P, TT, E])
        expd = sb("expd", [P, TT, E])
        row_sum = sb("row_sum", [P, TT])
        row_inv = sb("row_inv", [P, TT])
        probs = sb("probs", [P, 2, TT, E])
        top = sb("top", [P, 2, TT])
        equal = sb("equal", [P, 2, TT, E])
        key = sb("key", [P, 2, TT, E])
        key_max = sb("key_max", [P, 2, TT])
        chosen = sb("chosen", [P, 2, TT, E])
        top_sum = sb("top_sum", [P, TT])
        top_inv = sb("top_inv", [P, TT])
        rw = sb("rw", [P, 2, TT])
        diff = sb("diff", [P, TT, E])
        select = sb("select", [P, TT, 4, E])
        select_t = sb("select_t", [4 * E, 2, T], F32R)
        rw_all = sb("rw_all", [P, 2, 2, T])
        z_mask = sb("z_mask", [P, 2, T])
        silu = sb("silu", [P, 2, T])
        a = sb("a", [P, 2, T])
        a_parts = sb("a_parts", [P, 2, 2, T], F32R)
        aw = sb("aw", [P, 2, T])
        aw_parts = sb("aw_parts", [P, 2, T], F32R)
        zm = sb("zm", [P, 2, T])
        o = sb("o", [P, TT, DM])
        stats = sb("stats", [P, TT, 6])
        mv = sb("mv", [P, TT, 2])
        lnv = sb("lnv", [P, TT])
        rstd = sb("rstd", [P, TT])
        xr = sb("xr", [P, TT, DM])

        gu_ps = ctx.enter_context(nc.psum_tensor("gu_ps", [P, 2, 512], F32))
        z_ps = ctx.enter_context(nc.psum_tensor("z_ps", [P, 2, 512], F32))
        o_ps = ctx.enter_context(nc.psum_tensor("o_ps", [P, 2, 512], F32))
        side = ctx.enter_context(nc.psum_tensor("f_side", [P, 2, 512], F32))

        dve_passed = sem("dve_passed")
        xg_loaded = sem("xg_loaded")
        xg_st_done = sem("xg_st_done")
        xg_mv_done = sem("xg_mv_done")
        xg_lnv_done = sem("xg_lnv_done")
        xg_rstd_done = sem("xg_rstd_done")
        xn_done = sem("xn_done")
        xn_tp = sem("xn_tp")
        xh_ready = sem("xh_ready")
        xl_ready = sem("xl_ready")
        logits_done = sem("logits_done")
        rt = sem("rt")
        exp_done = sem("exp_done")
        hx_done = sem("hx_done")
        hxh_ready = sem("hxh_ready")
        hxl_ready = sem("hxl_ready")
        select_tp = sem("select_tp")
        select_h = sem("select_h")
        select_l = sem("select_l")
        pick_done = sem("pick_done")
        hm_ready = sem("hm_ready")
        rw_done = sem("rw_done")
        rw_ready = sem("rw_ready")
        mask_done = sem("mask_done")
        mask_ready = sem("mask_ready")
        base_done = sem("base_done")
        diff_done = sem("diff_done")
        silu_ready = sem("silu_ready")
        a_ready = sem("a_ready")
        ah_ready = sem("ah_ready")
        al_ready = sem("al_ready")
        aw_step = sem("aw_step")
        awh_ready = sem("awh_ready")
        awl_ready = sem("awl_ready")
        z_done = sem("z_done")
        down_done = sem("down_done")
        zm_step = sem("zm_step")
        o_done = sem("o_done")
        o_ready = sem("o_ready")
        st_done = sem("st_done")
        mv_done = sem("mv_done")
        lnv_done = sem("lnv_done")
        rstd_done = sem("rstd_done")
        yn_done = sem("yn_done")
        xr_loaded = sem("xr_loaded")
        y_ready = sem("y_ready")
        y_stored = sem("y_stored")

        x_v = x2_dram.rearrange("s (j p) d -> s p j d", p=P)
        out_v = out.rearrange("s (j p) d -> s p j d", p=P)
        RT = 25
        PAIRS = ((0, 0), (0, 1), (1, 0))

        def over_groups(main):
            def run(eng):
                main(0, 0, 0)
                main(1, 1, 1)
                with eng.Fori(2, GROUPS - 3, 2) as m:
                    main(m, 0, None)
                    main(m + 1, 1, None)
                main(GROUPS - 2, 0, GROUPS - 2)
                main(GROUPS - 1, 1, GROUPS - 1)
                main(GROUPS, 0, GROUPS)
            return run

        def on(edge):
            return edge != GROUPS, edge != 0, edge not in (GROUPS - 1, GROUPS), edge in (None, 0, 1)

        block = ctx.enter_context(nc.Block())

        @block.sync
        def _(sp):
            sp.dma_start(xg[:, :, :], x_v[0]).then_inc(xg_loaded, 16)
            sp.wait_ge(xn_tp, MC)
            sp.dma_start(xg[:, :, :], x_v[1]).then_inc(xg_loaded, 16)

            def main(m, par, edge):
                act_on, tail_on, prep_on, norm_on = on(edge)
                if norm_on:
                    sp.wait_ge(xn_tp, MC * (m + 2))
                    sp.dma_start(xg[:, :, :], row(x_v, m + 2)).then_inc(xg_loaded, 16)
                if tail_on:
                    if edge != 1:
                        sp.wait_ge(y_ready, m - 1)
                    sp.dma_start(xr[:, :, :], row(x_v, m - 1)).then_inc(xr_loaded, 16)
                    sp.wait_ge(y_ready, m)
                    sp.dma_start(row(out_v, m - 1), o[:, :, :]).then_inc(y_stored, 16)

            over_groups(main)(sp)
            sp.wait_ge(y_stored, 16 * GROUPS)

        @block.gpsimd
        def _(pool):
            def main(m, par, edge):
                act_on, tail_on, _, _ = on(edge)
                for f in range(FC):
                    if act_on:
                        at = FC * m + f
                        if f == 0:
                            pool.wait_ge(rw_ready, 2 * (m + 1))
                        for k in range(2):
                            pool.wait_ge(a_ready, 2 * at + k + 1)
                            if k == 0 and begun(at):
                                pool.wait_ge(awl_ready, at)
                            nc.gpsimd.tensor_tensor(aw[:, k], a[:, k], rw_all[:, par, k], ALU.mult).then_inc(aw_step, 1)
                        pool.wait_ge(aw_step, 3 * at + 2)
                        nc.gpsimd.tensor_tensor(aw[:, 0], aw[:, 0], aw[:, 1], ALU.add).then_inc(aw_step, 1)
                    if tail_on and f == 5:
                        pool.wait_ge(yn_done, TT * m)
                        pool.wait_ge(xr_loaded, 16 * m)
                        nc.gpsimd.tensor_tensor(o[:, :, :], o[:, :, :], xr[:, :, :], ALU.add).then_inc(y_ready, 1)

            over_groups(main)(pool)

        @block.scalar
        def _(act):
            def norm(s, f):
                if f == 3:
                    act.wait_ge(xg_mv_done, TT * (s + 1))
                    nc.scalar.activation(xg_lnv[:, :], xg_mv[:, :, 1], ACT.Ln, bias=eps[:, 0:1]).then_inc(xg_lnv_done, 1)
                    act.wait_ge(xg_lnv_done, s + 1)
                    nc.scalar.activation(xg_rstd[:, :], xg_lnv[:, :], ACT.Exp, scale=-0.5).then_inc(xg_rstd_done, 1)

            def prep(s, par, f):
                if f == 0:
                    if begun(FC * (s - 1)):
                        act.wait_ge(base_done, FC * (s - 1))
                    if begun(s):
                        act.wait_ge(logits_done, s)
                    for k in range(MC):
                        act.wait_ge(xn_tp, MC * s + k + 1)
                        nc.scalar.activation(x_t[:, par, 0, k], side[:, k], ACT.Copy).then_inc(xh_ready, 1)
                        nc.scalar.activation(x_f[:, k], side[:, k], ACT.Copy).then_inc(xh_ready, 1)
                if f in (2, 3):
                    t = f - 2
                    if begun(8 * s):
                        act.wait_ge(hm_ready, 8 * s)
                    act.wait_ge(hx_done, 2 * s + t + 1)
                    nc.scalar.activation(hx[:, 0, t], side[:, 0], ACT.Copy).then_inc(hxh_ready, 1)
                if f == 3:
                    act.wait_ge(rt, RT * s + 2)
                    nc.scalar.activation(expd[:, :, :], shifted[:, :, :], ACT.Exp).then_inc(exp_done, 1)
                if f == 5:
                    if begun(2 * s):
                        act.wait_ge(mask_done, 2 * s)
                    act.wait_ge(select_tp, s + 1)
                    nc.scalar.activation(select_t[:, 0], side[0:4 * E, 0], ACT.Copy).then_inc(select_h, 1)
                if f == 7:
                    if begun(3 * FC * (s - 1)):
                        act.wait_ge(aw_step, 3 * FC * (s - 1))
                    for k in range(2):
                        act.wait_ge(rw_done, 2 * s + k + 1)
                        nc.scalar.activation(rw_all[:, par, k], side[:, k], ACT.Copy).then_inc(rw_ready, 1)

            def high_of_sum(at):
                act.wait_ge(aw_step, 3 * (at + 1))
                if begun(at):
                    act.wait_ge(down_done, at)
                nc.scalar.activation(aw_parts[:, 0], aw[:, 0], ACT.Copy).then_inc(awh_ready, 1)

            def main(m, par, edge):
                act_on, tail_on, prep_on, norm_on = on(edge)
                for f in range(FC):
                    at = FC * m + f
                    if f > 0 and act_on or f == 0 and tail_on:
                        high_of_sum(at - 1)
                    for k in range(2):
                        if act_on:
                            act.wait_ge((base_done, diff_done)[k], at + 1)
                            if begun(2 * at + k - 1):
                                act.wait_ge(a_ready, 2 * at + k - 1)
                            nc.scalar.activation(silu[:, k], gu_ps[:, 0], ACT.Silu).then_inc(silu_ready, 1)
                            act.wait_ge(a_ready, 2 * at + k + 1)
                            if begun(at):
                                act.wait_ge(z_done, at)
                            nc.scalar.activation(a_parts[:, k, 0], a[:, k], ACT.Copy).then_inc(ah_ready, 1)
                        if tail_on and f == 1 and k == 0:
                            if edge != 1:
                                act.wait_ge(y_stored, 16 * (m - 1))
                            for i in range(2):
                                act.wait_ge(o_done, 2 * (m - 1) + i + 1)
                                nc.scalar.activation(o[:, 2 * i:2 * i + 2].rearrange("p j d -> p (j d)"), o_ps[:, i],
                                                     ACT.Copy).then_inc(o_ready, 1)
                    if act_on and f in (1, 2):
                        k = f - 1
                        if begun(3 * m):
                            act.wait_ge(zm_step, 3 * m)
                        act.wait_ge(mask_done, 2 * m + k + 1)
                        nc.scalar.activation(z_mask[:, k], side[:, 1], ACT.Copy).then_inc(mask_ready, 1)
                    if f == 3 and (tail_on or prep_on or norm_on):
                        nc.scalar.preload_act_table_set("natural_log_exp_and_others")
                    if tail_on and f == 3:
                        act.wait_ge(mv_done, TT * m)
                        nc.scalar.activation(lnv[:, :], mv[:, :, 1], ACT.Ln, bias=eps[:, 0:1]).then_inc(lnv_done, 1)
                        act.wait_ge(lnv_done, m)
                        nc.scalar.activation(rstd[:, :], lnv[:, :], ACT.Exp, scale=-0.5).then_inc(rstd_done, 1)
                    if prep_on:
                        prep(m + 1, 1 - par, f)
                    if norm_on:
                        norm(m + 2, f)

            nc.scalar.preload_act_table_set("natural_log_exp_and_others")
            for f in range(FC):
                norm(0, f)
            for f in range(FC):
                prep(0, 0, f)
            for f in range(FC):
                norm(1, f)
            over_groups(main)(act)

        @block.vector
        def _(dve):
            def last_axis(ap):
                return ap.unsqueeze(2).broadcast_to([P, TT, E])

            def prep(s, par, f):
                logits = side[:, 0, 0:TT * E].rearrange("p (j e) -> p j e", e=E)
                if f == 1:
                    dve.wait_ge(logits_done, s + 1)
                    if begun(RT * s):
                        dve.wait_ge(rt, RT * s)
                    nc.vector.tensor_reduce(row_max[:, :], logits, AX.X, ALU.max).then_inc(rt, 1)
                    dve.wait_ge(rt, RT * s + 1)
                    nc.vector.tensor_tensor(shifted[:, :, :], logits, last_axis(row_max[:, :]), ALU.subtract).then_inc(rt, 1)
                if f == 4:
                    dve.wait_ge(exp_done, s + 1)
                    if begun(s):
                        dve.wait_ge(select_tp, s)
                    dve.wait_ge(rt, RT * s + 2)
                    nc.vector.tensor_reduce(row_sum[:, :], expd[:, :, :], AX.X, ALU.add).then_inc(rt, 1)
                    dve.wait_ge(rt, RT * s + 3)
                    nc.vector.reciprocal(row_inv[:, :], row_sum[:, :]).then_inc(rt, 1)
                    dve.wait_ge(rt, RT * s + 4)
                    nc.vector.tensor_tensor(probs[:, 0], expd[:, :, :], last_axis(row_inv[:, :]), ALU.mult).then_inc(rt, 1)
                    for k in range(2):
                        at = RT * s + 5 + 6 * k
                        dve.wait_ge(rt, at)
                        nc.vector.tensor_reduce(top[:, k], probs[:, k], AX.X, ALU.max).then_inc(rt, 1)
                        dve.wait_ge(rt, at + 1)
                        nc.vector.tensor_tensor(equal[:, k], probs[:, k], last_axis(top[:, k]), ALU.is_equal).then_inc(rt, 1)
                        dve.wait_ge(rt, at + 2)
                        nc.vector.tensor_tensor(key[:, k], equal[:, k], rank[:, :, :], ALU.mult).then_inc(rt, 1)
                        dve.wait_ge(rt, at + 3)
                        nc.vector.tensor_reduce(key_max[:, k], key[:, k], AX.X, ALU.max).then_inc(rt, 1)
                        dve.wait_ge(rt, at + 4)
                        nc.vector.tensor_tensor(chosen[:, k], key[:, k], last_axis(key_max[:, k]), ALU.is_equal).then_inc(rt, 1)
                        if k == 0:
                            dve.wait_ge(rt, at + 5)
                            nc.vector.scalar_tensor_tensor(probs[:, 1], chosen[:, 0], -2.0, probs[:, 0],
                                                           ALU.mult, ALU.add).then_inc(rt, 1)
                    dve.wait_ge(rt, RT * s + 16)
                    nc.vector.tensor_tensor(top_sum[:, :], top[:, 0], top[:, 1], ALU.add).then_inc(rt, 1)
                    dve.wait_ge(rt, RT * s + 17)
                    nc.vector.reciprocal(top_inv[:, :], top_sum[:, :]).then_inc(rt, 1)
                    dve.wait_ge(rt, RT * s + 18)
                    nc.vector.tensor_tensor(rw[:, 0], top[:, 0], top_inv[:, :], ALU.mult).then_inc(rt, 1)
                    dve.wait_ge(rt, RT * s + 19)
                    nc.vector.tensor_tensor(rw[:, 1], top[:, 1], top_inv[:, :], ALU.mult).then_inc(rt, 1)
                    dve.wait_ge(rt, RT * s + 20)
                    nc.vector.tensor_scalar(select[:, :, 0], chosen[:, 0], LORA_SCALE, None, ALU.mult).then_inc(rt, 1)
                    dve.wait_ge(rt, RT * s + 21)
                    nc.vector.tensor_tensor(diff[:, :, :], chosen[:, 1], chosen[:, 0], ALU.subtract).then_inc(rt, 1)
                    dve.wait_ge(rt, RT * s + 22)
                    nc.vector.tensor_scalar(select[:, :, 1], diff[:, :, :], LORA_SCALE, None, ALU.mult).then_inc(rt, 1)
                    for k in range(2):
                        dve.wait_ge(rt, RT * s + 23 + k)
                        nc.vector.scalar_tensor_tensor(select[:, :, 2 + k], chosen[:, k], LORA_SCALE, last_axis(rw[:, k]),
                                                       ALU.mult, ALU.mult).then_inc(rt, 1)
                if f == 0:
                    if begun(FC * (s - 1)):
                        dve.wait_ge(base_done, FC * (s - 1))
                    for k in range(MC):
                        dve.wait_ge(xh_ready, 2 * (MC * s + k) + 2)
                        nc.vector.tensor_tensor(x_t[:, par, 1, k], x_f[:, k], x_t[:, par, 0, k].bitcast(F32),
                                                ALU.subtract).then_inc(xl_ready, 1)
                if f in (2, 3):
                    t = f - 2
                    if begun(8 * s):
                        dve.wait_ge(hm_ready, 8 * s)
                    dve.wait_ge(hxh_ready, 2 * s + t + 1)
                    nc.vector.tensor_tensor(hx[:, 1, t], side[:, 0], hx[:, 0, t].bitcast(F32), ALU.subtract)\
                        .then_inc(hxl_ready, 1)
                if f == 5:
                    if begun(2 * s):
                        dve.wait_ge(mask_done, 2 * s)
                    dve.wait_ge(select_h, s + 1)
                    nc.vector.tensor_tensor(select_t[:, 1], side[0:4 * E, 0], select_t[:, 0].bitcast(F32), ALU.subtract)\
                        .then_inc(select_l, 1)
                if f == 6:
                    if begun(FC * (s - 1)):
                        dve.wait_ge(diff_done, FC * (s - 1))
                    for k in range(2):
                        dve.wait_ge(pick_done, 2 * s + k + 1)
                        for i in range(4):
                            part, t = divmod(i, 2)
                            dve.wait_ge(hxl_ready, 2 * s + t + 1)
                            nc.vector.tensor_tensor(hm[:, par, part, k, t], side[:, k], hx[:, part, t].bitcast(F32),
                                                    ALU.mult).then_inc(hm_ready, 1)

            def norm(s, f):
                if f == 2:
                    dve.wait_ge(xg_loaded, 16 * (s + 1))
                    for j in range(TT):
                        nc.vector.bn_stats(xg_stats[:, j], xg[:, j]).then_inc(xg_st_done, 1)
                    dve.wait_ge(xg_st_done, TT * (s + 1))
                    pass_waits(dve, dve_passed)
                    for j in range(TT):
                        nc.vector.bn_aggr(xg_mv[:, j], xg_stats[:, j]).then_inc(xg_mv_done, 1)
                if f == 4:
                    dve.wait_ge(xg_rstd_done, s + 1)
                    for j in range(TT):
                        nc.vector.tensor_scalar(xg[:, j], xg[:, j], xg_mv[:, j, 0:1], xg_rstd[:, j:j + 1],
                                                ALU.subtract, ALU.mult).then_inc(xn_done, 1)

            def low_of_sum(at):
                dve.wait_ge(awh_ready, at + 1)
                if begun(at):
                    dve.wait_ge(down_done, at)
                nc.vector.tensor_tensor(aw_parts[:, 1], aw[:, 0], aw_parts[:, 0].bitcast(F32), ALU.subtract)\
                    .then_inc(awl_ready, 1)

            def main(m, par, edge):
                act_on, tail_on, prep_on, norm_on = on(edge)
                for f in range(FC):
                    at = FC * m + f
                    if f > 0 and act_on or f == 0 and tail_on:
                        low_of_sum(at - 1)
                    if act_on:
                        for k in range(2):
                            dve.wait_ge(silu_ready, 2 * at + k + 1)
                            if begun(at):
                                dve.wait_ge(aw_step, 3 * at)
                                dve.wait_ge(al_ready, 2 * at)
                            nc.vector.tensor_tensor(a[:, k], silu[:, k], gu_ps[:, 1], ALU.mult).then_inc(a_ready, 1)
                            dve.wait_ge(ah_ready, 2 * at + k + 1)
                            if begun(at):
                                dve.wait_ge(z_done, at)
                            nc.vector.tensor_tensor(a_parts[:, k, 1], a[:, k], a_parts[:, k, 0].bitcast(F32),
                                                    ALU.subtract).then_inc(al_ready, 1)
                    if tail_on and f == 0:
                        if edge != 1:
                            dve.wait_ge(o_done, 2 * (m - 1))
                        dve.wait_ge(mask_ready, 2 * m)
                        dve.wait_ge(z_done, FC * m)
                        for k in range(2):
                            nc.vector.tensor_tensor(zm[:, k], z_ps[:, k], z_mask[:, k], ALU.mult).then_inc(zm_step, 1)
                        dve.wait_ge(zm_step, 3 * m - 1)
                        nc.vector.tensor_tensor(zm[:, 0], zm[:, 0], zm[:, 1], ALU.add).then_inc(zm_step, 1)
                    if tail_on and f == 2:
                        dve.wait_ge(o_ready, 2 * m)
                        for j in range(TT):
                            nc.vector.bn_stats(stats[:, j], o[:, j]).then_inc(st_done, 1)
                        dve.wait_ge(st_done, TT * m)
                        pass_waits(dve, dve_passed)
                        for j in range(TT):
                            nc.vector.bn_aggr(mv[:, j], stats[:, j]).then_inc(mv_done, 1)
                    if tail_on and f == 4:
                        dve.wait_ge(rstd_done, m)
                        for j in range(TT):
                            nc.vector.tensor_scalar(o[:, j], o[:, j], mv[:, j, 0:1], rstd[:, j:j + 1],
                                                    ALU.subtract, ALU.mult).then_inc(yn_done, 1)
                    if prep_on:
                        prep(m + 1, 1 - par, f)
                    if norm_on:
                        norm(m + 2, f)

            for f in range(FC):
                norm(0, f)
            for f in range(FC):
                prep(0, 0, f)
            for f in range(FC):
                norm(1, f)
            over_groups(main)(dve)

        @block.tensor
        def _(pe):
            def mm(out_, lhs, rhs, start, stop):
                return nc.tensor.matmul(out_, lhs, rhs, start=start, stop=stop)

            def onto(out_, lhs, rhs, start=False):
                return nc.tensor.matmul(out_, lhs, rhs, start=start, stop=True, skip_group_check=True)

            def flip(out_, blocks, width=P):
                for i, b in enumerate(blocks):
                    last = nc.tensor.transpose(out_[:, i * P:(i + 1) * P], b, ident[:, :])
                return last

            def prep(s, par, f):
                if f == 0:
                    pe.wait_ge(xn_done, TT * (s + 1))
                    for k in range(MC):
                        if begun(2 * s + k - 1):
                            pe.wait_ge(rw_ready, 2 * s + k - 1)
                        flip(side[:, k], [xg[:, j, k * P:(k + 1) * P] for j in range(TT)]).then_inc(xn_tp, 1)
                if f == 1:
                    pe.wait_ge(xh_ready, 2 * MC * (s + 1))
                    pe.wait_ge(xl_ready, MC * (s + 1))
                    for j in range(TT):
                        for k in range(MC):
                            last = mm(side[:, 0, j * E:(j + 1) * E], x_f[:, k, j * P:(j + 1) * P], w_router[:, k], k == 0,
                                      k == MC - 1)
                    last.then_inc(logits_done, 1)
                if f in (2, 3):
                    t = f - 2
                    if t == 0:
                        pe.wait_ge(rt, RT * s + 2)
                    else:
                        pe.wait_ge(hxl_ready, 2 * s + 1)
                    for i, (u, v) in enumerate(PAIRS):
                        for k in range(MC):
                            last = mm(side[:, 0], w_h[:, u, k, t * ER:(t + 1) * ER], x_t[:, par, v, k],
                                      i == 0 and k == 0, i == 2 and k == MC - 1)
                    last.then_inc(hx_done, 1)
                if f == 5:
                    pe.wait_ge(rt, RT * (s + 1))
                    pe.wait_ge(hxl_ready, 2 * (s + 1))
                    for j in range(TT):
                        last = nc.tensor.transpose(side[0:4 * E, 0, j * P:(j + 1) * P],
                                                   select[:, j].rearrange("p q e -> p (q e)"), ident[:, :])
                    last.then_inc(select_tp, 1)
                if f == 6:
                    pe.wait_ge(select_l, s + 1)
                    for k in range(2):
                        if k == 1 and begun(2 * s):
                            pe.wait_ge(mask_ready, 2 * s)
                        mm(side[:, k], expand[:, k], select_t[:, 0], True, True).then_inc(pick_done, 1)
                if f == 7:
                    for k in range(2):
                        pe.wait_ge(hm_ready, 8 * s + 4 * (k + 1))
                        for part in range(2):
                            last = mm(side[:, k], half[:, k], select_t[:, part], part == 0, part == 1)
                        last.then_inc(rw_done, 1)

            def z_product(f, at):
                pe.wait_ge(al_ready, 2 * at + 2)
                for k in range(2):
                    for i, (u, v) in enumerate(PAIRS):
                        last = mm(z_ps[:, k], a2[:, u, f], a_parts[:, k, v], f == 0 and i == 0, f == FC - 1 and i == 2)
                last.then_inc(z_done, 1)

            def down(f, at):
                pe.wait_ge(awl_ready, at + 1)
                for j in range(TT):
                    for i, (u, v) in enumerate(PAIRS):
                        last = onto(o_ps[:, j // 2, (j % 2) * DM:(j % 2 + 1) * DM], aw_parts[:, u, j * P:(j + 1) * P],
                                    w_down[:, v, f], start=f == 0 and i == 0 and j % 2 == 0)
                last.then_inc(down_done, 1)

            def main(m, par, edge):
                act_on, tail_on, prep_on, norm_on = on(edge)
                for f in range(FC):
                    cols = slice(f * P, (f + 1) * P)
                    at = FC * m + f
                    back = f > 0 and act_on or f == 0 and tail_on
                    if act_on:
                        if f == 0:
                            pe.wait_ge(xh_ready, 2 * MC * (m + 1))
                            pe.wait_ge(xl_ready, MC * (m + 1))
                            pe.wait_ge(hm_ready, 8 * m + 4)
                        if begun(2 * at):
                            pe.wait_ge(a_ready, 2 * at)
                        for t, wide, lora in ((0, w_gate, b_gate), (1, w_up, b_up)):
                            for i, (u, v) in enumerate(PAIRS):
                                for k in range(MC):
                                    mm(gu_ps[:, t], wide[:, u, k, cols], x_t[:, par, v, k], i == 0 and k == 0, False)
                            for i, (u, v) in enumerate(PAIRS):
                                last = mm(gu_ps[:, t], lora[:, u, cols], hm[:, par, v, 0, t], False, i == 2)
                        last.then_inc(base_done, 1)
                    if tail_on and f == 1:
                        pe.wait_ge(zm_step, 3 * m)
                        for j in range(TT):
                            last = onto(o_ps[:, j // 2, (j % 2) * DM:(j % 2 + 1) * DM], zm[:, 0, j * P:(j + 1) * P],
                                        b_down[:, :])
                            if j % 2:
                                last.then_inc(o_done, 1)
                    if back:
                        if f == 1 and tail_on:
                            pe.wait_ge(zm_step, 3 * m)
                        z_product((f - 1) % FC, at - 1)
                    if act_on:
                        if f == 0:
                            pe.wait_ge(hm_ready, 8 * (m + 1))
                        pe.wait_ge(a_ready, 2 * at + 1)
                        for t, lora in ((0, b_gate), (1, b_up)):
                            for u, v in PAIRS:
                                last = onto(gu_ps[:, t], lora[:, u, cols], hm[:, par, v, 1, t])
                        last.then_inc(diff_done, 1)
                    if back:
                        if f == 1 and tail_on:
                            pe.wait_ge(o_ready, 2 * m)
                        down((f - 1) % FC, at - 1)
                    if act_on and f in (1, 2):
                        k = f - 1
                        if k == 0:
                            pe.wait_ge(rw_ready, 2 * (m + 1))
                            if prep_on:
                                pe.wait_ge(xl_ready, MC * (m + 2))
                                pe.wait_ge(xh_ready, 2 * MC * (m + 2))
                        else:
                            pe.wait_ge(mask_ready, 2 * m + 1)
                        for part in range(2):
                            last = mm(side[:, 1], expand[:, 2 + k], select_t[:, part], part == 0, part == 1)
                        last.then_inc(mask_done, 1)
                    if prep_on:
                        prep(m + 1, 1 - par, f)

            for f in range(FC):
                prep(0, 0, f)
            over_groups(main)(pe)


@contextmanager
def consts_of(nc):
    with (nc.sbuf_tensor("ident", [P, P], F32) as ident, nc.sbuf_tensor("eps", [P, 1], F32) as eps,
          nc.sbuf_tensor("one", [P, 1], F32) as one):
        yield ident, eps, one


def build(nc, dram, out):
    x2 = nc.dram_tensor("x2_between", out.shape, F32, kind="Internal").ap()
    with consts_of(nc) as consts:
        mamba_phase(nc, dram["x"], dram, x2, consts)
        ffn_phase(nc, x2, dram, out, consts)


def lay_out(i):
    import numpy as np

    def chunks(a):
        a = np.asarray(a)
        return np.ascontiguousarray(a.reshape(-1, P, *a.shape[1:]).swapaxes(0, 1))

    at, ff = (lambda n: np.asarray(i["L0_attn_" + n])), (lambda n: np.asarray(i["L0_ffn_" + n]))
    return {
        "x": at("x"),
        "w_in": chunks(at("W_in").T), "conv_w": chunks(at("conv_w")), "conv_b": chunks(at("conv_b")),
        "w_x": chunks(at("W_x").T), "w_dt": np.ascontiguousarray(at("W_dt").T), "b_dt": chunks(at("b_dt")),
        "a_log": chunks(at("A_log")), "d_skip": chunks(at("Dp")), "w_out": chunks(at("W_out").T),
        "w_h": chunks(np.concatenate([ff("A1").reshape(ER, DM), ff("A3").reshape(ER, DM)]).T),
        "w_router": chunks(ff("gate_w").T),
        "w_gate": chunks(ff("w_gate").T), "w_up": chunks(ff("w_up").T),
        "b_gate": np.ascontiguousarray(ff("B1").transpose(0, 2, 1).reshape(ER, FF)),
        "b_up": np.ascontiguousarray(ff("B3").transpose(0, 2, 1).reshape(ER, FF)),
        "w_down": chunks(ff("w_down").T), "a2": chunks(ff("A2").reshape(ER, FF).T),
        "b_down": np.ascontiguousarray(ff("B2").transpose(0, 2, 1).reshape(ER, DM)),
    }


def kernel(**inputs):
    import numpy as np
    import concourse.bacc as bacc
    from concourse.bass_utils import run_bass_kernel_spmd

    arrays = lay_out(inputs)
    nc = bacc.Bacc("TRN2", target_bir_lowering=False, num_devices=1)
    dram = {n: nc.dram_tensor("in_" + n, a.shape, mybir.dt.from_np(a.dtype), kind="ExternalInput").ap()
            for n, a in arrays.items()}
    out = nc.dram_tensor("out", arrays["x"].shape, F32, kind="ExternalOutput").ap()
    build(nc, dram, out)
    r = run_bass_kernel_spmd(nc, [{"in_" + n: a for n, a in arrays.items()}], core_ids=[0])
    return r.results[0]["out"]
```

```python
import math
from contextlib import ExitStack, contextmanager

import concourse.bass as bass
import concourse.mybir as mybir
from concourse.alu_op_type import AluOpType as ALU

F32 = mybir.dt.float32
F32R = mybir.dt.float32r
ACT = mybir.ActivationFunctionType
AX = mybir.AxisListType

P = 128
SEQS, T, DM = 16, 512, 256
DI, NS, DTR, TAPS = 512, 16, 64, 4
TT, MC, DC = T // P, DM // P, DI // P
UNITS = NS * DC
E, R, FF = 8, 16, 1024
ER, FC = E * R, FF // P
EPS = 1e-5
LORA_SCALE = 2.0


def begun(count):
    return not isinstance(count, int) or count > 0


def pass_waits(eng, passed):
    eng.sem_inc(passed, 1)


def up_to(s):
    return min(s, SEQS) if isinstance(s, int) else s


def over_tiles(eng, count, step):
    step(0, 0, 0)
    step(1, 1, 1)
    with eng.Fori(2, count - 3, 2) as i:
        step(i, 0, None)
        step(i + 1, 1, None)
    step(count - 2, 0, count - 2)
    step(count - 1, 1, count - 1)


def row(ap4, s):
    if isinstance(s, int):
        return ap4[s]
    return ap4[bass.ds(s, 1)].rearrange("a p j d -> (a p) j d")


def mamba_phase(nc, x, w, x2_dram, consts, stage, next_weights):
    ident, eps, one = consts
    with ExitStack() as ctx:
        def sb(name, shape):
            return ctx.enter_context(nc.sbuf_tensor(name, shape, F32))

        def sem(name):
            return ctx.enter_context(nc.semaphore(name))

        w_in = sb("w_in", [P, MC, 2 * DI])
        conv_w = sb("conv_w", [P, DC, TAPS])
        conv_b = sb("conv_b", [P, DC])
        w_x = sb("w_x", [P, DC, DTR + 2 * NS])
        w_dt = sb("w_dt", [DTR, DI])
        b_dt = sb("b_dt", [P, DC])
        a_neg = sb("a_neg", [P, DC, NS])
        d_skip = sb("d_skip", [P, DC])
        w_out = sb("w_out", [P, DC, DM])
        xs = sb("xs", [P, TT, DM])
        stats = sb("stats", [P, TT, 6])
        mv = sb("mv", [P, TT, 2])
        lnv = sb("lnv", [P, TT])
        rstd = sb("rstd", [P, TT])
        xn = sb("xn", [P, TT, DM])
        xn_t = sb("xn_t", [P, MC, T])
        tap = sb("tap", [P, 2, TAPS - 1, T])
        xc = sb("xc", [P, 2, DC, T])
        zs = sb("zs", [P, 2, DC, T])
        dt_raw = sb("dt_raw", [DTR, T])
        bc = sb("bc", [P, 2, TT, 2 * NS])
        delta = sb("delta", [P, 2, DC, T])
        u_t = sb("u_t", [P, 2, TT, DI])
        v = stage[0].rearrange("p (a j d) -> p a j d", a=2, j=TT)
        da = stage[1].rearrange("p (a c t) -> p a c t", a=2, c=DC)
        h = stage[2].rearrange("p (a c t) -> p a c t", a=2, c=DC)
        y_acc = sb("y_acc", [P, 2, TT, DI])
        o = sb("o", [P, TT, DM])
        stats2 = sb("stats2", [P, TT, 6])
        mv2 = sb("mv2", [P, TT, 2])
        lnv2 = sb("lnv2", [P, TT])
        rstd2 = sb("rstd2", [P, TT])
        xr = sb("xr", [P, TT, DM])
        x2 = sb("x2", [P, TT, DM])
        work_a = sb("work_a", [P, DC, T])
        work_b = sb("work_b", [P, DC, T])
        y1, sp_abs = work_a, work_a
        g, sp_relu, u = work_b, work_b, work_b

        bx_ps = [ctx.enter_context(nc.psum_tensor(f"bx_ps{i}", [P, 512], F32)) for i in range(DC)]
        ht_ps = [ctx.enter_context(nc.psum_tensor(f"ht_ps{i}", [P, 512], F32)) for i in range(2)]
        side = ctx.enter_context(nc.psum_tensor("side", [P, 2, 512], F32))

        loaded = sem("loaded")
        a_exp = sem("a_exp")
        setup = sem("setup")
        ident_ready = sem("ident_ready")
        xs_loaded = sem("xs_loaded")
        dve_passed = sem("dve_passed")
        pool_passed = sem("pool_passed")
        st_done = sem("st_done")
        mv_done = sem("mv_done")
        rstd_done = sem("rstd_done")
        xn_done = sem("xn_done")
        xn_tp = sem("xn_tp")
        xn_t_ready = sem("xn_t_ready")
        xin_done = sem("xin_done")
        zin_done = sem("zin_done")
        tap_step = sem("tap_step")
        tap_ready = sem("tap_ready")
        conv_step = sem("conv_step")
        z_raw_ready = sem("z_raw_ready")
        xc_ready = sem("xc_ready")
        dtr_done = sem("dtr_done")
        bc_done = sem("bc_done")
        dt_raw_ready = sem("dt_raw_ready")
        bc_ready = sem("bc_ready")
        dt_done = sem("dt_done")
        abs_ready = sem("abs_ready")
        relu_ready = sem("relu_ready")
        exp_ready = sem("exp_ready")
        ln_ready = sem("ln_ready")
        delta_ready = sem("delta_ready")
        u_ready = sem("u_ready")
        u_tp = sem("u_tp")
        u_t_ready = sem("u_t_ready")
        v_ready = sem("v_ready")
        bx_done = sem("bx_done")
        da_ready = sem("da_ready")
        scan_done = sem("scan_done")
        ht_done = sem("ht_done")
        y_done = sem("y_done")
        acc_tp = sem("acc_tp")
        y1_done = sem("y1_done")
        g_done = sem("g_done")
        oproj_done = sem("oproj_done")
        o_ready = sem("o_ready")
        st2_done = sem("st2_done")
        mv2_done = sem("mv2_done")
        lnv2_done = sem("lnv2_done")
        lnv_done = sem("lnv_done")
        rstd2_done = sem("rstd2_done")
        yn_done = sem("yn_done")
        xr_loaded = sem("xr_loaded")
        x2_ready = sem("x2_ready")
        x2_stored = sem("x2_stored")

        x_v = x.rearrange("s (j p) d -> s p j d", p=P)
        x2_v = x2_dram.rearrange("s (j p) d -> s p j d", p=P)
        LOADS = [(w_in[:, :, :], w["w_in"]), (conv_w[:, :, :], w["conv_w"]), (conv_b[:, :], w["conv_b"]),
                 (w_x[:, :, :], w["w_x"]), (w_dt[:, :], w["w_dt"]), (b_dt[:, :], w["b_dt"]),
                 (a_neg[:, :, :], w["a_log"]), (d_skip[:, :], w["d_skip"]), (w_out[:, :, :], w["w_out"])]
        ALL_LOADED = 16 * len(LOADS)
        SETUP = 1
        PIECES = UNITS + 2
        XN_FLIP = (0, 1)
        ACC_FLIP = (5, 6, 7, 8)
        X_IN, Z_IN = (11, 15, 18, 25), (22, 29, 31, 33)
        OUT = (20, 24, 28, 36, 37, 39, 40, 42)
        DT_IN = (43, 44, 45, 46)
        DT = (48, 50, 52, 54)
        BC_IN = (47, 49, 51, 53)
        U_FLIP = (56, 58, 60, 62)
        XN_COPY, IN_COPY = (4, 5), 6
        SILU, DT_COPY, BC_COPY = 43, 49, 57
        SOFTPLUS = (51, 53, 56, 59)
        U_COPY = (60, 62, 64, 65)
        O_COPY = (40, 47)
        RSTD, RSTD2 = 39, 61
        GATE = (12, 13, 16, 17)
        CONV = ((20, 21, 22), (24, 25, 28), (29, 30, 32), (33, 34, 36))
        Y1 = (6, 7, 8, 9)
        DELTA = (53, 55, 58, 60)
        STATS, NORM = (30, 31, 32, 33), (42, 43, 44, 45)
        STATS2 = (43, 44, 49, 51)
        NORM2 = (1, 2, 3, 4)

        IN_ORDER = sorted(X_IN + Z_IN)

        def in_bank(s, at):
            return IN_ORDER.index(at) % 2 if isinstance(s, int) and s == 0 else 0

        def in_before(s, at, which):
            turns = 2 if isinstance(s, int) and s == 0 else 1
            return sum(a in which for a in IN_ORDER[:max(0, IN_ORDER.index(at) - turns + 1)])

        block = ctx.enter_context(nc.Block())

        @block.sync
        def _(sp):
            sp.dma_start(xs[:, :, :], x_v[0]).then_inc(xs_loaded, 16)
            for dst, src in LOADS:
                sp.dma_start(dst, src).then_inc(loaded, 16)
            sp.wait_ge(xn_done, TT)
            sp.dma_start(xs[:, :, :], x_v[1]).then_inc(xs_loaded, 16)
            sp.sem_inc(x2_stored, 16)

            def main(m, par, edge):
                first, last = edge == 0, edge == SEQS - 1
                ahead = edge in (None, 0, 1)
                if ahead:
                    sp.wait_ge(xn_done, TT * (m + 2))
                    sp.dma_start(xs[:, :, :], row(x_v, m + 2)).then_inc(xs_loaded, 16)
                if edge not in (0, 1):
                    sp.wait_ge(x2_ready, m - 1)
                    sp.dma_start(row(x2_v, m - 2), x2[:, :, :]).then_inc(x2_stored, 16)
                if not first:
                    sp.dma_start(xr[:, :, :], row(x_v, m - 1)).then_inc(xr_loaded, 16)

            over_tiles(sp, SEQS, main)
            sp.wait_ge(ht_done, UNITS * SEQS)
            for dst, src, raw_loaded in next_weights:
                sp.dma_start(dst, src).then_inc(raw_loaded, 16)
            sp.wait_ge(x2_ready, SEQS - 1)
            sp.dma_start(x2_v[SEQS - 2], x2[:, :, :]).then_inc(x2_stored, 16)
            sp.dma_start(xr[:, :, :], x_v[SEQS - 1]).then_inc(xr_loaded, 16)
            sp.wait_ge(x2_ready, SEQS)
            sp.dma_start(x2_v[SEQS - 1], x2[:, :, :]).then_inc(x2_stored, 16)
            sp.wait_ge(x2_stored, 16 * (SEQS + 1))

        @block.gpsimd
        def _(pool):
            def prep(s, par, q):
                for c in range(DC):
                    if q in CONV[c]:
                        back = 1 + CONV[c].index(q)
                        if back == 1:
                            pool.wait_ge(tap_ready, DC * s + c + 1)
                        else:
                            pool.wait_ge(conv_step, (TAPS - 1) * (DC * s + c) + back - 1)
                        nc.gpsimd.tensor_tensor(xc[:, par, c, back:T], xc[:, par, c, back:T],
                                                tap[:, c % 2, TAPS - 1 - back, 0:T - back], ALU.add).then_inc(conv_step, 1)

            def tail(s, par, q):
                if q in GATE:
                    c = GATE.index(q)
                    pool.wait_ge(u_tp, DC * up_to(s + 2))
                    pool.wait_ge(y1_done, DC * s + c + 1)
                    nc.gpsimd.tensor_tensor(g[:, c], y1[:, c], zs[:, par, c], ALU.mult).then_inc(g_done, 1)


            def residual(s, q):
                if q == 8:
                    pool.wait_ge(yn_done, TT * (s + 1))
                    pool.wait_ge(xr_loaded, 16 * (s + 1))
                    pool.wait_ge(x2_stored, 16 * (s + 1))
                    nc.gpsimd.tensor_tensor(x2[:, :, :], o[:, :, :], xr[:, :, :], ALU.add).then_inc(x2_ready, 1)

            def main(m, par, edge):
                first, last = edge == 0, edge == SEQS - 1
                ahead = edge in (None, 0, 1)
                pool.wait_ge(u_t_ready, DC * (m + 1))
                pool.wait_ge(bc_ready, m + 1)
                for n in range(NS):
                    if begun(UNITS * m + DC * (n - 1)):
                        pool.wait_ge(bx_done, UNITS * m + DC * (n - 1))
                    pass_waits(pool, pool_passed)
                    for j in range(TT):
                        nc.gpsimd.tensor_scalar(v[:, n % 2, j], u_t[:, par, j], bc[:, par, j, n:n + 1], 1.0,
                                                ALU.mult, ALU.mult).then_inc(v_ready, 1)
                    for q in range(DC * n, DC * (n + 1)):
                        if not first:
                            tail(m - 1, 1 - par, q)
                        if not last:
                            prep(m + 1, 1 - par, q)
                        if edge not in (0, 1):
                            residual(m - 2, q)

            nc.gpsimd.memset(ident[:, :], 0.0).then_inc(ident_ready, 1)
            nc.gpsimd.memset(eps[:, :], EPS).then_inc(ident_ready, 1)
            nc.gpsimd.memset(one[:, :], 1.0).then_inc(ident_ready, 1)
            pool.wait_ge(ident_ready, 3)
            nc.gpsimd.affine_select(out=ident[:, :], in_=ident[:, :], compare_op=ALU.not_equal, fill=1.0,
                                    base=0, pattern=[[-1, P]], channel_multiplier=1).then_inc(ident_ready, 1)
            pool.wait_ge(loaded, ALL_LOADED)
            for q in range(PIECES):
                prep(0, 0, q)
            over_tiles(pool, SEQS, main)
            residual(SEQS - 2, 8)
            for q in range(PIECES):
                tail(SEQS - 1, 1, q)
            residual(SEQS - 1, 8)

        @block.scalar
        def _(act):
            def norm(s, q):
                if q == RSTD:
                    act.wait_ge(mv_done, TT * (s + 1))
                    nc.scalar.activation(lnv[:, :], mv[:, :, 1], ACT.Ln, bias=eps[:, 0:1]).then_inc(lnv_done, 1)
                    act.wait_ge(lnv_done, s + 1)
                    nc.scalar.activation(rstd[:, :], lnv[:, :], ACT.Exp, scale=-0.5).then_inc(rstd_done, 1)

            def prep(s, par, q):
                if q in XN_COPY:
                    k = XN_COPY.index(q)
                    if begun(DC * s):
                        act.wait_ge(zin_done, DC * s)
                    act.wait_ge(xn_tp, MC * s + k + 1)
                    nc.scalar.activation(xn_t[:, k], side[:, k], ACT.Copy).then_inc(xn_t_ready, 1)
                for c in range(DC):
                    if q == X_IN[c] + IN_COPY:
                        if begun(DC * (s - 2) + c + 1):
                            act.wait_ge(y1_done, DC * (s - 2) + c + 1)
                            act.wait_ge(u_ready, DC * (s - 1))
                        if begun(DC * s + c - 1):
                            act.wait_ge(conv_step, (TAPS - 1) * (DC * s + c - 1))
                        act.wait_ge(xin_done, DC * s + c + 1)
                        for k in range(TAPS - 1):
                            nc.scalar.activation(tap[:, c % 2, k], side[:, in_bank(s, X_IN[c])], ACT.Copy, scale=conv_w[:, c, k:k + 1])\
                                .then_inc(tap_step, 1)
                        nc.scalar.activation(xc[:, par, c], side[:, in_bank(s, X_IN[c])], ACT.Identity, bias=conv_b[:, c:c + 1],
                                             scale=conv_w[:, c, TAPS - 1:TAPS]).then_inc(tap_ready, 1)
                    if q == Z_IN[c] + IN_COPY:
                        if begun(DC * (s - 2) + c + 1):
                            act.wait_ge(g_done, DC * (s - 2) + c + 1)
                        act.wait_ge(zin_done, DC * s + c + 1)
                        nc.scalar.activation(zs[:, par, c], side[:, in_bank(s, Z_IN[c])], ACT.Copy).then_inc(z_raw_ready, 1)
                if q == SILU:
                    act.wait_ge(conv_step, (TAPS - 1) * DC * (s + 1))
                    nc.scalar.activation(xc[:, par], xc[:, par], ACT.Silu).then_inc(xc_ready, 1)
                    act.wait_ge(z_raw_ready, DC * (s + 1))
                    nc.scalar.activation(zs[:, par], zs[:, par], ACT.Silu).then_inc(xc_ready, 1)
                    nc.scalar.preload_act_table_set("natural_log_exp_and_others")
                if q == DT_COPY:
                    if begun(DC * s):
                        act.wait_ge(dt_done, DC * s)
                    act.wait_ge(dtr_done, s + 1)
                    nc.scalar.activation(dt_raw[:, :], side[0:DTR, 0], ACT.Copy).then_inc(dt_raw_ready, 1)
                if q == BC_COPY:
                    if begun(UNITS * (s - 1)):
                        act.wait_ge(y_done, UNITS * (s - 1))
                        act.wait_ge(v_ready, UNITS * (s - 1))
                    act.wait_ge(bc_done, s + 1)
                    nc.scalar.activation(bc[:, par].rearrange("p j n -> p (j n)"), side[:, 1, 0:TT * 2 * NS], ACT.Copy)\
                        .then_inc(bc_ready, 1)
                if q in SOFTPLUS:
                    c = SOFTPLUS.index(q)
                    if begun(2 * (s - 1)):
                        act.wait_ge(oproj_done, 2 * (s - 1))
                    if begun(DC * (s - 1)):
                        act.wait_ge(g_done, DC * (s - 1))
                    if begun(DC * s):
                        act.wait_ge(u_tp, DC * s)
                        act.wait_ge(u_ready, DC * s)
                    act.wait_ge(dt_done, DC * s + c + 1)
                    nc.scalar.activation(sp_abs[:, c], side[:, 0], ACT.Abs, bias=b_dt[:, c:c + 1]).then_inc(abs_ready, 1)
                    nc.scalar.activation(sp_relu[:, c], side[:, 0], ACT.Relu, bias=b_dt[:, c:c + 1])\
                        .then_inc(relu_ready, 1)
                    act.wait_ge(abs_ready, DC * s + c + 1)
                    nc.scalar.activation(sp_abs[:, c], sp_abs[:, c], ACT.Exp, scale=-1.0).then_inc(exp_ready, 1)
                    act.wait_ge(exp_ready, DC * s + c + 1)
                    nc.scalar.activation(sp_abs[:, c], sp_abs[:, c], ACT.Ln, bias=one[:, 0:1]).then_inc(ln_ready, 1)

                for c in range(DC):
                    if q == U_COPY[c]:
                        if begun(UNITS * (s - 1)):
                            act.wait_ge(v_ready, UNITS * (s - 1))
                        act.wait_ge(u_tp, DC * s + c + 1)
                        nc.scalar.activation(u_t[:, par, :, c * P:(c + 1) * P],
                                             side[:, 1].rearrange("p (j d) -> p j d", j=TT), ACT.Copy)\
                            .then_inc(u_t_ready, 1)

            def tail(s, par, q):
                if q in O_COPY:
                    k = O_COPY.index(q)
                    act.wait_ge(y_done, UNITS * (s + 1))
                    act.wait_ge(x2_stored, 16 * (s + 1))
                    act.wait_ge(oproj_done, 2 * s + k + 1)
                    nc.scalar.activation(o[:, 2 * k:2 * k + 2].rearrange("p j d -> p (j d)"), side[:, 1], ACT.Copy)\
                        .then_inc(o_ready, 1)
                if q == RSTD2:
                    act.wait_ge(mv2_done, TT * (s + 1))
                    nc.scalar.activation(lnv2[:, :], mv2[:, :, 1], ACT.Ln, bias=eps[:, 0:1]).then_inc(lnv2_done, 1)
                    act.wait_ge(lnv2_done, s + 1)
                    nc.scalar.activation(rstd2[:, :], lnv2[:, :], ACT.Exp, scale=-0.5).then_inc(rstd2_done, 1)

            def main(m, par, edge):
                first, last = edge == 0, edge == SEQS - 1
                ahead = edge in (None, 0, 1)
                for n in range(NS):
                    for i in range(DC):
                        if n == 0:
                            act.wait_ge(delta_ready, DC * m + i + 1)
                        if begun(UNITS * m + DC * (n - 2) + i + 1):
                            act.wait_ge(scan_done, UNITS * m + DC * (n - 2) + i + 1)
                        nc.scalar.activation(da[:, n % 2, i], delta[:, par, i], ACT.Exp, scale=a_neg[:, i, n:n + 1])\
                            .then_inc(da_ready, 1)
                        if not first:
                            tail(m - 1, 1 - par, DC * n + i)
                        if not last:
                            prep(m + 1, 1 - par, DC * n + i)
                        if ahead:
                            norm(m + 2, DC * n + i)
                if not last:
                    for q in range(UNITS, PIECES):
                        prep(m + 1, 1 - par, q)

            act.wait_ge(loaded, ALL_LOADED)
            act.wait_ge(ident_ready, 3)
            nc.scalar.preload_act_table_set("natural_log_exp_and_others")
            nc.scalar.activation(a_neg[:, :, :], a_neg[:, :, :], ACT.Exp).then_inc(a_exp, 1)
            for q in range(PIECES):
                norm(0, q)
            for q in range(PIECES):
                prep(0, 0, q)
            for q in range(PIECES):
                norm(1, q)
            act.wait_ge(setup, SETUP)
            over_tiles(act, SEQS, main)
            for q in range(PIECES):
                tail(SEQS - 1, 1, q)

        @block.vector
        def _(dve):
            def norm(s, q):
                if q in STATS:
                    dve.wait_ge(xs_loaded, 16 * (s + 1))
                    if begun(TT * s):
                        dve.wait_ge(mv_done, TT * s)
                    nc.vector.bn_stats(stats[:, STATS.index(q)], xs[:, STATS.index(q)]).then_inc(st_done, 1)
                if q - 1 in STATS:
                    j = STATS.index(q - 1)
                    if begun(TT * s):
                        dve.wait_ge(xn_done, TT * s)
                    dve.wait_ge(st_done, TT * s + j + 1)
                    pass_waits(dve, dve_passed)
                    nc.vector.bn_aggr(mv[:, j], stats[:, j]).then_inc(mv_done, 1)
                if q in NORM:
                    j = NORM.index(q)
                    dve.wait_ge(rstd_done, s + 1)
                    if begun(MC * s):
                        dve.wait_ge(xn_tp, MC * s)
                    nc.vector.tensor_scalar(xn[:, j], xs[:, j], mv[:, j, 0:1], rstd[:, j:j + 1],
                                            ALU.subtract, ALU.mult).then_inc(xn_done, 1)

            def prep(s, par, q):
                if q in DELTA:
                    c = DELTA.index(q)
                    if begun(UNITS * (s - 1)):
                        dve.wait_ge(da_ready, UNITS * (s - 1))
                    dve.wait_ge(ln_ready, DC * s + c + 1)
                    nc.vector.tensor_tensor(delta[:, par, c], sp_relu[:, c], sp_abs[:, c], ALU.add).then_inc(delta_ready, 1)
                    dve.wait_ge(delta_ready, DC * s + c + 1)
                    nc.vector.tensor_tensor(u[:, c], delta[:, par, c], xc[:, par, c], ALU.mult).then_inc(u_ready, 1)

            def tail(s, par, q):
                for c in range(DC):
                    if q == Y1[c]:
                        dve.wait_ge(u_ready, DC * up_to(s + 2))
                        dve.wait_ge(acc_tp, DC * s + c + 1)
                        nc.vector.scalar_tensor_tensor(y1[:, c], xc[:, par, c], d_skip[:, c:c + 1], side[:, c % 2],
                                                       ALU.mult, ALU.add).then_inc(y1_done, 1)
                if q in STATS2:
                    j = STATS2.index(q)
                    dve.wait_ge(o_ready, 2 * s + j // 2 + 1)
                    dve.wait_ge(y_done, UNITS * (s + 1))
                    nc.vector.bn_stats(stats2[:, j], o[:, j]).then_inc(st2_done, 1)
                if q - 1 in STATS2:
                    j = STATS2.index(q - 1)
                    dve.wait_ge(st2_done, TT * s + j + 1)
                    pass_waits(dve, dve_passed)
                    nc.vector.bn_aggr(mv2[:, j], stats2[:, j]).then_inc(mv2_done, 1)

            def late(s, q):
                if q in NORM2:
                    j = NORM2.index(q)
                    dve.wait_ge(rstd2_done, s + 1)
                    nc.vector.tensor_scalar(o[:, j], o[:, j], mv2[:, j, 0:1], rstd2[:, j:j + 1],
                                            ALU.subtract, ALU.mult).then_inc(yn_done, 1)

            def add(m, par, n, i):
                at = UNITS * m + DC * n + i
                scale = bc[:, par, i, NS + n:NS + n + 1]
                dve.wait_ge(ht_done, at + 1)
                if n == 0:
                    nc.vector.tensor_scalar(y_acc[:, par, i], ht_ps[i % 2][:, :], scale, None, ALU.mult).then_inc(y_done, 1)
                else:
                    dve.wait_ge(y_done, at - DC + 1)
                    nc.vector.scalar_tensor_tensor(y_acc[:, par, i], ht_ps[i % 2][:, :], scale, y_acc[:, par, i],
                                                   ALU.mult, ALU.add).then_inc(y_done, 1)

            def main(m, par, edge):
                first, last = edge == 0, edge == SEQS - 1
                ahead = edge in (None, 0, 1)
                for n in range(NS):
                    for i in range(DC):
                        at = UNITS * m + DC * n + i
                        if begun(UNITS * m + DC * (n - 1)):
                            dve.wait_ge(ht_done, UNITS * m + DC * (n - 1))
                        dve.wait_ge(da_ready, at + 1)
                        dve.wait_ge(bx_done, at + 1)
                        nc.vector.tensor_tensor_scan(h[:, n % 2, i], da[:, n % 2, i], bx_ps[i][:, :], 0.0,
                                                     ALU.mult, ALU.add).then_inc(scan_done, 1)
                        if n > 0:
                            add(m, par, n - 1, i)
                        elif not first:
                            add(m - 1, 1 - par, NS - 1, i)
                        if not first:
                            tail(m - 1, 1 - par, DC * n + i)
                        if edge not in (0, 1):
                            late(m - 2, DC * n + i)
                        if not last:
                            prep(m + 1, 1 - par, DC * n + i)
                        if ahead:
                            norm(m + 2, DC * n + i)

            dve.wait_ge(loaded, ALL_LOADED)
            dve.wait_ge(a_exp, 1)
            nc.vector.tensor_scalar(a_neg[:, :, :], a_neg[:, :, :], -1.0, None, ALU.mult).then_inc(setup, 1)
            for q in range(PIECES):
                norm(0, q)
            for q in range(PIECES):
                prep(0, 0, q)
            for q in range(PIECES):
                norm(1, q)
            dve.wait_ge(bc_ready, 1)
            over_tiles(dve, SEQS, main)
            for i in range(DC):
                add(SEQS - 1, 1, NS - 1, i)
            for q in range(PIECES):
                late(SEQS - 2, q)
            for q in range(PIECES):
                tail(SEQS - 1, 1, q)
            for q in range(PIECES):
                late(SEQS - 1, q)

        @block.tensor
        def _(pe):
            def mm(out, lhs, rhs, start, stop):
                return nc.tensor.matmul(out, lhs, rhs, start=start, stop=stop)

            def flip(out, blocks):
                for i, b in enumerate(blocks):
                    last = nc.tensor.transpose(out[:, i * P:(i + 1) * P], b, ident[:, :])
                return last

            def prep(s, par, q):
                if q in XN_FLIP:
                    k = XN_FLIP.index(q)
                    pe.wait_ge(xn_done, TT * (s + 1))
                    if begun(DC * s):
                        pe.wait_ge(u_t_ready, DC * s)
                    flip(side[:, k], [xn[:, j, k * P:(k + 1) * P] for j in range(TT)]).then_inc(xn_tp, 1)
                for c in range(DC):
                    for start, first_col, done in ((X_IN, 0, xin_done), (Z_IN, DI, zin_done)):
                        e = q - start[c]
                        if e == 0:
                            pe.wait_ge(xn_t_ready, MC * (s + 1))
                            if begun(DC * (s - 1)):
                                pe.wait_ge(y1_done, DC * (s - 1))
                            if begun(DC * s + in_before(s, q, X_IN)):
                                pe.wait_ge(tap_ready, DC * s + in_before(s, q, X_IN))
                            if begun(DC * s + in_before(s, q, Z_IN)):
                                pe.wait_ge(z_raw_ready, DC * s + in_before(s, q, Z_IN))
                        if e in range(MC):
                            cols = slice(first_col + c * P, first_col + (c + 1) * P)
                            last = mm(side[:, in_bank(s, start[c])], w_in[:, e, cols], xn_t[:, e], e == 0, e == MC - 1)
                            if e == MC - 1:
                                last.then_inc(done, 1)
                if q in DT_IN:
                    c = DT_IN.index(q)
                    pe.wait_ge(xc_ready, 2 * s + 1)
                    pe.wait_ge(z_raw_ready, DC * (s + 1))
                    last = mm(side[0:DTR, 0], w_x[:, c, 0:DTR], xc[:, par, c], c == 0, c == DC - 1)
                    if c == DC - 1:
                        last.then_inc(dtr_done, 1)
                if q in BC_IN:
                    j = BC_IN.index(q)
                    if begun(2 * (s - 1)):
                        pe.wait_ge(o_ready, 2 * (s - 1))
                    elif j == 0:
                        pe.wait_ge(xn_t_ready, MC * (s + 1))
                    for c in range(DC):
                        last = mm(side[:, 1, j * 2 * NS:(j + 1) * 2 * NS], xc[:, par, c, j * P:(j + 1) * P],
                                  w_x[:, c, DTR:DTR + 2 * NS], c == 0, c == DC - 1)
                    if j == TT - 1:
                        last.then_inc(bc_done, 1)
                if q in DT:
                    c = DT.index(q)
                    pe.wait_ge(dt_raw_ready, s + 1)
                    if begun(DC * s + c):
                        pe.wait_ge(relu_ready, DC * s + c)
                    mm(side[:, 0], w_dt[:, c * P:(c + 1) * P], dt_raw[:, :], True, True).then_inc(dt_done, 1)
                if q in U_FLIP:
                    c = U_FLIP.index(q)
                    pe.wait_ge(u_ready, DC * s + c + 1)
                    if c == 0:
                        pe.wait_ge(bc_ready, s + 1)
                    else:
                        pe.wait_ge(u_t_ready, DC * s + c)
                    flip(side[:, 1], [u[:, c, j * P:(j + 1) * P] for j in range(TT)]).then_inc(u_tp, 1)

            def tail(s, par, q):
                if q in ACC_FLIP:
                    c = ACC_FLIP.index(q)
                    pe.wait_ge(y_done, UNITS * (s + 1))
                    if c < 2:
                        pe.wait_ge(u_t_ready, DC * up_to(s + 2))
                        pe.wait_ge(xn_t_ready, MC * up_to(s + 3))
                    else:
                        pe.wait_ge(y1_done, DC * s + c - 1)
                    flip(side[:, c % 2], [y_acc[:, par, j, c * P:(c + 1) * P] for j in range(TT)]).then_inc(acc_tp, 1)
                if q in OUT:
                    j, half = divmod(OUT.index(q), 2)
                    pe.wait_ge(g_done, DC * (s + 1))
                    pe.wait_ge(y1_done, DC * (s + 1))
                    if j >= 2:
                        pe.wait_ge(o_ready, 2 * s + 1)
                    for c in (2 * half, 2 * half + 1):
                        last = mm(side[:, 1, (j % 2) * DM:(j % 2 + 1) * DM], g[:, c, j * P:(j + 1) * P],
                                  w_out[:, c], c == 0, c == DC - 1)
                    if j % 2 and half:
                        last.then_inc(oproj_done, 1)

            def flip_h(m, n, i):
                at = UNITS * m + DC * n + i
                pe.wait_ge(scan_done, UNITS * m + DC * (n + 1))
                if begun(at - 1):
                    pe.wait_ge(y_done, at - 1)
                flip(ht_ps[i % 2], [h[:, n % 2, c, i * P:(i + 1) * P] for c in range(DC)]).then_inc(ht_done, 1)

            def main(m, par, edge):
                first, last = edge == 0, edge == SEQS - 1
                ahead = edge in (None, 0, 1)
                for n in range(NS):
                    for i in range(DC):
                        at = UNITS * m + DC * n + i
                        pe.wait_ge(v_ready, UNITS * m + TT * (n + 1))
                        if begun(at - DC + 1):
                            pe.wait_ge(scan_done, at - DC + 1)
                        flip(bx_ps[i], [v[:, n % 2, j, i * P:(i + 1) * P] for j in range(TT)]).then_inc(bx_done, 1)
                        if n > 0:
                            flip_h(m, n - 1, i)
                        elif not first:
                            flip_h(m - 1, NS - 1, i)
                        if not first:
                            tail(m - 1, 1 - par, DC * n + i)
                        if not last:
                            prep(m + 1, 1 - par, DC * n + i)
                if not last:
                    for q in range(UNITS, PIECES):
                        prep(m + 1, 1 - par, q)

            pe.wait_ge(loaded, ALL_LOADED)
            pe.wait_ge(ident_ready, 4)
            for q in range(PIECES):
                prep(0, 0, q)
            over_tiles(pe, SEQS, main)
            for i in range(DC):
                flip_h(SEQS - 1, NS - 1, i)
            for q in range(PIECES):
                tail(SEQS - 1, 1, q)



RAW = ("w_h", "w_gate", "w_up", "b_gate", "b_up", "w_down", "a2")
RAW_SHAPES = ([MC, 2 * ER], [MC, FF], [MC, FF], [FF], [FF], [FC, DM], [FC, ER])
STAGE = 2 * TT * DI
RAW_AT = {"w_gate": (0, 0), "w_up": (0, MC * FF), "w_down": (1, 0), "b_gate": (1, FC * DM), "b_up": (1, FC * DM + FF),
          "a2": (2, 0), "w_h": (2, FC * ER)}


def raw_weights(stage, w, sems):
    places = []
    for n, shape in zip(RAW, RAW_SHAPES):
        b, at = RAW_AT[n]
        flat = w[n].rearrange("p k d -> p (k d)") if len(shape) == 2 else w[n]
        places.append((stage[b][:, at:at + int(math.prod(shape))], flat, sems[n]))
    return places


def split_weights(nc, ctx, w, stage, raw_sems):
    def sb(name, shape, dtype):
        return ctx.enter_context(nc.sbuf_tensor("f_" + name, shape, dtype))

    names, shapes = RAW, RAW_SHAPES
    places = raw_weights(stage, w, raw_sems)
    sizes = [int(math.prod(s)) for s in shapes]
    split = {n: sb(n, [P, 2, size], F32R) for n, size in zip(names, sizes)}
    weights = {"b_down": sb("b_down", [P, DM], F32), "w_router": sb("w_router", [P, MC, E], F32),
               "expand": sb("expand", [4 * E, 4, P], F32R), "half": sb("half", [4 * E, 2, P], F32R),
               "rank": sb("rank", [P, TT, E], F32)}
    with ExitStack() as setup:
        raw, raw_loaded = [p[0] for p in places], [p[2] for p in places]
        expand = stage[2][0:4 * E, STAGE // 2:STAGE // 2 + 4 * P].rearrange("p (q c) -> p q c", q=4)
        half = stage[2][0:4 * E, STAGE // 2 + 4 * P:STAGE // 2 + 6 * P].rearrange("p (q c) -> p q c", q=2)
        small_loaded = setup.enter_context(nc.semaphore("small_loaded"))
        high_ready = setup.enter_context(nc.semaphore("high_ready"))
        low_ready = setup.enter_context(nc.semaphore("low_ready"))
        const_step = setup.enter_context(nc.semaphore("const_step"))
        rank_ready = setup.enter_context(nc.semaphore("rank_ready"))
        block = setup.enter_context(nc.Block())

        @block.sync
        def _(sp):
            sp.dma_start(weights["b_down"][:, :], w["b_down"]).then_inc(small_loaded, 16)
            sp.dma_start(weights["w_router"][:, :, :], w["w_router"]).then_inc(small_loaded, 16)
            sp.wait_ge(small_loaded, 32)

        @block.scalar
        def _(act):
            for i, n in enumerate(names):
                act.wait_ge(raw_loaded[i], 16)
                nc.scalar.activation(split[n][:, 0], raw[i], ACT.Copy).then_inc(high_ready, 1)
            act.wait_ge(const_step, 5)
            nc.scalar.activation(weights["expand"][:, :, :], expand[:, :, :], ACT.Copy).then_inc(high_ready, 1)
            nc.scalar.activation(weights["half"][:, :, :], half[:, :, :], ACT.Copy).then_inc(high_ready, 1)
            act.wait_ge(high_ready, len(names) + 2)

        @block.vector
        def _(dve):
            for i, n in enumerate(names):
                dve.wait_ge(raw_loaded[i], 16)
                dve.wait_ge(high_ready, i + 1)
                nc.vector.tensor_tensor(split[n][:, 1], raw[i], split[n][:, 0].bitcast(F32), ALU.subtract)\
                    .then_inc(low_ready, 1)
            dve.wait_ge(low_ready, len(names))

        @block.gpsimd
        def _(pool):
            nc.gpsimd.memset(expand[:, :, :], 0.0).then_inc(const_step, 1)
            pool.wait_ge(const_step, 1)
            expand_er = expand.rearrange("p q (e r) -> p q e r", e=E)
            nc.gpsimd.affine_select(out=expand_er, in_=expand_er, compare_op=ALU.not_equal, fill=1.0, base=0,
                                    pattern=[[-E, 4], [-1, E], [0, R]], channel_multiplier=1).then_inc(const_step, 1)
            nc.gpsimd.memset(half[:, :, :], 1.0 / LORA_SCALE).then_inc(const_step, 1)
            pool.wait_ge(const_step, 3)
            nc.gpsimd.affine_select(out=half[:, :, :], in_=half[:, :, :], compare_op=ALU.is_ge, fill=0.0, base=-2 * E,
                                    pattern=[[-E, 2], [0, P]], channel_multiplier=1).then_inc(const_step, 1)
            pool.wait_ge(const_step, 4)
            nc.gpsimd.affine_select(out=half[:, :, :], in_=half[:, :, :], compare_op=ALU.is_ge, fill=0.0, base=3 * E - 1,
                                    pattern=[[E, 2], [0, P]], channel_multiplier=-1).then_inc(const_step, 1)
            for e in range(E):
                nc.gpsimd.memset(weights["rank"][:, :, e:e + 1], float(E - e)).then_inc(rank_ready, 1)
            pool.wait_ge(rank_ready, E)
            pool.wait_ge(const_step, 5)

    for n, shape in zip(names, shapes):
        t = split[n]
        weights[n] = t.rearrange("p a (k d) -> p a k d", k=shape[0]) if len(shape) == 2 else t[:, :, :]
    return weights


def ffn_phase(nc, x2_dram, w, out, consts, stage, raw_sems):
    ident, eps, _ = consts
    with ExitStack() as ctx:
        weights = split_weights(nc, ctx, w, stage, raw_sems)
        w_h, w_gate, w_up, b_gate, b_up = (weights[n] for n in ("w_h", "w_gate", "w_up", "b_gate", "b_up"))
        w_down, a2, b_down, w_router = (weights[n] for n in ("w_down", "a2", "b_down", "w_router"))
        expand, half, rank = (weights[n] for n in ("expand", "half", "rank"))

        def sb(name, shape, dtype=F32):
            return ctx.enter_context(nc.sbuf_tensor("f_" + name, shape, dtype))

        def staged(b, quarter, dims, pattern):
            size = int(math.prod(dims))
            at = quarter * STAGE // 4
            return stage[b][:, at:at + size].rearrange(pattern, **dict(zip("abc", dims)))

        def sem(name):
            return ctx.enter_context(nc.semaphore("f_" + name))

        GROUPS = SEQS
        xg = staged(0, 0, [TT, DM], "p (a b) -> p a b")
        xg_stats = sb("xg_stats", [P, TT, 6])
        xg_mv = sb("xg_mv", [P, TT, 2])
        xg_lnv = sb("xg_lnv", [P, TT])
        xg_rstd = sb("xg_rstd", [P, TT])
        x_t = sb("x_t", [P, 2, 2, MC, T], F32R)
        x_f = staged(0, 1, [MC, T], "p (a b) -> p a b")
        hx = sb("hx", [P, 2, 2, T], F32R)
        hm = sb("hm", [P, 2, 2, 2, 2, T], F32R)
        row_max = sb("row_max", [P, TT])
        shifted = sb("shifted", [P, TT, E])
        expd = sb("expd", [P, TT, E])
        row_sum = sb("row_sum", [P, TT])
        row_inv = sb("row_inv", [P, TT])
        probs = sb("probs", [P, 2, TT, E])
        top = sb("top", [P, 2, TT])
        equal = sb("equal", [P, 2, TT, E])
        key = sb("key", [P, 2, TT, E])
        key_max = sb("key_max", [P, 2, TT])
        chosen = sb("chosen", [P, 2, TT, E])
        top_sum = sb("top_sum", [P, TT])
        top_inv = sb("top_inv", [P, TT])
        rw = sb("rw", [P, 2, TT])
        diff = sb("diff", [P, TT, E])
        select = sb("select", [P, TT, 4, E])
        select_t = sb("select_t", [4 * E, 2, T], F32R)
        rw_all = staged(0, 2, [2, 2, T], "p (a b c) -> p a b c")
        z_mask = staged(1, 0, [2, T], "p (a b) -> p a b")
        silu = staged(1, 1, [2, T], "p (a b) -> p a b")
        a = staged(1, 2, [2, T], "p (a b) -> p a b")
        a_parts = sb("a_parts", [P, 2, 2, T], F32R)
        aw = staged(1, 3, [2, T], "p (a b) -> p a b")
        aw_parts = sb("aw_parts", [P, 2, T], F32R)
        zm = staged(2, 0, [2, T], "p (a b) -> p a b")
        o = staged(2, 1, [TT, DM], "p (a b) -> p a b")
        stats = sb("stats", [P, TT, 6])
        mv = sb("mv", [P, TT, 2])
        lnv = sb("lnv", [P, TT])
        rstd = sb("rstd", [P, TT])
        xr = staged(2, 2, [TT, DM], "p (a b) -> p a b")

        gu_ps = ctx.enter_context(nc.psum_tensor("gu_ps", [P, 2, 512], F32))
        z_ps = ctx.enter_context(nc.psum_tensor("z_ps", [P, 2, 512], F32))
        o_ps = ctx.enter_context(nc.psum_tensor("o_ps", [P, 2, 512], F32))
        side = ctx.enter_context(nc.psum_tensor("f_side", [P, 2, 512], F32))

        dve_passed = sem("dve_passed")
        xg_loaded = sem("xg_loaded")
        xg_st_done = sem("xg_st_done")
        xg_mv_done = sem("xg_mv_done")
        xg_lnv_done = sem("xg_lnv_done")
        xg_rstd_done = sem("xg_rstd_done")
        xn_done = sem("xn_done")
        xn_tp = sem("xn_tp")
        xh_ready = sem("xh_ready")
        xl_ready = sem("xl_ready")
        logits_done = sem("logits_done")
        rt = sem("rt")
        exp_done = sem("exp_done")
        hx_done = sem("hx_done")
        hxh_ready = sem("hxh_ready")
        hxl_ready = sem("hxl_ready")
        select_tp = sem("select_tp")
        select_h = sem("select_h")
        select_l = sem("select_l")
        pick_done = sem("pick_done")
        hm_ready = sem("hm_ready")
        rw_done = sem("rw_done")
        rw_ready = sem("rw_ready")
        mask_done = sem("mask_done")
        mask_ready = sem("mask_ready")
        base_done = sem("base_done")
        diff_done = sem("diff_done")
        silu_ready = sem("silu_ready")
        a_ready = sem("a_ready")
        ah_ready = sem("ah_ready")
        al_ready = sem("al_ready")
        aw_step = sem("aw_step")
        awh_ready = sem("awh_ready")
        awl_ready = sem("awl_ready")
        z_done = sem("z_done")
        down_done = sem("down_done")
        zm_step = sem("zm_step")
        o_done = sem("o_done")
        o_ready = sem("o_ready")
        st_done = sem("st_done")
        mv_done = sem("mv_done")
        lnv_done = sem("lnv_done")
        rstd_done = sem("rstd_done")
        yn_done = sem("yn_done")
        xr_loaded = sem("xr_loaded")
        y_ready = sem("y_ready")
        y_stored = sem("y_stored")

        x_v = x2_dram.rearrange("s (j p) d -> s p j d", p=P)
        out_v = out.rearrange("s (j p) d -> s p j d", p=P)
        RT = 25
        PAIRS = ((0, 0), (0, 1), (1, 0))

        PIECES = 2 * FC
        def over_groups(main):
            def run(eng):
                main(0, 0, 0)
                main(1, 1, 1)
                with eng.Fori(2, GROUPS - 3, 2) as m:
                    main(m, 0, None)
                    main(m + 1, 1, None)
                main(GROUPS - 2, 0, GROUPS - 2)
                main(GROUPS - 1, 1, GROUPS - 1)
                main(GROUPS, 0, GROUPS)
            return run

        def on(edge):
            return edge != GROUPS, edge != 0, edge not in (GROUPS - 1, GROUPS), edge in (None, 0, 1)

        block = ctx.enter_context(nc.Block())

        @block.sync
        def _(sp):
            sp.dma_start(xg[:, :, :], x_v[0]).then_inc(xg_loaded, 16)
            sp.wait_ge(xn_tp, MC)
            sp.dma_start(xg[:, :, :], x_v[1]).then_inc(xg_loaded, 16)

            def main(m, par, edge):
                act_on, tail_on, prep_on, norm_on = on(edge)
                if norm_on:
                    sp.wait_ge(xn_tp, MC * (m + 2))
                    sp.dma_start(xg[:, :, :], row(x_v, m + 2)).then_inc(xg_loaded, 16)
                if tail_on:
                    if edge != 1:
                        sp.wait_ge(y_ready, m - 1)
                    sp.dma_start(xr[:, :, :], row(x_v, m - 1)).then_inc(xr_loaded, 16)
                    sp.wait_ge(y_ready, m)
                    sp.dma_start(row(out_v, m - 1), o[:, :, :]).then_inc(y_stored, 16)

            over_groups(main)(sp)
            sp.wait_ge(y_stored, 16 * GROUPS)

        @block.gpsimd
        def _(pool):
            def main(m, par, edge):
                act_on, tail_on, _, _ = on(edge)
                for f in range(FC):
                    if act_on:
                        at = FC * m + f
                        if f == 0:
                            pool.wait_ge(rw_ready, 2 * (m + 1))
                        for k in range(2):
                            pool.wait_ge(a_ready, 2 * at + k + 1)
                            if k == 0 and begun(at):
                                pool.wait_ge(awl_ready, at)
                            nc.gpsimd.tensor_tensor(aw[:, k], a[:, k], rw_all[:, par, k], ALU.mult).then_inc(aw_step, 1)
                        pool.wait_ge(aw_step, 3 * at + 2)
                        nc.gpsimd.tensor_tensor(aw[:, 0], aw[:, 0], aw[:, 1], ALU.add).then_inc(aw_step, 1)
                    if tail_on and f == 4:
                        pool.wait_ge(yn_done, TT * m)
                        pool.wait_ge(xr_loaded, 16 * m)
                        nc.gpsimd.tensor_tensor(o[:, :, :], o[:, :, :], xr[:, :, :], ALU.add).then_inc(y_ready, 1)

            over_groups(main)(pool)

        @block.scalar
        def _(act):
            def norm(s, q):
                if q == 5:
                    act.wait_ge(xg_mv_done, TT * (s + 1))
                    nc.scalar.activation(xg_lnv[:, :], xg_mv[:, :, 1], ACT.Ln, bias=eps[:, 0:1]).then_inc(xg_lnv_done, 1)
                    act.wait_ge(xg_lnv_done, s + 1)
                    nc.scalar.activation(xg_rstd[:, :], xg_lnv[:, :], ACT.Exp, scale=-0.5).then_inc(xg_rstd_done, 1)

            def prep(s, par, q):
                if q == 1:
                    if begun(FC * (s - 1)):
                        act.wait_ge(base_done, FC * (s - 1))
                    if begun(s):
                        act.wait_ge(logits_done, s)
                    for k in range(MC):
                        act.wait_ge(xn_tp, MC * s + k + 1)
                        nc.scalar.activation(x_t[:, par, 0, k], side[:, k], ACT.Copy).then_inc(xh_ready, 1)
                        nc.scalar.activation(x_f[:, k], side[:, k], ACT.Copy).then_inc(xh_ready, 1)
                if q in (5, 7):
                    t = (q - 5) // 2
                    if begun(8 * s):
                        act.wait_ge(hm_ready, 8 * s)
                    act.wait_ge(hx_done, 2 * s + t + 1)
                    nc.scalar.activation(hx[:, 0, t], side[:, 0], ACT.Copy).then_inc(hxh_ready, 1)
                if q == 5:
                    act.wait_ge(rt, RT * s + 2)
                    nc.scalar.activation(expd[:, :, :], shifted[:, :, :], ACT.Exp).then_inc(exp_done, 1)
                if q == 12:
                    if begun(2 * s):
                        act.wait_ge(mask_done, 2 * s)
                    act.wait_ge(select_tp, s + 1)
                    nc.scalar.activation(select_t[:, 0], side[0:4 * E, 0], ACT.Copy).then_inc(select_h, 1)
                if q in (13, 14):
                    k = q - 13
                    if begun(3 * FC * (s - 1)):
                        act.wait_ge(aw_step, 3 * FC * (s - 1))
                    act.wait_ge(rw_done, 2 * s + k + 1)
                    nc.scalar.activation(rw_all[:, par, k], side[:, 1], ACT.Copy).then_inc(rw_ready, 1)

            def tail(s, q):
                if q == 2:
                    if begun(16 * s):
                        act.wait_ge(y_stored, 16 * s)
                    for i in range(2):
                        act.wait_ge(o_done, 2 * s + i + 1)
                        nc.scalar.activation(o[:, 2 * i:2 * i + 2].rearrange("p j d -> p (j d)"), o_ps[:, i],
                                             ACT.Copy).then_inc(o_ready, 1)
                if q == 5:
                    act.wait_ge(mv_done, TT * (s + 1))
                    nc.scalar.activation(lnv[:, :], mv[:, :, 1], ACT.Ln, bias=eps[:, 0:1]).then_inc(lnv_done, 1)
                    act.wait_ge(lnv_done, s + 1)
                    nc.scalar.activation(rstd[:, :], lnv[:, :], ACT.Exp, scale=-0.5).then_inc(rstd_done, 1)

            def high_of_sum(at):
                act.wait_ge(aw_step, 3 * (at + 1))
                if begun(at):
                    act.wait_ge(down_done, at)
                nc.scalar.activation(aw_parts[:, 0], aw[:, 0], ACT.Copy).then_inc(awh_ready, 1)

            def main(m, par, edge):
                act_on, tail_on, prep_on, norm_on = on(edge)
                for f in range(FC):
                    at = FC * m + f
                    if f > 0 and act_on or f == 0 and tail_on:
                        high_of_sum(at - 1)
                    for k in range(2):
                        if act_on:
                            act.wait_ge((base_done, diff_done)[k], at + 1)
                            if begun(2 * at + k - 1):
                                act.wait_ge(a_ready, 2 * at + k - 1)
                            nc.scalar.activation(silu[:, k], gu_ps[:, 0], ACT.Silu).then_inc(silu_ready, 1)
                            act.wait_ge(a_ready, 2 * at + k + 1)
                            if begun(at):
                                act.wait_ge(z_done, at)
                            nc.scalar.activation(a_parts[:, k, 0], a[:, k], ACT.Copy).then_inc(ah_ready, 1)
                        if k == 1 and act_on and f in (1, 2):
                            if begun(3 * m):
                                act.wait_ge(zm_step, 3 * m)
                            act.wait_ge(mask_done, 2 * m + f)
                            nc.scalar.activation(z_mask[:, f - 1], side[:, 1], ACT.Copy).then_inc(mask_ready, 1)
                        if f == 2 and k == 1:
                            nc.scalar.preload_act_table_set("natural_log_exp_and_others")
                        if tail_on:
                            tail(m - 1, 2 * f + k)
                        if prep_on:
                            prep(m + 1, 1 - par, 2 * f + k)
                        if norm_on:
                            norm(m + 2, 2 * f + k)

            nc.scalar.preload_act_table_set("natural_log_exp_and_others")
            for q in range(PIECES):
                norm(0, q)
            for q in range(PIECES):
                prep(0, 0, q)
            for q in range(PIECES):
                norm(1, q)
            over_groups(main)(act)

        @block.vector
        def _(dve):
            def last_axis(ap):
                return ap.unsqueeze(2).broadcast_to([P, TT, E])

            def prep(s, par, q):
                logits = side[:, 0, 0:TT * E].rearrange("p (j e) -> p j e", e=E)
                if q == 3:
                    dve.wait_ge(logits_done, s + 1)
                    if begun(RT * s):
                        dve.wait_ge(rt, RT * s)
                    nc.vector.tensor_reduce(row_max[:, :], logits, AX.X, ALU.max).then_inc(rt, 1)
                    dve.wait_ge(rt, RT * s + 1)
                    nc.vector.tensor_tensor(shifted[:, :, :], logits, last_axis(row_max[:, :]), ALU.subtract).then_inc(rt, 1)
                if q == 6:
                    dve.wait_ge(exp_done, s + 1)
                    if begun(s):
                        dve.wait_ge(select_tp, s)
                    dve.wait_ge(rt, RT * s + 2)
                    nc.vector.tensor_reduce(row_sum[:, :], expd[:, :, :], AX.X, ALU.add).then_inc(rt, 1)
                    dve.wait_ge(rt, RT * s + 3)
                    nc.vector.reciprocal(row_inv[:, :], row_sum[:, :]).then_inc(rt, 1)
                    dve.wait_ge(rt, RT * s + 4)
                    nc.vector.tensor_tensor(probs[:, 0], expd[:, :, :], last_axis(row_inv[:, :]), ALU.mult).then_inc(rt, 1)
                if q in (7, 8):
                    k = q - 7
                    at = RT * s + 5 + 6 * k
                    dve.wait_ge(rt, at)
                    nc.vector.tensor_reduce(top[:, k], probs[:, k], AX.X, ALU.max).then_inc(rt, 1)
                    dve.wait_ge(rt, at + 1)
                    nc.vector.tensor_tensor(equal[:, k], probs[:, k], last_axis(top[:, k]), ALU.is_equal).then_inc(rt, 1)
                    dve.wait_ge(rt, at + 2)
                    nc.vector.tensor_tensor(key[:, k], equal[:, k], rank[:, :, :], ALU.mult).then_inc(rt, 1)
                    dve.wait_ge(rt, at + 3)
                    nc.vector.tensor_reduce(key_max[:, k], key[:, k], AX.X, ALU.max).then_inc(rt, 1)
                    dve.wait_ge(rt, at + 4)
                    nc.vector.tensor_tensor(chosen[:, k], key[:, k], last_axis(key_max[:, k]), ALU.is_equal).then_inc(rt, 1)
                    if k == 0:
                        dve.wait_ge(rt, at + 5)
                        nc.vector.scalar_tensor_tensor(probs[:, 1], chosen[:, 0], -2.0, probs[:, 0],
                                                       ALU.mult, ALU.add).then_inc(rt, 1)
                if q == 9:
                    dve.wait_ge(rt, RT * s + 16)
                    nc.vector.tensor_tensor(top_sum[:, :], top[:, 0], top[:, 1], ALU.add).then_inc(rt, 1)
                    dve.wait_ge(rt, RT * s + 17)
                    nc.vector.reciprocal(top_inv[:, :], top_sum[:, :]).then_inc(rt, 1)
                    dve.wait_ge(rt, RT * s + 18)
                    nc.vector.tensor_tensor(rw[:, 0], top[:, 0], top_inv[:, :], ALU.mult).then_inc(rt, 1)
                    dve.wait_ge(rt, RT * s + 19)
                    nc.vector.tensor_tensor(rw[:, 1], top[:, 1], top_inv[:, :], ALU.mult).then_inc(rt, 1)
                if q == 10:
                    dve.wait_ge(rt, RT * s + 20)
                    nc.vector.tensor_scalar(select[:, :, 0], chosen[:, 0], LORA_SCALE, None, ALU.mult).then_inc(rt, 1)
                    dve.wait_ge(rt, RT * s + 21)
                    nc.vector.tensor_tensor(diff[:, :, :], chosen[:, 1], chosen[:, 0], ALU.subtract).then_inc(rt, 1)
                    dve.wait_ge(rt, RT * s + 22)
                    nc.vector.tensor_scalar(select[:, :, 1], diff[:, :, :], LORA_SCALE, None, ALU.mult).then_inc(rt, 1)
                    for k in range(2):
                        dve.wait_ge(rt, RT * s + 23 + k)
                        nc.vector.scalar_tensor_tensor(select[:, :, 2 + k], chosen[:, k], LORA_SCALE, last_axis(rw[:, k]),
                                                       ALU.mult, ALU.mult).then_inc(rt, 1)
                if q == 1:
                    if begun(FC * (s - 1)):
                        dve.wait_ge(base_done, FC * (s - 1))
                    for k in range(MC):
                        dve.wait_ge(xh_ready, 2 * (MC * s + k) + 2)
                        nc.vector.tensor_tensor(x_t[:, par, 1, k], x_f[:, k], x_t[:, par, 0, k].bitcast(F32),
                                                ALU.subtract).then_inc(xl_ready, 1)
                if q in (5, 7):
                    t = (q - 5) // 2
                    if begun(8 * s):
                        dve.wait_ge(hm_ready, 8 * s)
                    dve.wait_ge(hxh_ready, 2 * s + t + 1)
                    nc.vector.tensor_tensor(hx[:, 1, t], side[:, 0], hx[:, 0, t].bitcast(F32), ALU.subtract)\
                        .then_inc(hxl_ready, 1)
                if q == 12:
                    if begun(2 * s):
                        dve.wait_ge(mask_done, 2 * s)
                    dve.wait_ge(select_h, s + 1)
                    nc.vector.tensor_tensor(select_t[:, 1], side[0:4 * E, 0], select_t[:, 0].bitcast(F32), ALU.subtract)\
                        .then_inc(select_l, 1)
                if q in (13, 14, 15):
                    if begun(FC * (s - 1)):
                        dve.wait_ge(diff_done, FC * (s - 1))
                    k = 0 if q == 13 else 1
                    dve.wait_ge(pick_done, 2 * s + k + 1)
                    for part in ((0, 1), (0,), (1,))[q - 13]:
                        for t in range(2):
                            dve.wait_ge(hxl_ready, 2 * s + t + 1)
                            nc.vector.tensor_tensor(hm[:, par, part, k, t], side[:, 0], hx[:, part, t].bitcast(F32),
                                                    ALU.mult).then_inc(hm_ready, 1)

            def norm(s, q):
                if q == 4:
                    dve.wait_ge(xg_loaded, 16 * (s + 1))
                    for j in range(TT):
                        nc.vector.bn_stats(xg_stats[:, j], xg[:, j]).then_inc(xg_st_done, 1)
                    dve.wait_ge(xg_st_done, TT * (s + 1))
                    pass_waits(dve, dve_passed)
                    for j in range(TT):
                        nc.vector.bn_aggr(xg_mv[:, j], xg_stats[:, j]).then_inc(xg_mv_done, 1)
                if q == 9:
                    dve.wait_ge(xg_rstd_done, s + 1)
                    for j in range(TT):
                        nc.vector.tensor_scalar(xg[:, j], xg[:, j], xg_mv[:, j, 0:1], xg_rstd[:, j:j + 1],
                                                ALU.subtract, ALU.mult).then_inc(xn_done, 1)

            def tail(s, q):
                if q == 1:
                    if begun(2 * s):
                        dve.wait_ge(o_done, 2 * s)
                    dve.wait_ge(mask_ready, 2 * (s + 1))
                    dve.wait_ge(z_done, FC * (s + 1))
                    for k in range(2):
                        nc.vector.tensor_tensor(zm[:, k], z_ps[:, k], z_mask[:, k], ALU.mult).then_inc(zm_step, 1)
                    dve.wait_ge(zm_step, 3 * s + 2)
                    nc.vector.tensor_tensor(zm[:, 0], zm[:, 0], zm[:, 1], ALU.add).then_inc(zm_step, 1)
                if q == 3:
                    dve.wait_ge(o_ready, 2 * (s + 1))
                    for j in range(TT):
                        nc.vector.bn_stats(stats[:, j], o[:, j]).then_inc(st_done, 1)
                    dve.wait_ge(st_done, TT * (s + 1))
                    pass_waits(dve, dve_passed)
                    for j in range(TT):
                        nc.vector.bn_aggr(mv[:, j], stats[:, j]).then_inc(mv_done, 1)
                if q == 7:
                    dve.wait_ge(rstd_done, s + 1)
                    for j in range(TT):
                        nc.vector.tensor_scalar(o[:, j], o[:, j], mv[:, j, 0:1], rstd[:, j:j + 1],
                                                ALU.subtract, ALU.mult).then_inc(yn_done, 1)

            def low_of_sum(at):
                dve.wait_ge(awh_ready, at + 1)
                if begun(at):
                    dve.wait_ge(down_done, at)
                nc.vector.tensor_tensor(aw_parts[:, 1], aw[:, 0], aw_parts[:, 0].bitcast(F32), ALU.subtract)\
                    .then_inc(awl_ready, 1)

            def main(m, par, edge):
                act_on, tail_on, prep_on, norm_on = on(edge)
                for f in range(FC):
                    at = FC * m + f
                    if f > 0 and act_on or f == 0 and tail_on:
                        low_of_sum(at - 1)
                    for k in range(2):
                        if act_on:
                            dve.wait_ge(silu_ready, 2 * at + k + 1)
                            if begun(at):
                                dve.wait_ge(aw_step, 3 * at)
                                dve.wait_ge(al_ready, 2 * at)
                            nc.vector.tensor_tensor(a[:, k], silu[:, k], gu_ps[:, 1], ALU.mult).then_inc(a_ready, 1)
                            dve.wait_ge(ah_ready, 2 * at + k + 1)
                            if begun(at):
                                dve.wait_ge(z_done, at)
                            nc.vector.tensor_tensor(a_parts[:, k, 1], a[:, k], a_parts[:, k, 0].bitcast(F32),
                                                    ALU.subtract).then_inc(al_ready, 1)
                        if tail_on:
                            tail(m - 1, 2 * f + k)
                        if prep_on:
                            prep(m + 1, 1 - par, 2 * f + k)
                        if norm_on:
                            norm(m + 2, 2 * f + k)

            for q in range(PIECES):
                norm(0, q)
            for q in range(PIECES):
                prep(0, 0, q)
            for q in range(PIECES):
                norm(1, q)
            over_groups(main)(dve)

        @block.tensor
        def _(pe):
            def mm(out_, lhs, rhs, start, stop):
                return nc.tensor.matmul(out_, lhs, rhs, start=start, stop=stop)

            def onto(out_, lhs, rhs, start=False):
                return nc.tensor.matmul(out_, lhs, rhs, start=start, stop=True, skip_group_check=True)

            def flip(out_, blocks):
                for i, b in enumerate(blocks):
                    last = nc.tensor.transpose(out_[:, i * P:(i + 1) * P], b, ident[:, :])
                return last

            def prep(s, par, q):
                if q == 1:
                    pe.wait_ge(xn_done, TT * (s + 1))
                    for k in range(MC):
                        if begun(8 * s):
                            if k == 0:
                                pe.wait_ge(hm_ready, 8 * s)
                            else:
                                pe.wait_ge(rw_ready, 2 * s)
                        flip(side[:, k], [xg[:, j, k * P:(k + 1) * P] for j in range(TT)]).then_inc(xn_tp, 1)
                if q == 3:
                    pe.wait_ge(xh_ready, 2 * MC * (s + 1))
                    pe.wait_ge(xl_ready, MC * (s + 1))
                    for j in range(TT):
                        for k in range(MC):
                            last = mm(side[:, 0, j * E:(j + 1) * E], x_f[:, k, j * P:(j + 1) * P], w_router[:, k], k == 0,
                                      k == MC - 1)
                    last.then_inc(logits_done, 1)
                if q in (5, 7):
                    t = (q - 5) // 2
                    if t == 0:
                        pe.wait_ge(rt, RT * s + 2)
                    else:
                        pe.wait_ge(hxl_ready, 2 * s + 1)
                    for i, (u, v) in enumerate(PAIRS):
                        for k in range(MC):
                            last = mm(side[:, 0], w_h[:, u, k, t * ER:(t + 1) * ER], x_t[:, par, v, k],
                                      i == 0 and k == 0, i == 2 and k == MC - 1)
                    last.then_inc(hx_done, 1)
                if q == 12:
                    pe.wait_ge(rt, RT * (s + 1))
                    pe.wait_ge(hxl_ready, 2 * (s + 1))
                    for j in range(TT):
                        last = nc.tensor.transpose(side[0:4 * E, 0, j * P:(j + 1) * P],
                                                   select[:, j].rearrange("p q e -> p (q e)"), ident[:, :])
                    last.then_inc(select_tp, 1)
                if q in (13, 14):
                    k = q - 13
                    if k == 0:
                        pe.wait_ge(select_l, s + 1)
                    else:
                        pe.wait_ge(hm_ready, 8 * s + 4)
                    mm(side[:, 0], expand[:, k], select_t[:, 0], True, True).then_inc(pick_done, 1)
                    if k == 1:
                        pe.wait_ge(rw_ready, 2 * s + 1)
                    elif begun(2 * s):
                        pe.wait_ge(mask_ready, 2 * s)
                    for part in range(2):
                        last = mm(side[:, 1], half[:, k], select_t[:, part], part == 0, part == 1)
                    last.then_inc(rw_done, 1)

            def z_product(f, at):
                pe.wait_ge(al_ready, 2 * at + 2)
                for k in range(2):
                    for i, (u, v) in enumerate(PAIRS):
                        last = mm(z_ps[:, k], a2[:, u, f], a_parts[:, k, v], f == 0 and i == 0, f == FC - 1 and i == 2)
                last.then_inc(z_done, 1)

            def down(f, at):
                pe.wait_ge(awl_ready, at + 1)
                for j in range(TT):
                    for i, (u, v) in enumerate(PAIRS):
                        last = onto(o_ps[:, j // 2, (j % 2) * DM:(j % 2 + 1) * DM], aw_parts[:, u, j * P:(j + 1) * P],
                                    w_down[:, v, f], start=f == 0 and i == 0 and j % 2 == 0)
                last.then_inc(down_done, 1)

            def main(m, par, edge):
                act_on, tail_on, prep_on, norm_on = on(edge)
                for f in range(FC):
                    cols = slice(f * P, (f + 1) * P)
                    at = FC * m + f
                    back = f > 0 and act_on or f == 0 and tail_on
                    if act_on:
                        if f == 0:
                            pe.wait_ge(xh_ready, 2 * MC * (m + 1))
                            pe.wait_ge(xl_ready, MC * (m + 1))
                            pe.wait_ge(hm_ready, 8 * m + 4)
                        for t, wide, lora in ((0, w_gate, b_gate), (1, w_up, b_up)):
                            if begun(2 * at):
                                pe.wait_ge((silu_ready, a_ready)[t], 2 * at)
                            for i, (u, v) in enumerate(PAIRS):
                                for k in range(MC):
                                    mm(gu_ps[:, t], wide[:, u, k, cols], x_t[:, par, v, k], i == 0 and k == 0, False)
                            for i, (u, v) in enumerate(PAIRS):
                                last = mm(gu_ps[:, t], lora[:, u, cols], hm[:, par, v, 0, t], False, i == 2)
                        last.then_inc(base_done, 1)
                    if tail_on and f == 1:
                        pe.wait_ge(zm_step, 3 * m)
                        for j in range(TT):
                            last = onto(o_ps[:, j // 2, (j % 2) * DM:(j % 2 + 1) * DM], zm[:, 0, j * P:(j + 1) * P],
                                        b_down[:, :])
                            if j % 2:
                                last.then_inc(o_done, 1)
                    if prep_on:
                        prep(m + 1, 1 - par, 2 * f)
                    if back:
                        if f == 1 and tail_on:
                            pe.wait_ge(zm_step, 3 * m)
                        z_product((f - 1) % FC, at - 1)
                    if act_on:
                        if f == 0:
                            pe.wait_ge(hm_ready, 8 * (m + 1))
                        for t, lora in ((0, b_gate), (1, b_up)):
                            pe.wait_ge((silu_ready, a_ready)[t], 2 * at + 1)
                            for u, v in PAIRS:
                                last = onto(gu_ps[:, t], lora[:, u, cols], hm[:, par, v, 1, t])
                        last.then_inc(diff_done, 1)
                    if back:
                        if f == 1 and tail_on:
                            pe.wait_ge(o_ready, 2 * m)
                        down((f - 1) % FC, at - 1)
                    if act_on and f in (1, 2):
                        k = f - 1
                        if k == 0:
                            pe.wait_ge(rw_ready, 2 * (m + 1))
                            if prep_on:
                                pe.wait_ge(xh_ready, 2 * MC * (m + 2))
                        else:
                            pe.wait_ge(mask_ready, 2 * m + 1)
                        for part in range(2):
                            last = mm(side[:, 1], expand[:, 2 + k], select_t[:, part], part == 0, part == 1)
                        last.then_inc(mask_done, 1)
                    if prep_on:
                        prep(m + 1, 1 - par, 2 * f + 1)

            for q in range(PIECES):
                prep(0, 0, q)
            over_groups(main)(pe)


@contextmanager
def consts_of(nc):
    with (nc.sbuf_tensor("ident", [P, P], F32) as ident, nc.sbuf_tensor("eps", [P, 1], F32) as eps,
          nc.sbuf_tensor("one", [P, 1], F32) as one):
        yield ident, eps, one


def build(nc, dram, out):
    x2 = nc.dram_tensor("x2_between", out.shape, F32, kind="Internal").ap()
    with ExitStack() as ctx:
        consts = ctx.enter_context(consts_of(nc))
        stage = [ctx.enter_context(nc.sbuf_tensor(f"stage{i}", [P, STAGE], F32)) for i in range(3)]
        raw_sems = {n: ctx.enter_context(nc.semaphore("loaded_" + n)) for n in RAW}
        mamba_phase(nc, dram["x"], dram, x2, consts, stage, raw_weights(stage, dram, raw_sems))
        ffn_phase(nc, x2, dram, out, consts, stage, raw_sems)


def lay_out(i):
    import numpy as np

    def chunks(a):
        a = np.asarray(a)
        return np.ascontiguousarray(a.reshape(-1, P, *a.shape[1:]).swapaxes(0, 1))

    at, ff = (lambda n: np.asarray(i["L0_attn_" + n])), (lambda n: np.asarray(i["L0_ffn_" + n]))
    return {
        "x": at("x"),
        "w_in": chunks(at("W_in").T), "conv_w": chunks(at("conv_w")), "conv_b": chunks(at("conv_b")),
        "w_x": chunks(at("W_x").T), "w_dt": np.ascontiguousarray(at("W_dt").T), "b_dt": chunks(at("b_dt")),
        "a_log": chunks(at("A_log")), "d_skip": chunks(at("Dp")), "w_out": chunks(at("W_out").T),
        "w_h": chunks(np.concatenate([ff("A1").reshape(ER, DM), ff("A3").reshape(ER, DM)]).T),
        "w_router": chunks(ff("gate_w").T),
        "w_gate": chunks(ff("w_gate").T), "w_up": chunks(ff("w_up").T),
        "b_gate": np.ascontiguousarray(ff("B1").transpose(0, 2, 1).reshape(ER, FF)),
        "b_up": np.ascontiguousarray(ff("B3").transpose(0, 2, 1).reshape(ER, FF)),
        "w_down": chunks(ff("w_down").T), "a2": chunks(ff("A2").reshape(ER, FF).T),
        "b_down": np.ascontiguousarray(ff("B2").transpose(0, 2, 1).reshape(ER, DM)),
    }


def kernel(**inputs):
    import numpy as np
    import concourse.bacc as bacc
    from concourse.bass_utils import run_bass_kernel_spmd

    arrays = lay_out(inputs)
    nc = bacc.Bacc("TRN2", target_bir_lowering=False, num_devices=1)
    dram = {n: nc.dram_tensor("in_" + n, a.shape, mybir.dt.from_np(a.dtype), kind="ExternalInput").ap()
            for n, a in arrays.items()}
    out = nc.dram_tensor("out", arrays["x"].shape, F32, kind="ExternalOutput").ap()
    build(nc, dram, out)
    r = run_bass_kernel_spmd(nc, [{"in_" + n: a for n, a in arrays.items()}], core_ids=[0])
    return r.results[0]["out"]
```
